# Optimizing a Trainium2 kernel written in Bass

```python
import numpy as np
import jax
import jax.numpy as jnp

def _softmax(x, axis=-1):
    return jax.nn.softmax(x, axis=axis)

def _gelu(x):
    return jax.nn.gelu(x, approximate=True)

def _silu(x):
    return jax.nn.silu(x)

def _sigmoid(x):
    return jax.nn.sigmoid(x)

def _layernorm(x, axis=-1, eps=1e-05):
    m = jnp.mean(x, axis=axis, keepdims=True)
    v = jnp.var(x, axis=axis, keepdims=True)
    return (x - m) / jnp.sqrt(v + eps)

def _scatter_add(tgt, idx, src, axis=0):
    return tgt.at[idx].add(src)

def _segment_sum(src, seg, n):
    return jax.ops.segment_sum(src, seg, n)
kernel_name = 'mk_audio_tower_d1_tok_aud1d768_r4_e335ca'

def setup_inputs(seed: int=0):
    np.random.seed(seed)
    _w = jnp.asarray

    def _rec_inputs():
        import jax
        import jax.numpy as jnp
        _rk = jax.random.key(seed)
        x = -0.000869125 + 1.00042 * jax.random.normal(jax.random.fold_in(_rk, 1), (64, 20000), jnp.float32)
        return x
    x = _rec_inputs()

    def _L0_tok_setup():
        import jax, jax.numpy as jnp
        import numpy as np
        CONVS = [(128, 10, 5)] + [(128, 3, 2)] * 4 + [(128, 2, 2)] * 2

        def _fp32_layernorm(x, g, b, eps=1e-05):
            xf = x.astype(jnp.float32)
            mu = xf.mean(-1, keepdims=True)
            var = xf.var(-1, keepdims=True)
            y = (xf - mu) * jax.lax.rsqrt(var + eps) * g.astype(jnp.float32) + b.astype(jnp.float32)
            return y.astype(x.dtype)

        def _conv1d(x, w, stride):
            return jax.lax.conv_general_dilated(x, w, (stride,), 'VALID', dimension_numbers=('NCH', 'OIH', 'NCH'))
        key = jax.random.key(seed)
        keys = jax.random.split(key, 16)
        inp = {'x': jax.random.normal(keys[0], (8, 40000), jnp.float32)}
        in_d = 1
        for i, (dim, k, s) in enumerate(CONVS):
            fan_in = in_d * k
            inp[f'conv_w{i}'] = jax.random.normal(keys[1 + i], (dim, in_d, k), jnp.float32) * np.float32(np.sqrt(2.0 / fan_in))
            inp[f'ln_g{i}'] = jnp.ones((dim,), jnp.float32)
            inp[f'ln_b{i}'] = jnp.zeros((dim,), jnp.float32)
            in_d = dim
        inp['fln_g'] = jnp.ones((128,), jnp.float32)
        inp['fln_b'] = jnp.zeros((128,), jnp.float32)
        inp['proj_w'] = jax.random.normal(keys[9], (128, 192), jnp.float32) * np.float32(0.02)
        inp['proj_b'] = jnp.zeros((192,), jnp.float32)
        return inp
    _L0_tok_all = _L0_tok_setup()
    _L0_tok_in = {k: v for k, v in _L0_tok_all.items() if k in ('conv_w0', 'ln_g0', 'ln_b0', 'conv_w1', 'ln_g1', 'ln_b1', 'conv_w2', 'ln_g2', 'ln_b2', 'conv_w3', 'ln_g3', 'ln_b3', 'conv_w4', 'ln_g4', 'ln_b4', 'conv_w5', 'ln_g5', 'ln_b5', 'conv_w6', 'ln_g6', 'ln_b6', 'fln_g', 'fln_b', 'proj_w', 'proj_b')}
    del _L0_tok_all

    def _L0_attn_setup():
        import jax, jax.numpy as jnp
        import numpy as np
        NUM_HEADS = 12
        key = jax.random.key(seed)
        k1, k2, k3 = jax.random.split(key, 3)
        B, N, C = (2, 1024, 192)
        x = jax.random.normal(k1, (B, N, C), dtype=jnp.float32)
        w_qkv = jax.random.normal(k2, (C, 3 * C), dtype=jnp.float32) * 0.02
        b_qkv = jnp.zeros((3 * C,), dtype=jnp.float32)
        w_proj = jax.random.normal(k3, (C, C), dtype=jnp.float32) * 0.02
        b_proj = jnp.zeros((C,), dtype=jnp.float32)
        return {'x': x, 'w_qkv': w_qkv, 'b_qkv': b_qkv, 'w_proj': w_proj, 'b_proj': b_proj}
    _L0_attn_all = _L0_attn_setup()
    _L0_attn_in = {k: v for k, v in _L0_attn_all.items() if k in ('w_qkv', 'b_qkv', 'w_proj', 'b_proj')}
    del _L0_attn_all

    def _L0_ffn_setup():
        import jax, jax.numpy as jnp
        import numpy as np
        B, S, H, F = (4, 256, 192, 768)
        EC, EU = (4, 4)
        CAP_FACTOR = 1.0

        def _ffn(x, W1, b1, W2, b2):
            return jax.nn.gelu(x @ W1 + b1, approximate=False) @ W2 + b2

        def _expert_mix(h, route, W1, b1, W2, b2, n_exp):
            out = jnp.zeros_like(h)
            for e in range(n_exp):
                m = (route == e).astype(h.dtype)[:, None]
                out = out + m * _ffn(h, W1[e], b1[e], W2[e], b2[e])
            return out

        def _drop_mask(route, pmax, capacity):
            N = route.shape[0]
            order = jnp.lexsort((-jax.lax.stop_gradient(pmax), route))
            rs = route[order]
            starts = jnp.searchsorted(rs, rs, side='left')
            rank_sorted = jnp.arange(N) - starts
            rank = jnp.zeros((N,), jnp.int32).at[order].set(rank_sorted.astype(jnp.int32))
            return rank >= capacity
        key = jax.random.key(seed)
        ks = jax.random.split(key, 8)

        def w(k, shape, s=0.02):
            return jax.random.normal(k, shape, jnp.float32) * s
        return {'hidden_states': jax.random.normal(ks[0], (B, S, H), jnp.float32), 'Wsc': w(ks[1], (H, EC)), 'bsc': jnp.zeros((EC,), jnp.float32), 'W1c': w(ks[2], (EC, H, F)), 'b1c': jnp.zeros((EC, F), jnp.float32), 'W2c': w(ks[3], (EC, F, H)), 'b2c': jnp.zeros((EC, H), jnp.float32), 'Wsu': w(ks[4], (H, EU)), 'bsu': jnp.zeros((EU,), jnp.float32), 'W1u': w(ks[5], (EU, H, F)), 'b1u': jnp.zeros((EU, F), jnp.float32), 'W2u': w(ks[6], (EU, F, H)), 'b2u': jnp.zeros((EU, H), jnp.float32)}
    _L0_ffn_all = _L0_ffn_setup()
    _L0_ffn_in = {k: v for k, v in _L0_ffn_all.items() if k in ('Wsc', 'bsc', 'W1c', 'b1c', 'W2c', 'b2c', 'Wsu', 'bsu', 'W1u', 'b1u', 'W2u', 'b2u')}
    del _L0_ffn_all
    return {'x': x, 'L0_tok_conv_w0': _L0_tok_in['conv_w0'], 'L0_tok_ln_g0': _L0_tok_in['ln_g0'], 'L0_tok_ln_b0': _L0_tok_in['ln_b0'], 'L0_tok_conv_w1': _L0_tok_in['conv_w1'], 'L0_tok_ln_g1': _L0_tok_in['ln_g1'], 'L0_tok_ln_b1': _L0_tok_in['ln_b1'], 'L0_tok_conv_w2': _L0_tok_in['conv_w2'], 'L0_tok_ln_g2': _L0_tok_in['ln_g2'], 'L0_tok_ln_b2': _L0_tok_in['ln_b2'], 'L0_tok_conv_w3': _L0_tok_in['conv_w3'], 'L0_tok_ln_g3': _L0_tok_in['ln_g3'], 'L0_tok_ln_b3': _L0_tok_in['ln_b3'], 'L0_tok_conv_w4': _L0_tok_in['conv_w4'], 'L0_tok_ln_g4': _L0_tok_in['ln_g4'], 'L0_tok_ln_b4': _L0_tok_in['ln_b4'], 'L0_tok_conv_w5': _L0_tok_in['conv_w5'], 'L0_tok_ln_g5': _L0_tok_in['ln_g5'], 'L0_tok_ln_b5': _L0_tok_in['ln_b5'], 'L0_tok_conv_w6': _L0_tok_in['conv_w6'], 'L0_tok_ln_g6': _L0_tok_in['ln_g6'], 'L0_tok_ln_b6': _L0_tok_in['ln_b6'], 'L0_tok_fln_g': _L0_tok_in['fln_g'], 'L0_tok_fln_b': _L0_tok_in['fln_b'], 'L0_tok_proj_w': _L0_tok_in['proj_w'], 'L0_tok_proj_b': _L0_tok_in['proj_b'], 'L0_attn_w_qkv': _L0_attn_in['w_qkv'], 'L0_attn_b_qkv': _L0_attn_in['b_qkv'], 'L0_attn_w_proj': _L0_attn_in['w_proj'], 'L0_attn_b_proj': _L0_attn_in['b_proj'], 'L0_ffn_Wsc': _L0_ffn_in['Wsc'], 'L0_ffn_bsc': _L0_ffn_in['bsc'], 'L0_ffn_W1c': _L0_ffn_in['W1c'], 'L0_ffn_b1c': _L0_ffn_in['b1c'], 'L0_ffn_W2c': _L0_ffn_in['W2c'], 'L0_ffn_b2c': _L0_ffn_in['b2c'], 'L0_ffn_Wsu': _L0_ffn_in['Wsu'], 'L0_ffn_bsu': _L0_ffn_in['bsu'], 'L0_ffn_W1u': _L0_ffn_in['W1u'], 'L0_ffn_b1u': _L0_ffn_in['b1u'], 'L0_ffn_W2u': _L0_ffn_in['W2u'], 'L0_ffn_b2u': _L0_ffn_in['b2u']}

def reference(x, L0_tok_conv_w0, L0_tok_ln_g0, L0_tok_ln_b0, L0_tok_conv_w1, L0_tok_ln_g1, L0_tok_ln_b1, L0_tok_conv_w2, L0_tok_ln_g2, L0_tok_ln_b2, L0_tok_conv_w3, L0_tok_ln_g3, L0_tok_ln_b3, L0_tok_conv_w4, L0_tok_ln_g4, L0_tok_ln_b4, L0_tok_conv_w5, L0_tok_ln_g5, L0_tok_ln_b5, L0_tok_conv_w6, L0_tok_ln_g6, L0_tok_ln_b6, L0_tok_fln_g, L0_tok_fln_b, L0_tok_proj_w, L0_tok_proj_b, L0_attn_w_qkv, L0_attn_b_qkv, L0_attn_w_proj, L0_attn_b_proj, L0_ffn_Wsc, L0_ffn_bsc, L0_ffn_W1c, L0_ffn_b1c, L0_ffn_W2c, L0_ffn_b2c, L0_ffn_Wsu, L0_ffn_bsu, L0_ffn_W1u, L0_ffn_b1u, L0_ffn_W2u, L0_ffn_b2u):
    import jax
    import jax.numpy as jnp

    def _L0_tok_ref(x, conv_w0, ln_g0, ln_b0, conv_w1, ln_g1, ln_b1, conv_w2, ln_g2, ln_b2, conv_w3, ln_g3, ln_b3, conv_w4, ln_g4, ln_b4, conv_w5, ln_g5, ln_b5, conv_w6, ln_g6, ln_b6, fln_g, fln_b, proj_w, proj_b):
        import jax, jax.numpy as jnp
        import numpy as np
        CONVS = [(128, 10, 5)] + [(128, 3, 2)] * 4 + [(128, 2, 2)] * 2

        def _fp32_layernorm(x, g, b, eps=1e-05):
            xf = x.astype(jnp.float32)
            mu = xf.mean(-1, keepdims=True)
            var = xf.var(-1, keepdims=True)
            y = (xf - mu) * jax.lax.rsqrt(var + eps) * g.astype(jnp.float32) + b.astype(jnp.float32)
            return y.astype(x.dtype)

        def _conv1d(x, w, stride):
            return jax.lax.conv_general_dilated(x, w, (stride,), 'VALID', dimension_numbers=('NCH', 'OIH', 'NCH'))
        conv_ws = [conv_w0, conv_w1, conv_w2, conv_w3, conv_w4, conv_w5, conv_w6]
        ln_gs = [ln_g0, ln_g1, ln_g2, ln_g3, ln_g4, ln_g5, ln_g6]
        ln_bs = [ln_b0, ln_b1, ln_b2, ln_b3, ln_b4, ln_b5, ln_b6]
        strides = [s for _, _, s in CONVS]
        h = x[:, None, :]
        for w, g, b, s in zip(conv_ws, ln_gs, ln_bs, strides):
            h = _conv1d(h, w, s)
            h = jnp.swapaxes(h, -2, -1)
            h = _fp32_layernorm(h, g, b)
            h = jnp.swapaxes(h, -2, -1)
            h = jax.nn.gelu(h, approximate=False)
        h = jnp.swapaxes(h, 1, 2)
        norm_h = _fp32_layernorm(h, fln_g, fln_b)
        out = norm_h @ proj_w + proj_b
        return out

    def _L0_attn_ref(x, w_qkv, b_qkv, w_proj, b_proj):
        import jax, jax.numpy as jnp
        import numpy as np
        NUM_HEADS = 12
        B, N, C = x.shape
        H = NUM_HEADS
        D = C // H
        qkv = (x @ w_qkv + b_qkv).reshape(B, N, 3, H, D).transpose(2, 0, 3, 1, 4)
        q, k, v = (qkv[0], qkv[1], qkv[2])
        attn = jnp.einsum('bhnd,bhmd->bhnm', q, k) / jnp.sqrt(jnp.float32(D))
        out = jnp.einsum('bhnm,bhmd->bhnd', attn, v)
        out = out.transpose(0, 2, 1, 3).reshape(B, N, C)
        return out @ w_proj + b_proj

    def _L0_ffn_ref(hidden_states, Wsc, bsc, W1c, b1c, W2c, b2c, Wsu, bsu, W1u, b1u, W2u, b2u):
        import jax, jax.numpy as jnp
        import numpy as np
        B, S, H, F = (4, 256, 192, 768)
        EC, EU = (4, 4)
        CAP_FACTOR = 1.0

        def _ffn(x, W1, b1, W2, b2):
            return jax.nn.gelu(x @ W1 + b1, approximate=False) @ W2 + b2

        def _expert_mix(h, route, W1, b1, W2, b2, n_exp):
            out = jnp.zeros_like(h)
            for e in range(n_exp):
                m = (route == e).astype(h.dtype)[:, None]
                out = out + m * _ffn(h, W1[e], b1[e], W2[e], b2[e])
            return out

        def _drop_mask(route, pmax, capacity):
            N = route.shape[0]
            order = jnp.lexsort((-jax.lax.stop_gradient(pmax), route))
            rs = route[order]
            starts = jnp.searchsorted(rs, rs, side='left')
            rank_sorted = jnp.arange(N) - starts
            rank = jnp.zeros((N,), jnp.int32).at[order].set(rank_sorted.astype(jnp.int32))
            return rank >= capacity
        shp = hidden_states.shape
        h = hidden_states.reshape(-1, shp[-1])
        N = h.shape[0]
        capacity = int(CAP_FACTOR * N / EC)
        pc = jax.nn.softmax(h @ Wsc + bsc, axis=-1)
        pmax_c = jnp.max(pc, axis=-1)
        route_c = jnp.argmax(pc, axis=-1)
        dropped = _drop_mask(route_c, pmax_c, capacity)
        scale_c = (pmax_c / jax.lax.stop_gradient(pmax_c))[:, None]
        common = _expert_mix(h, route_c, W1c, b1c, W2c, b2c, EC) * scale_c
        pu = jax.nn.softmax(h @ Wsu + bsu, axis=-1)
        pmax_u = jnp.max(pu, axis=-1)
        route_u = jnp.argmax(pu, axis=-1)
        scale_u = (pmax_u / jax.lax.stop_gradient(pmax_u))[:, None]
        unique = _expert_mix(h, route_u, W1u, b1u, W2u, b2u, EU) * scale_u
        out = common + dropped[:, None].astype(h.dtype) * unique
        return out.reshape(shp)
    h = _L0_tok_ref(x, L0_tok_conv_w0, L0_tok_ln_g0, L0_tok_ln_b0, L0_tok_conv_w1, L0_tok_ln_g1, L0_tok_ln_b1, L0_tok_conv_w2, L0_tok_ln_g2, L0_tok_ln_b2, L0_tok_conv_w3, L0_tok_ln_g3, L0_tok_ln_b3, L0_tok_conv_w4, L0_tok_ln_g4, L0_tok_ln_b4, L0_tok_conv_w5, L0_tok_ln_g5, L0_tok_ln_b5, L0_tok_conv_w6, L0_tok_ln_g6, L0_tok_ln_b6, L0_tok_fln_g, L0_tok_fln_b, L0_tok_proj_w, L0_tok_proj_b)
    h = h + _L0_attn_ref(_layernorm(h, axis=-1), L0_attn_w_qkv, L0_attn_b_qkv, L0_attn_w_proj, L0_attn_b_proj)
    h = h + _L0_ffn_ref(_layernorm(h, axis=-1), L0_ffn_Wsc, L0_ffn_bsc, L0_ffn_W1c, L0_ffn_b1c, L0_ffn_W2c, L0_ffn_b2c, L0_ffn_Wsu, L0_ffn_bsu, L0_ffn_W1u, L0_ffn_b1u, L0_ffn_W2u, L0_ffn_b2u)
    return h

_drawn_inputs = setup_inputs


def setup_inputs(seed=0):
    import zlib

    import numpy as np

    out = dict(_drawn_inputs(seed))
    spreads = {'L0_tok_ln_g0': (1.0, 0.2),
     'L0_tok_ln_b0': (0.0, 0.1),
     'L0_tok_ln_g1': (1.0, 0.2),
     'L0_tok_ln_b1': (0.0, 0.1),
     'L0_tok_ln_g2': (1.0, 0.2),
     'L0_tok_ln_b2': (0.0, 0.1),
     'L0_tok_ln_g3': (1.0, 0.2),
     'L0_tok_ln_b3': (0.0, 0.1),
     'L0_tok_ln_g4': (1.0, 0.2),
     'L0_tok_ln_b4': (0.0, 0.1),
     'L0_tok_ln_g5': (1.0, 0.2),
     'L0_tok_ln_b5': (0.0, 0.1),
     'L0_tok_ln_g6': (1.0, 0.2),
     'L0_tok_ln_b6': (0.0, 0.1),
     'L0_tok_fln_g': (1.0, 0.2),
     'L0_tok_fln_b': (0.0, 0.1),
     'L0_tok_proj_b': (0.0, 0.1),
     'L0_attn_b_qkv': (0.0, 0.1),
     'L0_attn_b_proj': (0.0, 0.1),
     'L0_ffn_bsc': (0.0, 0.1),
     'L0_ffn_b1c': (0.0, 0.1),
     'L0_ffn_b2c': (0.0, 0.1),
     'L0_ffn_bsu': (0.0, 0.1),
     'L0_ffn_b1u': (0.0, 0.1),
     'L0_ffn_b2u': (0.0, 0.1)}
    factors = {}
    for name, (base, spread) in spreads.items():
        noise = np.random.default_rng([zlib.crc32(name.encode()), seed]).standard_normal(out[name].shape)
        drawn = base * np.exp(spread * noise) if base else spread * noise
        out[name] = jnp.asarray(drawn.astype(out[name].dtype))
    for name, factor in factors.items():
        out[name] = (out[name] * factor).astype(out[name].dtype)
    return out
```

```python
from contextlib import ExitStack

import numpy as np

import concourse.bass as bass
from concourse import mybir

ALU = mybir.AluOpType
ACT = mybir.ActivationFunctionType
F32 = mybir.dt.float32
I32 = mybir.dt.int32
AX_X = mybir.AxisListType.X

P = 128
B, SAMPLES = 64, 20000
STRIDE0, TAPS0 = 5, 10
RES0 = 16
Q = SAMPLES // (STRIDE0 * RES0)
SPAN = STRIDE0 * RES0
HALF = RES0 // 2
XR = HALF * TAPS0
PAIRS = B // 2
N = 2 * Q
BLK = Q // 2
T5, T6 = 124, 62
PAD6 = 64
C, C2 = 128, 192
CB = C2 - P
HEAD = 16
EPS = 1e-5
NE, FF = 4, 768
FC = FF // P
CAP = B * T6 // NE
TAPS = {1: 3, 2: 3, 3: 3, 4: 3, 5: 2, 6: 2, 7: 1}
TAP0 = {1: 0, 2: 3, 3: 6, 4: 9, 5: 12, 6: 14, 7: 16}
NTAP = 17

SLOTS = [(1, 0), (1, 1), (4, 0), (1, 2), (1, 3), (5, 0), (1, 4), (1, 5), (6, 0), (1, 6), (2, 0), (1, 7),
         (2, 1), (2, 2), (2, 3), (7, 0), (3, 0), (3, 1)]
TAIL = [(4, 0), (5, 0), (6, 0), (7, 0)]
NS = len(SLOTS)
SPREAD = {4: N, 5: 2 * T5, 6: 2 * T6, 7: 2 * T6}
EXTRA = {1: "z", 2: "a0", 3: "pc", 4: "a1", 5: "pb", 6: "a2", 8: "a3", 9: "a4", 11: "a5 l", 12: "l l l", 13: "a6 l l",
         14: "l l l", 15: "a7 l l", 16: "a8 l l", 17: "l R S l l R"}
ATT = 9


def order(slots, with_next, with_att):
    n, l0 = len(slots), 0
    if n < NS:
        return [(what, s) for s in range(n) for what in ("tap0", "tap1", "conv", "colsum", "bcast")]
    out, bc = [], 0
    for s in range(n):
        out.append(("tap0", s))
        if s >= 2:
            out.append(("bcast", bc))
            bc += 1
        out.append(("tap1", s))
        if s:
            out.append(("colsum", s - 1))
        out.append(("conv", s))
        for word in EXTRA.get(s, "").split():
            if word == "S":
                out.append(("colsum", s))
            elif word == "R":
                out.append(("bcast", bc))
                bc += 1
            elif word[0] == "a":
                if with_att:
                    out.append(("att", int(word[1:])))
            elif with_next:
                if word == "l":
                    out.append(("l0", l0))
                    l0 += 1
                else:
                    out.append(({"z": "zmm", "pc": "psum", "pb": "pbc"}[word], s))
    assert bc == n and l0 in (0, RES0)
    return out


def blocks(n):
    k = -(-n // P)
    assert n % k == 0
    return [(j * (n // k), n // k) for j in range(k)]


def audio_tower(nc, xt, w0, wc, aff, projw, projb, wqkv, bq, bkv, wproj, bproj, wr, br, w1, b1, w2, b2,
                ident, center, ones, onesc, gmask, rmask, amask, valid, bmask, tri, out):
    with ExitStack() as ctx:
        def sb(name, shape, dt=F32):
            return ctx.enter_context(nc.sbuf_tensor(name, shape, dt))

        def psum(name, shape):
            return ctx.enter_context(nc.psum_tensor(name, shape, F32))

        def sem(name):
            return ctx.enter_context(nc.semaphore(name))

        ps_l0 = psum("ps_l0", [P, 2, 512])
        ps_y = psum("ps_y", [P, 2, 512])
        ps_r = psum("ps_r", [P, 2, 512])
        ps_v = psum("ps_v", [P, 512])
        ps_a = psum("ps_a", [P, 512])
        hid_banks = [ps_l0[:, 0, :], ps_l0[:, 1, :], ps_y[:, 0, :], ps_y[:, 1, :]]
        out_banks = [ps_r[:, 0, :], ps_r[:, 1, :], ps_v[:, :], ps_a[:, :]]

        id_sb = sb("id_sb", [P, P])
        ones_sb = sb("ones_sb", [P, 1])
        gmask_sb = sb("gmask_sb", [XR, XR])
        rmask_sb = sb("rmask_sb", [XR, HALF])
        ones_pp = sb("ones_pp", [P, P])
        amask_sb = sb("amask_sb", [P, C2])
        valid_sb = sb("valid_sb", [P, 1])
        bmask_sb = sb("bmask_sb", [P, 2])
        tri_sb = sb("tri_sb", [P, P])
        center_sb = sb("center_sb", [P, P])
        wcv = sb("wcv", [P, NTAP, C])
        wmean = sb("wmean", [P, NTAP])
        w0_sb = sb("w0_sb", [P, TAPS0])
        w0c = sb("w0c", [P, HALF, TAPS0])
        w0t = sb("w0t", [XR, P])
        w0r = sb("w0r", [XR, HALF, P])
        gram = sb("gram", [XR, XR])
        aff_sb = sb("aff_sb", [P, 2, 8])
        projw_sb = sb("projw_sb", [P, C2])
        projb_sb = sb("projb_sb", [P, C2])
        wqkv_sb = sb("wqkv_sb", [P, 2, 3 * C2])
        bq_sb = sb("bq_sb", [P, 2])
        bkv_sb = sb("bkv_sb", [P, 2 * C2])
        wproj_sb = sb("wproj_sb", [P, 2, C2])
        bproj_sb = sb("bproj_sb", [P, C2])
        wr_sb = sb("wr_sb", [P, 2, 2 * NE])
        br_sb = sb("br_sb", [P, 2 * NE])
        mhalf = sb("mhalf", [P, 4])

        QP = Q + 1
        sizes = [RES0 * 2 * QP, 8 * 2 * QP, 4 * 2 * QP, 2 * 2 * QP, 2 * Q, 2 * T5, 2 * T6]
        pool = sb("pool", [P, sum(sizes) + 10 * N])
        at = np.cumsum([0] + sizes)
        act0 = pool[:, 0:at[1]].rearrange("p (r b q) -> p r b q", r=RES0, b=2)
        act1 = pool[:, at[1]:at[2]].rearrange("p (r b q) -> p r b q", r=8, b=2)
        act2 = pool[:, at[2]:at[3]].rearrange("p (r b q) -> p r b q", r=4, b=2)
        act3 = pool[:, at[3]:at[4]].rearrange("p (r b q) -> p r b q", r=2, b=2)
        act4 = pool[:, at[4]:at[5]].rearrange("p (b q) -> p b q", b=2)
        act5 = pool[:, at[5]:at[6]].rearrange("p (b q) -> p b q", b=2)
        act6 = pool[:, at[6]:at[7]]
        work = pool[:, at[7]:]
        sq = work[:, 0:2 * N].rearrange("p (a n) -> p a n", a=2)
        ycp = work[:, 2 * N:4 * N].rearrange("p (a n) -> p a n", a=2)
        nrm = work[:, 4 * N:6 * N].rearrange("p (a n) -> p a n", a=2)
        xin = work[0:XR, 6 * N:8 * N].rearrange("p (a n) -> p a n", a=2)
        prod = work[0:XR, 8 * N:10 * N].rearrange("p (a n) -> p a n", a=2)
        xnorm = sb("xnorm", [XR, 2, N])
        nout = sb("nout", [P, 2, PAD6])
        vv = sb("vv", [P, 2, 4])
        rs = sb("rs", [P, 2, 4])
        pv = sb("pv", [P, 4 * 2 * HALF])
        prx = sb("prx", [P, 4 * 2 * XR])
        nt = sb("nt", [P, 4, 4 * 2 * HALF])

        hb = sb("hb", [P, C2])
        hp = sb("hp", [P, C2])
        xn = sb("xn", [P, 2 * P])
        xnT = sb("xnT", [P, 2, P])
        qT = sb("qT", [P, 2, P])
        kv = sb("kv", [P, 2 * C2])
        km = sb("km", [P, 2, C2])
        ms = sb("ms", [P, 2, C2])
        oT = sb("oT", [P, 2, P])
        st = sb("st", [P, 6])
        mv = sb("mv", [P, 2])
        zero1 = sb("zero1", [P, 1])
        credit = sb("credit", [P, 32])
        credits = iter(range(32))

        def spare():
            c = next(credits)
            return credit[:, c:c + 1]
        tv = sb("tv", [P, 1])
        trs = sb("trs", [P, 1])
        x2T = sb("x2T", [P, 2, P])
        NT = PAIRS + 2
        h2 = sb("h2", [P, NT, C2])
        xT = sb("xT", [P, 2, NT * P])
        lg = sb("lg", [P, NT, 2 * NE])
        h2_flat = h2[:].rearrange("p j n -> p (j n)")
        lg_flat = lg[:].rearrange("p j n -> p (j n)")

        load_w = sem("load_w")
        load_x = sem("load_x")
        inited = sem("inited")
        w_center = sem("w_center")
        w0_ps = sem("w0_ps")
        w0_done = sem("w0_done")
        y_ready = sem("y_ready")
        sq_done = sem("sq_done")
        ycopy_done = sem("ycopy_done")
        colsum_ready = sem("colsum_ready")
        var_ready = sem("var_ready")
        rstd_ready = sem("rstd_ready")
        bcast_ready = sem("bcast_ready")
        norm_done = sem("norm_done")
        gelu_done = sem("gelu_done")
        z_ready = sem("z_ready")
        prod_done = sem("prod_done")
        psum_ready = sem("psum_ready")
        newton = sem("newton")
        prstd_ready = sem("prstd_ready")
        pbc_ready = sem("pbc_ready")
        xn_ready = sem("xn_ready")
        l0_ready = sem("l0_ready")
        l0_gelu = sem("l0_gelu")
        att_ps = sem("att_ps")
        att_sb = sem("att_sb")
        tvar_ready = sem("tvar_ready")
        trstd_ready = sem("trstd_ready")
        dve_seq = sem("dve_seq")
        logits_done = sem("logits_done")
        route_seq = sem("route_seq")
        shifted = sem("shifted")
        exp_done = sem("exp_done")
        count_ready = sem("count_ready")
        count_sum = sem("count_sum")
        route_done = sem("route_done")
        w_load = [sem("w_load0"), sem("w_load1")]
        hid_ps = sem("hid_ps")
        hid_sb = sem("hid_sb")
        ffn_ps = sem("ffn_ps")
        ffn_acc = sem("ffn_acc")
        ffn_tmp = sem("ffn_tmp")
        small_load = sem("small_load")
        stored = sem("stored")

        block = ctx.enter_context(nc.Block())

        o = 0

        def take(n):
            nonlocal o
            o += n
            return pool[:, o - n:o]
        w1_sb = [take(2 * FF).rearrange("p (c f) -> p c f", c=2) for _ in range(2)]
        w2_sb = [take(FC * C2).rearrange("p (c f) -> p c f", c=FC) for _ in range(2)]
        TG = 4
        GN = TG * P
        GROUPS = PAIRS // TG
        hid = [take(FC * GN).rearrange("p (c n) -> p c n", c=FC) for _ in range(2)]
        acc_tmp = take(2 * C2).rearrange("p (a n) -> p a n", a=2)
        rt = take(24 * PAIRS * NE).rearrange("p (r n) -> p r n", r=24)
        b1_sb = sb("b1_sb", [P, 2, FC])
        b2_sb = sb("b2_sb", [P, 2 * NE, C2])
        wm = sb("wm", [P, 2 * NE, PAIRS])
        cnt = sb("cnt", [P, 8, NE])

        BITS = 27
        NEWTON = 9
        N_WLOADS = 27

        @block.sync
        def _(sp):
            for dst, src in [(id_sb[:], ident), (ones_sb[:], onesc), (gmask_sb[:], gmask), (rmask_sb[:], rmask),
                             (ones_pp[:], ones), (center_sb[:], center), (amask_sb[:], amask), (valid_sb[:], valid), (bmask_sb[:], bmask),
                             (tri_sb[:], tri), (wcv[:, 0:TAP0[7], :], wc), (wcv[:, TAP0[7], :], ident),
                             (w0_sb[:], w0), (aff_sb[:], aff),
                             (projw_sb[:], projw), (projb_sb[:], projb.partition_broadcast(P)),
                             (wqkv_sb[:, 0, :], wqkv[0:P, :]), (wqkv_sb[0:CB, 1, :], wqkv[P:C2, :]),
                             (bq_sb[:, 0:1], bq[0:P, :]), (bq_sb[0:CB, 1:2], bq[P:C2, :]),
                             (bkv_sb[:], bkv.partition_broadcast(P)), (wproj_sb[:, 0, :], wproj[0:P, :]),
                             (wproj_sb[0:CB, 1, :], wproj[P:C2, :]), (bproj_sb[:], bproj.partition_broadcast(P)),
                             (wr_sb[:, 0, :], wr[0:P, :]), (wr_sb[0:CB, 1, :], wr[P:C2, :]),
                             (br_sb[:], br.partition_broadcast(P))]:
                sp.dma_start(dst, src).then_inc(load_w, 16)
            sp.dma_start(b2_sb[:].rearrange("p e n -> p (e n)"), b2.partition_broadcast(P)).then_inc(small_load, 16)

            def load_pair(i):
                cols = xt[:, bass.ds(i * N, N)]
                for r in range(RES0):
                    lo = STRIDE0 * r
                    k = min(TAPS0, SPAN - lo)
                    p0 = (r % HALF) * TAPS0
                    sp.dma_start(xin[p0:p0 + k, r // HALF, :], cols[lo:lo + k, :]).then_inc(load_x, 16)
                over = xt[0:TAPS0 - STRIDE0, bass.ds(i * N, N)].rearrange("p (b q) -> p b q", b=2)
                sp.dma_start(xin[XR - (TAPS0 - STRIDE0):XR, 1, :].rearrange("p (b q) -> p b q", b=2)[:, :, 0:Q - 1],
                             over[:, :, 1:Q]).then_inc(load_x, 16)

            sp.wait_ge(inited, 1)
            load_pair(0)
            with sp.Fori(0, PAIRS - 1) as i:
                sp.wait_ge(xn_ready, i + 1)
                load_pair(i + 1)

            sp.wait_ge(logits_done, 1)

            def load_expert(e, k):
                sp.dma_start(b1_sb[:, k, :], b1[bass.ds(e * P, P), :]).then_inc(w_load[k], 16)
                sp.dma_start(w1_sb[k][:, 0, :], w1[bass.ds(e * C2, P), :]).then_inc(w_load[k], 16)
                sp.dma_start(w1_sb[k][0:CB, 1, :], w1[bass.ds(e * C2 + P, CB), :]).then_inc(w_load[k], 16)
                sp.dma_start(w2_sb[k], w2[bass.ds(e * FF, FF), :].rearrange("(c p) n -> p c n", p=P)).then_inc(w_load[k], 16)
            load_expert(0, 0)
            load_expert(1, 1)
            with sp.Fori(0, NE - 1) as e2:
                for k in range(2):
                    sp.wait_ge(ffn_ps, e2 * (2 * PAIRS) + (k + 1) * PAIRS)
                    load_expert(2 * e2 + 2 + k, k)

            sp.wait_ge(ffn_acc, 2 * NE * PAIRS)
            for b in range(2):
                sp.dma_start(out[:, b, :, :].rearrange("j t n -> t j n"),
                             h2[PAD6 * b:PAD6 * b + T6, 2:2 + PAIRS, :]).then_inc(stored, 16)
            sp.wait_ge(stored, 32)

        XLOADS = RES0 + 1

        @block.gpsimd
        def _(pool_e):
            nc.gpsimd.memset(mhalf[:], -0.5)
            nc.gpsimd.memset(act0, 0.0)
            nc.gpsimd.memset(act1, 0.0)
            nc.gpsimd.memset(act2, 0.0)
            nc.gpsimd.memset(act3, 0.0)
            nc.gpsimd.memset(pool[:, at[4]:at[7]], 0.0)
            nc.gpsimd.memset(nout[:], 0.0)
            nc.gpsimd.memset(xn[:], 0.0)
            nc.gpsimd.memset(vv[:], 1.0)
            nc.gpsimd.memset(xin, 0.0).then_inc(inited, 1)

            def token_rstd(i, k):
                pool_e.wait_ge(tvar_ready, i * 2 + k // 6 + 1)
                nc.gpsimd.tensor_tensor(trs[:], tv[:], mhalf[:, 0:1], ALU.pow).then_inc(trstd_ready, 1)

            def body(i, slots, with_next, with_att):
                for what, k in order(slots, with_next, with_att):
                    if what == "bcast":
                        bl = blocks(SPREAD.get(slots[k][0], N))
                        pool_e.wait_ge(var_ready, i * NS + k + 1)
                        nc.gpsimd.tensor_tensor(rs[0:bl[0][1], k % 2, 0:len(bl)], vv[0:bl[0][1], k % 2, 0:len(bl)],
                                                mhalf[0:bl[0][1], 0:len(bl)], ALU.pow).then_inc(rstd_ready, 1)
                    elif what == "att" and k in (0, 6):
                        token_rstd(i, k)

            with pool_e.Fori(0, PAIRS - 1) as i:
                body(i, SLOTS, True, True)
            body(PAIRS - 1, SLOTS, False, True)
            for k in (0, 6):
                token_rstd(PAIRS, k)
            body(PAIRS, TAIL, False, False)
            for k in (0, 6):
                token_rstd(PAIRS + 1, k)

        @block.scalar
        def _(act):
            def l0_tile(i, r):
                act.wait_ge(l0_ready, i * RES0 + r + 1)
                act_in = ps_l0[:, r % 2, 0:N].rearrange("p (b q) -> p b q", b=2)
                nc.scalar.activation(act0[:, r, :, 0:Q], act_in, ACT.Gelu, bias=aff_sb[:, 1, 0:1],
                                     scale=aff_sb[:, 0, 0:1]).then_inc(l0_gelu, 1)

            def finish(i, slots, s):
                layer, t = slots[s]
                n = SPREAD.get(layer, N)
                act.wait_ge(norm_done, i * NS + s + 3)
                src = nrm[:, s % 2, 0:n].rearrange("p (b q) -> p b q", b=2)
                dst = {1: act1[:, t, :, 0:Q], 2: act2[:, t % 4, :, 0:Q], 3: act3[:, t % 2, :, 0:Q],
                       4: act4, 5: act5, 6: act6.rearrange("p (b q) -> p b q", b=2), 7: nout[:, :, 0:T6]}[layer]
                nc.scalar.activation(dst, src, ACT.Identity if layer == 7 else ACT.Gelu,
                                     bias=aff_sb[:, 1, layer:layer + 1],
                                     scale=aff_sb[:, 0, layer:layer + 1]).then_inc(gelu_done, 1)

            def body(i, slots, with_next):
                for what, k in order(slots, with_next, False):
                    if what == "conv":
                        act.wait_ge(ycopy_done, i * NS + k + 3)
                        n = SPREAD.get(slots[k][0], N)
                        nc.scalar.activation(sq[:, k % 2, 0:n], ycp[:, k % 2, 0:n], ACT.Square).then_inc(sq_done, 1)
                    elif what == "bcast":
                        finish(i, slots, k)
                    elif what == "l0":
                        l0_tile(i + 1, k)

            act.wait_ge(load_w, 16 * N_WLOADS)
            for _ in range(2):
                nc.scalar.activation(spare(), ones_sb[:], ACT.Gelu).then_inc(gelu_done, 1)
            for r in range(RES0):
                l0_tile(0, r)
            with act.Fori(0, PAIRS - 1) as i:
                body(i, SLOTS, True)
            body(PAIRS - 1, SLOTS, False)
            body(PAIRS, TAIL, False)

            act.wait_ge(shifted, 1)
            nc.scalar.activation(rt[:, 1:3, :], rt[:, 1:3, :], ACT.Exp).then_inc(exp_done, 1)

            def hidden(e, g, k, kb):
                for f in range(FC):
                    c = (e * GROUPS + g) * FC + f
                    act.wait_ge(hid_ps, c + 1)
                    nc.scalar.activation(hid[k][:, f, :], hid_banks[(k * FC + f) % 4], ACT.Gelu,
                                         bias=b1_sb[:, kb, f:f + 1]).then_inc(hid_sb, 1)

            for _ in range(4):
                nc.scalar.activation(spare(), ones_sb[:], ACT.Gelu).then_inc(hid_sb, 1)
            with act.Fori(0, NE) as e2:
                for kb in range(2):
                    with act.Fori(0, GROUPS // 2) as g2:
                        act.wait_ge(w_load[kb], (e2 + 1) * (4 * 16))
                        for k in range(2):
                            hidden(e2 * 2 + kb, g2 * 2 + k, k, kb)

        @block.vector
        def _(dve):
            links = [0]

            def link(ins, base=0):
                links[0] += 1
                ins.then_inc(dve_seq, 1)
                dve.wait_ge(dve_seq, base + links[0])

            dve.wait_ge(inited, 1)
            dve.wait_ge(load_w, 16 * N_WLOADS)
            nc.vector.memset(spare(), 0.0).then_inc(att_sb, 1)
            for _ in range(2):
                nc.vector.memset(spare(), 0.0).then_inc(norm_done, 1)
                nc.vector.memset(spare(), 0.0).then_inc(ycopy_done, 1)
            link(nc.vector.tensor_reduce(wmean[:], wcv[:], AX_X, ALU.add))
            link(nc.vector.tensor_scalar(wmean[:], wmean[:], 1.0 / C, None, ALU.mult))
            nc.vector.tensor_tensor(wcv[:], wcv[:], wmean[:].unsqueeze(2).to_broadcast([P, NTAP, C]),
                                    ALU.subtract).then_inc(w_center, 1)
            dve.wait_ge(w0_ps, 1)
            link(nc.vector.tensor_copy(w0c[:], ps_a[:, 0:TAPS0].unsqueeze(1).to_broadcast([P, HALF, TAPS0])))
            nc.vector.memset(spare(), 0.0).then_inc(w0_done, 1)
            dve.wait_ge(w0_ps, 2)
            link(nc.vector.tensor_tensor(gram[:], ps_a[0:XR, 0:XR], gmask_sb[:], ALU.mult))
            link(nc.vector.tensor_copy(w0t[:], ps_a[0:XR, P:2 * P]))
            for r in range(HALF):
                last = nc.vector.tensor_scalar(w0r[:, r, :], w0t[:], rmask_sb[:, r:r + 1], None, ALU.mult)
            last.then_inc(w0_done, 1)
            LINK0 = links[0]
            ATT_LINKS = 7

            def rsqrt(i):
                n = [0]

                def then(ins):
                    n[0] += 1
                    ins.then_inc(newton, 1)
                    dve.wait_ge(newton, i * NEWTON + n[0])
                v, y, a, c, d = pv[0:BLK, :], nt[0:BLK, 0, :], nt[0:BLK, 1, :], nt[0:BLK, 2, :], nt[0:BLK, 3, :]
                then(nc.vector.tensor_scalar(v, ps_v[0:BLK, 64:128], EPS, EPS, ALU.add, ALU.max))
                then(nc.vector.tensor_scalar(y.bitcast(I32), v.bitcast(I32), -0.5, float(0x5F3759DF), ALU.mult, ALU.add))
                then(nc.vector.tensor_tensor(a, y, y, ALU.mult))
                then(nc.vector.tensor_tensor(c, a, v, ALU.mult))
                then(nc.vector.tensor_scalar(d, c, 0.375, -1.25, ALU.mult, ALU.add))
                then(nc.vector.tensor_tensor(a, d, c, ALU.mult))
                then(nc.vector.scalar_tensor_tensor(d, a, 1.875, y, ALU.add, ALU.mult))
                then(nc.vector.scalar_tensor_tensor(a, d, -0.5, d, ALU.mult, ALU.mult))
                then(nc.vector.tensor_tensor(c, a, v, ALU.mult))
                wide = [BLK, 4 * 2 * HALF, TAPS0]
                nc.vector.scalar_tensor_tensor(prx[0:BLK].rearrange("p (m k) -> p m k", k=TAPS0),
                                               c.unsqueeze(2).to_broadcast(wide), 1.5,
                                               d.unsqueeze(2).to_broadcast(wide), ALU.add, ALU.mult).then_inc(prstd_ready, 1)

            def prep(i, what):
                if what == "zmm":
                    dve.wait_ge(z_ready, i + 1)
                    nc.vector.tensor_tensor(prod, ps_l0[0:XR, :, 0:N], xin, ALU.mult).then_inc(prod_done, 1)
                elif what == "psum":
                    dve.wait_ge(psum_ready, i + 1)
                    rsqrt(i)
                elif what == "pbc":
                    dve.wait_ge(pbc_ready, i + 1)
                    nc.vector.tensor_tensor(xnorm[:], ps_l0[0:XR, :, 0:N], xin, ALU.mult).then_inc(xn_ready, 1)

            def layernorm(i, half, src, base):
                link(nc.vector.bn_stats(st[:], src), base)
                nc.vector.memset(zero1[:], 0.0)
                link(nc.vector.bn_aggr(mv[:], st[:]), base)
                nc.vector.tensor_scalar(tv[:], mv[:, 1:2], EPS, None, ALU.add).then_inc(tvar_ready, 1)
                dve.wait_ge(trstd_ready, i * 2 + half + 1)
                return nc.vector.tensor_scalar(xn[:, 0:C2], src, mv[:, 0:1], trs[:], ALU.subtract, ALU.mult)

            def attention(i, k):
                if k == 0:
                    links[0] = LINK0
                base = i * ATT_LINKS
                dve.wait_ge(att_ps, i * ATT + k + 1)
                if k == 0:
                    link(nc.vector.tensor_tensor(hb[:], ps_a[:, 0:C2], projb_sb[:], ALU.add), base)
                    layernorm(i, 0, hb[:], base)
                    last = nc.vector.tensor_tensor(hp[:], hb[:], bproj_sb[:], ALU.add)
                elif k == 1:
                    last = nc.vector.tensor_copy(xnT[:], ps_a[:, 0:2 * P].rearrange("p (a n) -> p a n", a=2))
                elif k == 2:
                    nc.vector.tensor_scalar(qT[:, 0, :], ps_a[:, 0:P], bq_sb[:, 0:1], None, ALU.add)
                    last = nc.vector.tensor_scalar(qT[0:CB, 1, :], ps_a[0:CB, P:2 * P], bq_sb[0:CB, 1:2], None, ALU.add)
                elif k == 3:
                    link(nc.vector.tensor_tensor(kv[:], ps_a[:, 0:2 * C2], bkv_sb[:], ALU.add), base)
                    for b in range(2):
                        last = nc.vector.tensor_scalar(km[:, b, :], kv[:, 0:C2], bmask_sb[:, b:b + 1], None, ALU.mult)
                elif k == 4:
                    m = ps_a[:, 0:2 * C2].rearrange("p (b n) -> p b n", b=2)
                    nc.vector.tensor_tensor(ms[:, :, 0:P], m[:, :, 0:P],
                                            amask_sb[:, 0:P].unsqueeze(1).to_broadcast([P, 2, P]), ALU.mult)
                    last = nc.vector.tensor_tensor(ms[0:CB, :, P:C2], m[0:CB, :, P:C2],
                                                   amask_sb[0:CB, P:C2].unsqueeze(1).to_broadcast([CB, 2, CB]), ALU.mult)
                elif k == 5:
                    nc.vector.tensor_copy(oT[:, 0, :], ps_a[:, 0:P])
                    last = nc.vector.tensor_copy(oT[0:CB, 1, :], ps_a[0:CB, P:2 * P])
                elif k == 6:
                    nc.vector.tensor_tensor(h2_flat[:, bass.ds(i * C2, C2)], ps_a[:, 0:C2], hp[:], ALU.add)
                    link(nc.vector.tensor_tensor(hb[:], ps_a[:, 0:C2], hp[:], ALU.add), base)
                    last = layernorm(i, 1, hb[:], base)
                elif k == 7:
                    both = ps_a[:, 0:2 * P].rearrange("p (a n) -> p a n", a=2)
                    nc.vector.tensor_copy(xT[:, :, bass.ds(i * P, P)], both)
                    last = nc.vector.tensor_copy(x2T[:], both)
                else:
                    last = nc.vector.tensor_tensor(lg_flat[:, bass.ds(i * 2 * NE, 2 * NE)],
                                                   ps_a[:, 0:2 * NE], br_sb[:], ALU.add)
                last.then_inc(att_sb, 1)

            def body(i, slots, with_next, with_att):
                for what, k in order(slots, with_next, with_att):
                    T = i * NS + k
                    n = SPREAD.get(slots[k][0], N) if what in ("conv", "colsum", "bcast") else 0
                    if what == "conv":
                        dve.wait_ge(y_ready, T + 1)
                        dve.wait_ge(norm_done, T + 1)
                        nc.vector.tensor_copy(ycp[:, k % 2, 0:n], ps_y[:, k % 2, 0:n]).then_inc(ycopy_done, 1)
                    elif what == "colsum":
                        variance(i, slots, k)
                    elif what == "bcast":
                        dve.wait_ge(bcast_ready, T + 1)
                        dve.wait_ge(gelu_done, T + 1)
                        dve.wait_ge(ycopy_done, T + 3)
                        nc.vector.tensor_tensor(nrm[:, k % 2, 0:n], ycp[:, k % 2, 0:n], ps_r[:, k % 2, 0:n],
                                                ALU.mult).then_inc(norm_done, 1)
                    elif what == "att":
                        attention(i, k)
                    elif what in ("zmm", "psum", "pbc"):
                        prep(i + 1, what)

            def variance(i, slots, k):
                bl = blocks(SPREAD.get(slots[k][0], N))
                dve.wait_ge(colsum_ready, i * NS + k + 1)
                nc.vector.tensor_scalar(vv[0:bl[0][1], k % 2, 0:len(bl)], ps_v[0:bl[0][1], 0:len(bl)], EPS, None,
                                        ALU.add).then_inc(var_ready, 1)

            dve.wait_ge(load_x, 16 * XLOADS)
            for what in ("zmm", "psum", "pbc"):
                prep(0, what)
            with dve.Fori(0, PAIRS - 1) as i:
                body(i, SLOTS, True, True)
            body(PAIRS - 1, SLOTS, False, True)
            for k in range(ATT):
                attention(PAIRS, k)
            body(PAIRS, TAIL, False, False)
            for k in range(ATT):
                attention(PAIRS + 1, k)
            assert links[0] == LINK0 + ATT_LINKS, links[0] - LINK0

            dve.wait_ge(att_sb, ATT * (PAIRS + 2) + 1)
            nc.vector.memset(spare(), 0.0).then_inc(logits_done, 1)
            steps = [0]

            def then(ins):
                steps[0] += 1
                ins.then_inc(route_seq, 1)
                dve.wait_ge(route_seq, steps[0])

            def row(r, n=1):
                return rt[:, r, 0:n * PAIRS]

            def mat(r):
                return rt[:, r, :].rearrange("p (e j) -> p e j", e=NE)

            def rep(a):
                return a.unsqueeze(1).to_broadcast([P, NE, PAIRS])

            logit = [lg[:, 2:2 + PAIRS, NE * u:NE * (u + 1)] for u in range(2)]
            for u in range(2):
                then(nc.vector.tensor_reduce(row(3 + u), logit[u], AX_X, ALU.max))
                then(nc.vector.tensor_tensor(mat(1 + u), logit[u].rearrange("p j e -> p e j"), rep(row(3 + u)), ALU.subtract))
                then(nc.vector.tensor_scalar(rt[:, 5 + u, :], rt[:, 1 + u, :], 0.0, None, ALU.is_equal))
            nc.vector.memset(spare(), 0.0).then_inc(shifted, 1)
            dve.wait_ge(exp_done, 1)
            for u in range(2):
                then(nc.vector.tensor_reduce(row(3 + u), mat(1 + u).rearrange("p e j -> p j e"), AX_X, ALU.add))
                then(nc.vector.reciprocal(row(7 + u), row(3 + u)))
                then(nc.vector.reciprocal(row(9 + u), row(7 + u)))
                then(nc.vector.tensor_tensor(row(9 + u), row(9 + u), row(7 + u), ALU.mult))
                then(nc.vector.tensor_copy(row(11), mat(5 + u)[:, 0, :]))
                for e in range(1, NE):
                    then(nc.vector.tensor_copy(row(12), mat(5 + u)[:, e, :]))
                    then(nc.vector.tensor_tensor(mat(5 + u)[:, e, :], row(12), row(11), ALU.is_gt))
                    then(nc.vector.tensor_tensor(row(11), row(11), row(12), ALU.max))
                then(nc.vector.tensor_tensor(wm[:, NE * u:NE * (u + 1), :], mat(5 + u), rep(row(9 + u)), ALU.mult))
            then(nc.vector.tensor_tensor(mat(13), mat(5), rep(row(7)), ALU.mult))
            then(nc.vector.tensor_scalar(rt[:, 13, :], rt[:, 13, :], valid_sb[:], None, ALU.mult))
            thr, cand, step, ge = cnt[:, 0, :], cnt[:, 1, :], cnt[:, 2, :], cnt[:, 3, :]
            then(nc.vector.memset(step, 1.0))
            then(nc.vector.memset(thr, 0.0))
            PER = 5
            seq0 = steps[0]
            with dve.Fori(0, BITS) as b:
                n = [0]

                def link_b(ins):
                    n[0] += 1
                    ins.then_inc(route_seq, 1)
                    dve.wait_ge(route_seq, b * PER + (seq0 + n[0]))
                link_b(nc.vector.tensor_tensor(cand, thr, step, ALU.add))
                link_b(nc.vector.tensor_tensor(mat(14), mat(13), cand.unsqueeze(2).to_broadcast([P, NE, PAIRS]), ALU.is_ge))
                nc.vector.tensor_reduce(cnt[:, 4, :], mat(14), AX_X, ALU.add).then_inc(count_ready, 1)
                dve.wait_ge(count_sum, b + 1)
                link_b(nc.vector.scalar_tensor_tensor(ge, ps_a[:, 0:NE], float(CAP), step, ALU.is_ge, ALU.mult))
                link_b(nc.vector.tensor_tensor(thr, thr, ge, ALU.add))
                link_b(nc.vector.tensor_scalar(step, step, 0.5, None, ALU.mult))
            steps[0] += BITS * PER
            tb = thr.unsqueeze(2).to_broadcast([P, NE, PAIRS])
            then(nc.vector.tensor_tensor(mat(15), mat(13), tb, ALU.is_gt))
            then(nc.vector.tensor_tensor(mat(16), mat(13), tb, ALU.is_equal))
            then(nc.vector.tensor_tensor(mat(16), mat(16), mat(5), ALU.mult))
            then(nc.vector.tensor_scalar(rt[:, 16, :], rt[:, 16, :], valid_sb[:], None, ALU.mult))
            nc.vector.tensor_reduce(cnt[:, 4, :], mat(15), AX_X, ALU.add).then_inc(count_ready, 1)
            dve.wait_ge(count_sum, BITS + 1)
            then(nc.vector.tensor_scalar(cnt[:, 5, :], ps_a[:, 0:NE], -1.0, float(CAP), ALU.mult, ALU.add))
            then(nc.vector.tensor_copy(mat(17), ps_a[:, 128:256].rearrange("p (e j) -> p e j", e=NE)))
            then(nc.vector.memset(rt[:, 18, :], 0.0))
            then(nc.vector.tensor_copy(mat(18)[:, :, 1:PAIRS], mat(17)[:, :, 0:PAIRS - 1]))
            a, b_ = 18, 19
            d = 1
            while d < PAIRS:
                then(nc.vector.tensor_copy(rt[:, b_, :], rt[:, a, :]))
                then(nc.vector.tensor_tensor(mat(b_)[:, :, d:PAIRS], mat(a)[:, :, d:PAIRS], mat(a)[:, :, 0:PAIRS - d], ALU.add))
                a, b_ = b_, a
                d *= 2
            then(nc.vector.tensor_tensor(rt[:, a, :], rt[:, a, :], ps_a[:, 256:384], ALU.add))
            then(nc.vector.tensor_tensor(mat(20), mat(a), cnt[:, 5, :].unsqueeze(2).to_broadcast([P, NE, PAIRS]), ALU.is_lt))
            then(nc.vector.tensor_tensor(rt[:, 20, :], rt[:, 20, :], rt[:, 16, :], ALU.mult))
            then(nc.vector.tensor_tensor(rt[:, 15, :], rt[:, 15, :], rt[:, 20, :], ALU.add))
            then(nc.vector.tensor_reduce(row(21), mat(15).rearrange("p e j -> p j e"), AX_X, ALU.add))
            then(nc.vector.tensor_scalar(row(21), row(21), -1.0, 1.0, ALU.mult, ALU.add))
            then(nc.vector.tensor_tensor(wm[:, NE:2 * NE, :], wm[:, NE:2 * NE, :], rep(row(21)), ALU.mult))
            nc.vector.memset(spare(), 0.0).then_inc(route_done, 1)

            dve.wait_ge(small_load, 16)
            for _ in range(4):
                nc.vector.memset(spare(), 0.0).then_inc(ffn_tmp, 1)
            b2_flat = b2_sb[:].rearrange("p e n -> p (e n)")
            wm_flat = wm[:].rearrange("p e j -> p (e j)")

            def accumulate(e, g, t):
                c = (e * GROUPS + g) * TG + t
                dve.wait_ge(ffn_ps, c + 1)
                tmp = acc_tmp[:, t % 2, :]
                nc.vector.tensor_tensor(tmp, out_banks[t][:, 0:C2], b2_flat[:, bass.ds(e * C2, C2)],
                                        ALU.add).then_inc(ffn_tmp, 1)
                dve.wait_ge(ffn_tmp, c + 5)
                hrow = h2_flat[:, bass.ds((g * TG + (2 + t)) * C2, C2)]
                nc.vector.scalar_tensor_tensor(hrow, tmp, wm_flat[:, bass.ds(e * PAIRS + (g * TG + t), 1)],
                                               hrow, ALU.mult, ALU.add).then_inc(ffn_acc, 1)
            with dve.Fori(0, 2 * NE) as e:
                with dve.Fori(0, PAIRS // TG // 2) as g2:
                    for k in range(2):
                        for t in range(TG):
                            accumulate(e, 2 * g2 + k, t)

        @block.tensor
        def _(pe):
            mm = nc.tensor.matmul
            pe.wait_ge(load_w, 16 * N_WLOADS)
            last = mm(ps_a[:, 0:TAPS0], center_sb[:], w0_sb[:], start=True, stop=True)
            last.then_inc(w0_ps, 1)
            pe.wait_ge(w0_done, 1)
            w0flat = w0c[:].rearrange("p r k -> p (r k)")
            mm(ps_a[0:XR, 0:XR], w0flat, w0flat, start=True, stop=True)
            mm(ps_a[0:XR, P:2 * P], w0flat, id_sb[:], start=True, stop=True).then_inc(w0_ps, 1)
            pe.wait_ge(w0_done, 2)
            pe.wait_ge(w_center, 1)
            pe.wait_ge(inited, 1)

            def prep(i, what):
                if what == "zmm":
                    pe.wait_ge(load_x, (i + 1) * (16 * XLOADS))
                    pe.wait_ge(l0_gelu, i * RES0)
                    for h in range(2):
                        last = mm(ps_l0[0:XR, h, 0:N], gram[:], xin[:, h, :], start=True, stop=True)
                    last.then_inc(z_ready, 1)
                elif what == "psum":
                    pe.wait_ge(prod_done, i + 1)
                    for j in range(4):
                        for h in range(2):
                            c0 = 64 + (j * 2 + h) * HALF
                            last = mm(ps_v[0:BLK, c0:c0 + HALF], prod[:, h, j * BLK:(j + 1) * BLK], rmask_sb[:],
                                      start=True, stop=True)
                    last.then_inc(psum_ready, 1)
                elif what == "pbc":
                    pe.wait_ge(prstd_ready, i + 1)
                    for h in range(2):
                        for j in range(4):
                            last = mm(ps_l0[0:XR, h, j * BLK:(j + 1) * BLK], prx[0:BLK, (2 * j + h) * XR:(2 * j + h + 1) * XR], id_sb[0:BLK, 0:BLK], start=True, stop=True)
                    last.then_inc(pbc_ready, 1)

            def l0_tile(i, r):
                if r < 2:
                    pe.wait_ge(xn_ready, i + 1)
                else:
                    pe.wait_ge(l0_gelu, i * RES0 + r - 1)
                mm(ps_l0[:, r % 2, 0:N], w0r[:, r % HALF, :], xnorm[:, r // HALF, :], start=True, stop=True).then_inc(l0_ready, 1)

            def need(i, slots, s):
                layer, t = slots[s]
                at = {x: k for k, x in enumerate(slots)}
                if layer == 1:
                    pe.wait_ge(l0_gelu, i * RES0 + min(2 * t + 3, RES0))
                elif layer in (2, 3):
                    half = 4 if layer == 2 else 2
                    reads = [(layer - 1, (2 * t + k) % (2 * half)) for k in range(3)]
                    pe.wait_ge(gelu_done, i * NS + max(at[x] for x in reads) + 3)
                elif layer == 4:
                    pe.wait_ge(gelu_done, i * NS + 2)
                else:
                    pe.wait_ge(gelu_done, i * NS + at[(layer - 1, 0)] + 3)

            def taps(layer, t):
                if layer in (1, 2, 3):
                    src = {1: act0, 2: act1, 3: act2}[layer]
                    R = {1: 16, 2: 8, 3: 4}[layer]
                    return [src[:, (2 * t + k) % R, :, (2 * t + k) // R:(2 * t + k) // R + Q] for k in range(3)]
                if layer == 4:
                    return [act3[:, k % 2, :, k // 2:k // 2 + Q] for k in range(3)]
                if layer == 5:
                    return [act4[:, :, k:k + 2 * T5 - 1:2] for k in range(2)]
                if layer == 6:
                    return [act5[:, :, k:k + 2 * T6 - 1:2] for k in range(2)]
                return [act6.rearrange("p (b q) -> p b q", b=2)]

            def conv(i, slots, s, part):
                layer, t = slots[s]
                n = SPREAD.get(layer, N)
                rows = taps(layer, t)
                first = max(0, len(rows) - 2) if part == 1 else len(rows) - 1 if part == 2 else 0
                last_tap = {0: len(rows) - 2, 1: len(rows) - 1, 2: len(rows)}[part]
                if first == 0:
                    need(i, slots, s)
                    pe.wait_ge(ycopy_done, i * NS + s + 1)
                for k in range(first, last_tap):
                    last = mm(ps_y[:, s % 2, 0:n].rearrange("p (b q) -> p b q", b=2), wcv[:, TAP0[layer] + k, :], rows[k],
                              start=(k == 0), stop=(k == len(rows) - 1))
                if part == 2:
                    last.then_inc(y_ready, 1)

            def colsum(i, slots, s):
                pe.wait_ge(sq_done, i * NS + s + 1)
                bl = blocks(SPREAD.get(slots[s][0], N))
                for j, (c0, w) in enumerate(bl):
                    last = mm(ps_v[0:w, j:j + 1], sq[:, s % 2, c0:c0 + w], ones_sb[:], start=True, stop=True)
                last.then_inc(colsum_ready, 1)

            def bcast(i, slots, s):
                pe.wait_ge(rstd_ready, i * NS + s + 1)
                pe.wait_ge(norm_done, i * NS + s + 1)
                bl = blocks(SPREAD.get(slots[s][0], N))
                for j, (c0, w) in enumerate(bl):
                    last = mm(ps_r[:, s % 2, c0:c0 + w], rs[0:w, s % 2, j:j + 1].to_broadcast([w, P]), id_sb[0:w, 0:w],
                              start=True, stop=True)
                last.then_inc(bcast_ready, 1)

            def attention(i, k, before=None):
                pe.wait_ge(att_sb, i * ATT + k + 1)
                if k == 0:
                    pe.wait_ge(gelu_done, (i * NS if before is None else before) + 2)
                    last = mm(ps_a[:, 0:C2], nout[:].rearrange("p b q -> p (b q)"), projw_sb[:], start=True, stop=True)
                elif k in (1, 7):
                    for c in range(2):
                        last = nc.tensor.transpose(ps_a[:, c * P:(c + 1) * P], xn[:, c * P:(c + 1) * P], id_sb[:])
                elif k == 2:
                    for c, w in ((0, P), (1, CB)):
                        mm(ps_a[0:w, c * P:(c + 1) * P], wqkv_sb[:, 0, c * P:c * P + w], xnT[:, 0, :], start=True, stop=False)
                        last = mm(ps_a[0:w, c * P:(c + 1) * P], wqkv_sb[0:CB, 1, c * P:c * P + w], xnT[0:CB, 1, :],
                                  start=False, stop=True)
                elif k == 3:
                    mm(ps_a[:, 0:2 * C2], xnT[:, 0, :], wqkv_sb[:, 0, C2:3 * C2], start=True, stop=False)
                    last = mm(ps_a[:, 0:2 * C2], xnT[0:CB, 1, :], wqkv_sb[0:CB, 1, C2:3 * C2], start=False, stop=True)
                elif k == 4:
                    for b in range(2):
                        mm(ps_a[:, b * C2:b * C2 + P], km[:, b, 0:P], kv[:, C2:C2 + P], start=True, stop=True)
                        last = mm(ps_a[0:CB, b * C2 + P:(b + 1) * C2], km[:, b, P:C2], kv[:, C2 + P:2 * C2],
                                  start=True, stop=True)
                elif k == 5:
                    for b in range(2):
                        cols = slice(PAD6 * b, PAD6 * (b + 1))
                        mm(ps_a[:, cols], ms[:, b, 0:P], qT[:, 0, cols], start=True, stop=True)
                        last = mm(ps_a[0:CB, P + PAD6 * b:P + PAD6 * (b + 1)], ms[0:CB, b, P:C2], qT[0:CB, 1, cols],
                                  start=True, stop=True)
                elif k == 6:
                    mm(ps_a[:, 0:C2], oT[:, 0, :], wproj_sb[:, 0, :], start=True, stop=False)
                    last = mm(ps_a[:, 0:C2], oT[0:CB, 1, :], wproj_sb[0:CB, 1, :], start=False, stop=True)
                else:
                    mm(ps_a[:, 0:2 * NE], x2T[:, 0, :], wr_sb[:, 0, :], start=True, stop=False)
                    last = mm(ps_a[:, 0:2 * NE], x2T[0:CB, 1, :], wr_sb[0:CB, 1, :], start=False, stop=True)
                last.then_inc(att_ps, 1)

            def body(i, slots, with_next, with_att):
                for what, k in order(slots, with_next, with_att):
                    if what in ("tap0", "tap1", "conv"):
                        conv(i, slots, k, ("tap0", "tap1", "conv").index(what))
                    elif what == "colsum":
                        colsum(i, slots, k)
                    elif what == "bcast":
                        bcast(i, slots, k)
                    elif what == "att":
                        attention(i, k)
                    elif what == "l0":
                        l0_tile(i + 1, k)
                    elif what == "psum":
                        pe.wait_ge(var_ready, i * NS + k)
                        prep(i + 1, what)
                        pe.wait_ge(newton, (i + 1) * NEWTON + 1)
                    else:
                        prep(i + 1, what)

            for what in ("zmm", "psum", "pbc"):
                prep(0, what)
            for r in range(RES0):
                l0_tile(0, r)
            with pe.Fori(0, PAIRS - 1) as i:
                body(i, SLOTS, True, True)
            body(PAIRS - 1, SLOTS, False, True)
            for k in range(ATT):
                attention(PAIRS, k)
            body(PAIRS, TAIL, False, False)
            for k in range(ATT):
                attention(PAIRS + 1, k, before=PAIRS * NS + len(TAIL))

            with pe.Fori(0, BITS) as b:
                pe.wait_ge(count_ready, b + 1)
                mm(ps_a[:, 0:NE], ones_pp[:], cnt[:, 4, :], start=True, stop=True).then_inc(count_sum, 1)
            pe.wait_ge(count_ready, BITS + 1)
            mm(ps_a[:, 0:NE], ones_pp[:], cnt[:, 4, :], start=True, stop=True)
            mm(ps_a[:, 128:256], ones_pp[:], rt[:, 16, :], start=True, stop=True)
            mm(ps_a[:, 256:384], tri_sb[:], rt[:, 16, :], start=True, stop=True).then_inc(count_sum, 1)

            pe.wait_ge(route_done, 1)

            def up(group, g, k, kb):
                cols = bass.ds(g * GN + 2 * P, GN)
                for f in range(FC):
                    pe.wait_ge(hid_sb, group * FC + f + 1)
                    bank = hid_banks[(k * FC + f) % 4]
                    mm(bank, w1_sb[kb][:, 0, f * P:(f + 1) * P], xT[:, 0, cols], start=True, stop=False)
                    mm(bank, w1_sb[kb][0:CB, 1, f * P:(f + 1) * P], xT[0:CB, 1, cols], start=False, stop=True).then_inc(hid_ps, 1)

            def down(group, k, kb):
                pe.wait_ge(hid_sb, (group + 1) * FC + 4)
                for t in range(TG):
                    pe.wait_ge(ffn_tmp, group * TG + t + 1)
                    for f in range(FC):
                        last = mm(out_banks[t][:, 0:C2], hid[k][:, f, t * P:(t + 1) * P], w2_sb[kb][:, f, :],
                                  start=(f == 0), stop=(f == FC - 1))
                    last.then_inc(ffn_ps, 1)

            with pe.Fori(0, NE) as e2:
                for kb in range(2):
                    with pe.Fori(0, GROUPS // 2) as g2:
                        pe.wait_ge(w_load[kb], (e2 + 1) * (4 * 16))
                        group = e2 * (2 * GROUPS) + (g2 * 2 + kb * GROUPS)
                        for k in range(2):
                            up(group + k, g2 * 2 + k, k, kb)
                        for k in range(2):
                            down(group + k, k, kb)


_OUT = (B, T6, C2)


def _constants():
    f = np.float32
    p = np.arange(P)
    ident = np.eye(P, dtype=f)
    rows = np.arange(XR) // TAPS0
    amask = np.zeros((P, C2), f)
    amask[:, 0:P] = (p[:, None] // HEAD == p[None, :] // HEAD) * HEAD ** -0.5
    amask[0:CB, P:] = amask[0:CB, 0:CB]
    return {
        "ident": ident,
        "center": (ident - f(1.0 / P)).astype(f),
        "ones": np.ones((P, P), f),
        "onesc": np.full((P, 1), 1.0 / P, f),
        "gmask": ((rows[:, None] == rows[None, :]) / P).astype(f),
        "rmask": (rows[:, None] == np.arange(HALF)[None, :]).astype(f),
        "amask": amask,
        "valid": (p % PAD6 < T6).astype(f)[:, None].copy(),
        "bmask": ((p[:, None] // PAD6 == np.arange(2)[None, :]) & (p[:, None] % PAD6 < T6)).astype(f),
        "tri": (p[:, None] < p[None, :]).astype(f),
    }


def kernel(**inputs):
    import concourse.bacc as bacc
    from concourse.bass_utils import run_bass_kernel_spmd

    a = {k: np.asarray(v) for k, v in inputs.items()}
    tok, att, ffn = "L0_tok_", "L0_attn_", "L0_ffn_"
    arrays = {
        "xt": a["x"].reshape(B, Q, SPAN).transpose(2, 0, 1).reshape(SPAN, B * Q),
        "w0": a[tok + "conv_w0"][:, 0, :],
        "wc": np.concatenate([a[f"{tok}conv_w{i}"].transpose(1, 2, 0) for i in range(1, 7)], axis=1),
        "aff": np.stack([np.stack([a[f"{tok}ln_{c}{i}"] for i in range(7)] + [a[f"{tok}fln_{c}"]], axis=1)
                         for c in "gb"], axis=1),
        "projw": a[tok + "proj_w"], "projb": a[tok + "proj_b"],
        "wqkv": a[att + "w_qkv"], "bq": a[att + "b_qkv"][0:C2].reshape(C2, 1), "bkv": a[att + "b_qkv"][C2:],
        "wproj": a[att + "w_proj"], "bproj": a[att + "b_proj"],
        "wr": np.concatenate([a[ffn + "Wsc"], a[ffn + "Wsu"]], axis=1),
        "br": np.concatenate([a[ffn + "bsc"], a[ffn + "bsu"]]),
        "w1": np.concatenate([a[ffn + "W1c"], a[ffn + "W1u"]]).reshape(2 * NE * C2, FF),
        "b1": np.concatenate([a[ffn + "b1c"], a[ffn + "b1u"]]).reshape(2 * NE, FC, P).transpose(0, 2, 1).reshape(-1, FC),
        "w2": np.concatenate([a[ffn + "W2c"], a[ffn + "W2u"]]).reshape(2 * NE * FF, C2),
        "b2": np.concatenate([a[ffn + "b2c"], a[ffn + "b2u"]]).reshape(-1),
        **_constants(),
    }
    arrays = {f"in_{k}": np.ascontiguousarray(v) for k, v in arrays.items()}
    nc = bacc.Bacc("TRN2", target_bir_lowering=False, num_devices=1)
    args = [nc.dram_tensor(k, v.shape, mybir.dt.from_np(v.dtype), kind="ExternalInput").ap() for k, v in arrays.items()]
    out = nc.dram_tensor("out_dram", _OUT, F32, kind="ExternalOutput").ap()
    audio_tower(nc, *args, out.rearrange("(j b) t n -> j b t n", b=2))
    r = run_bass_kernel_spmd(nc, [arrays], core_ids=[0])
    return r.results[0]["out_dram"]
```

```python
from contextlib import ExitStack

import numpy as np

import concourse.bass as bass
from concourse import mybir

ALU = mybir.AluOpType
ACT = mybir.ActivationFunctionType
F32 = mybir.dt.float32
I32 = mybir.dt.int32
U32 = mybir.dt.uint32
AX_X = mybir.AxisListType.X

P = 128
B, SAMPLES = 64, 20000
STRIDE0, TAPS0 = 5, 10
RES0 = 16
Q = SAMPLES // (STRIDE0 * RES0)
SPAN = STRIDE0 * RES0
HALF = RES0 // 2
XR = HALF * TAPS0
PAIRS = B // 2
N = 2 * Q
BLK = Q // 2
T5, T6 = 124, 62
PAD6 = 64
C, C2 = 128, 192
CB = C2 - P
HEAD = 16
EPS = 1e-5
NE, FF = 4, 768
FC = FF // P
CAP = B * T6 // NE
TAPS = {1: 3, 2: 3, 3: 3, 4: 3, 5: 2, 6: 2, 7: 1}
TAP0 = {1: 0, 2: 3, 3: 6, 4: 9, 5: 12, 6: 14, 7: 16}
NTAP = 17

TOKENS = B * T6
COMMON = (TOKENS + NE * (P - 1)) // P
UNIQUE = (TOKENS - CAP + NE * (P - 1)) // P
UNIQUE += (COMMON + UNIQUE) % 2
TILES = COMMON + UNIQUE
ROWS = TILES * P
TRASH = [ROWS, ROWS + PAIRS * P]

SLOTS = [(1, 0), (1, 1), (4, 0), (1, 2), (1, 3), (5, 0), (1, 4), (1, 5), (6, 0), (1, 6), (2, 0), (1, 7),
         (2, 1), (2, 2), (2, 3), (7, 0), (3, 0), (3, 1)]
TAIL = [(4, 0), (5, 0), (6, 0), (7, 0)]
NS = len(SLOTS)
SPREAD = {4: N, 5: 2 * T5, 6: 2 * T6, 7: 2 * T6}
EXTRA = {1: "z", 2: "a0", 3: "pc", 4: "a1", 5: "pb", 6: "a2", 8: "a3", 9: "a4", 11: "a5 l", 12: "l l l", 13: "a6 l l",
         14: "l l l", 15: "a7 l l", 16: "a8 l l", 17: "l R S l l R"}
ATT = 9


def order(slots, with_next, with_att):
    n, l0 = len(slots), 0
    if n < NS:
        return [(what, s) for s in range(n) for what in ("tap0", "tap1", "conv", "colsum", "bcast")]
    out, bc = [], 0
    for s in range(n):
        out.append(("tap0", s))
        if s >= 2:
            out.append(("bcast", bc))
            bc += 1
        out.append(("tap1", s))
        if s:
            out.append(("colsum", s - 1))
        out.append(("conv", s))
        for word in EXTRA.get(s, "").split():
            if word == "S":
                out.append(("colsum", s))
            elif word == "R":
                out.append(("bcast", bc))
                bc += 1
            elif word[0] == "a":
                if with_att:
                    out.append(("att", int(word[1:])))
            elif with_next:
                if word == "l":
                    out.append(("l0", l0))
                    l0 += 1
                else:
                    out.append(({"z": "zmm", "pc": "psum", "pb": "pbc"}[word], s))
    assert bc == n and l0 in (0, RES0)
    return out


def blocks(n):
    k = -(-n // P)
    assert n % k == 0
    return [(j * (n // k), n // k) for j in range(k)]


def audio_tower(nc, xt, w0, wc, aff, projw, projb, wqkv, bq, bkv, wproj, bproj, wr, br, w1, b1, w2, b2,
                ident, center, ones, onesc, gmask, rmask, amask, valid, bmask, tri, iota, ids,
                xs_dram, yc_dram, yu_dram, out):
    with ExitStack() as ctx:
        def sb(name, shape, dt=F32):
            return ctx.enter_context(nc.sbuf_tensor(name, shape, dt))

        def psum(name, shape):
            return ctx.enter_context(nc.psum_tensor(name, shape, F32))

        def sem(name):
            return ctx.enter_context(nc.semaphore(name))

        ps_l0 = psum("ps_l0", [P, 2, 512])
        ps_y = psum("ps_y", [P, 2, 512])
        ps_r = psum("ps_r", [P, 2, 512])
        ps_v = psum("ps_v", [P, 512])
        ps_a = psum("ps_a", [P, 512])
        up_banks = [ps_l0, ps_y]
        out_banks = [ps_r[:, 0, :], ps_r[:, 1, :]]

        id_sb = sb("id_sb", [P, P])
        ones_sb = sb("ones_sb", [P, 1])
        gmask_sb = sb("gmask_sb", [XR, XR])
        rmask_sb = sb("rmask_sb", [XR, HALF])
        ones_pp = sb("ones_pp", [P, P])
        amask_sb = sb("amask_sb", [P, C2])
        valid_sb = sb("valid_sb", [P, 1])
        bmask_sb = sb("bmask_sb", [P, 2])
        tri_sb = sb("tri_sb", [P, P])
        wmean = sb("wmean", [P, NTAP])
        w0_sb = sb("w0_sb", [P, TAPS0])
        gram = sb("gram", [XR, XR])
        aff_sb = sb("aff_sb", [P, 2, 8])
        bq_sb = sb("bq_sb", [P, 2])
        wr_sb = sb("wr_sb", [P, 2, 2 * NE])
        br_sb = sb("br_sb", [P, 2 * NE])
        mhalf = sb("mhalf", [P, 4])

        QP = Q + 1
        sizes = [RES0 * 2 * QP, 8 * 2 * QP, 4 * 2 * QP, 2 * 2 * QP, 2 * Q, 2 * T5, 2 * T6]
        views = {"wcv": (P, NTAP, C), "center_sb": (P, P), "w0c": (P, HALF, TAPS0), "w0t": (XR, P),
                 "w0r": (XR, HALF, P), "projw_sb": (P, C2), "projb_sb": (P, C2), "wqkv_sb": (P, 2, 3 * C2),
                 "bkv_sb": (P, 2 * C2), "wproj_sb": (P, 2, C2), "bproj_sb": (P, C2), "xnorm": (XR, 2, N),
                 "prx": (P, 4 * 2 * XR), "nt": (P, 4, 4 * 2 * HALF), "hb": (P, C2), "hp": (P, C2), "xn": (P, 2 * P),
                 "xnT": (P, 2, P), "qT": (P, 2, P), "kv": (P, 2 * C2), "km": (P, 2, C2), "ms": (P, 2, C2),
                 "oT": (P, 2, P), "x2T": (P, 2, P)}
        size_of = {name: int(np.prod(shape[1:])) for name, shape in views.items()}
        pool = sb("pool", [P, sum(sizes) + 10 * N + sum(size_of.values())])
        at = np.cumsum([0] + sizes)
        act0 = pool[:, 0:at[1]].rearrange("p (r b q) -> p r b q", r=RES0, b=2)
        act1 = pool[:, at[1]:at[2]].rearrange("p (r b q) -> p r b q", r=8, b=2)
        act2 = pool[:, at[2]:at[3]].rearrange("p (r b q) -> p r b q", r=4, b=2)
        act3 = pool[:, at[3]:at[4]].rearrange("p (r b q) -> p r b q", r=2, b=2)
        act4 = pool[:, at[4]:at[5]].rearrange("p (b q) -> p b q", b=2)
        act5 = pool[:, at[5]:at[6]].rearrange("p (b q) -> p b q", b=2)
        act6 = pool[:, at[6]:at[7]]
        work = pool[:, at[7]:at[7] + 10 * N]
        starts = dict(zip(size_of, np.cumsum([at[7] + 10 * N] + list(size_of.values()))))

        def view(name):
            a = pool[0:views[name][0], starts[name]:starts[name] + size_of[name]]
            if len(views[name]) == 3:
                a = a.rearrange("p (a n) -> p a n", a=views[name][1])
            return a
        wcv, center_sb, w0c, w0t, w0r = view("wcv"), view("center_sb"), view("w0c"), view("w0t"), view("w0r")
        projw_sb, projb_sb, wqkv_sb, bkv_sb = view("projw_sb"), view("projb_sb"), view("wqkv_sb"), view("bkv_sb")
        wproj_sb, bproj_sb, xnorm, prx, nt = view("wproj_sb"), view("bproj_sb"), view("xnorm"), view("prx"), view("nt")
        hb, hp, xn, xnT, qT, kv = view("hb"), view("hp"), view("xn"), view("xnT"), view("qT"), view("kv")
        km, ms, oT, x2T = view("km"), view("ms"), view("oT"), view("x2T")
        sq = work[:, 0:2 * N].rearrange("p (a n) -> p a n", a=2)
        ycp = work[:, 2 * N:4 * N].rearrange("p (a n) -> p a n", a=2)
        nrm = work[:, 4 * N:6 * N].rearrange("p (a n) -> p a n", a=2)
        xin = work[0:XR, 6 * N:8 * N].rearrange("p (a n) -> p a n", a=2)
        prod = work[0:XR, 8 * N:10 * N].rearrange("p (a n) -> p a n", a=2)
        nout = sb("nout", [P, 2, PAD6])
        vv = sb("vv", [P, 2, 4])
        rs = sb("rs", [P, 2, 4])
        pv = sb("pv", [P, 4 * 2 * HALF])

        st = sb("st", [P, 6])
        mv = sb("mv", [P, 2])
        zero1 = sb("zero1", [P, 1])
        credit = sb("credit", [P, 32])
        credits = iter(range(32))

        def spare():
            c = next(credits)
            return credit[:, c:c + 1]
        tv = sb("tv", [P, 1])
        trs = sb("trs", [P, 1])
        NT = PAIRS + 2
        h2 = sb("h2", [P, NT, C2])
        x2 = sb("x2", [P, NT, C2])
        lg = sb("lg", [P, NT, 2 * NE])
        x2_flat = x2[:].rearrange("p j n -> p (j n)")
        h2_flat = h2[:].rearrange("p j n -> p (j n)")
        lg_flat = lg[:].rearrange("p j n -> p (j n)")

        load_w = sem("load_w")
        load_x = sem("load_x")
        inited = sem("inited")
        w_center = sem("w_center")
        w0_ps = sem("w0_ps")
        w0_done = sem("w0_done")
        y_ready = sem("y_ready")
        sq_done = sem("sq_done")
        ycopy_done = sem("ycopy_done")
        colsum_ready = sem("colsum_ready")
        var_ready = sem("var_ready")
        rstd_ready = sem("rstd_ready")
        bcast_ready = sem("bcast_ready")
        norm_done = sem("norm_done")
        gelu_done = sem("gelu_done")
        z_ready = sem("z_ready")
        prod_done = sem("prod_done")
        psum_ready = sem("psum_ready")
        newton = sem("newton")
        prstd_ready = sem("prstd_ready")
        pbc_ready = sem("pbc_ready")
        xn_ready = sem("xn_ready")
        l0_ready = sem("l0_ready")
        l0_gelu = sem("l0_gelu")
        att_ps = sem("att_ps")
        att_sb = sem("att_sb")
        tvar_ready = sem("tvar_ready")
        trstd_ready = sem("trstd_ready")
        dve_seq = sem("dve_seq")
        logits_done = sem("logits_done")
        route_seq = sem("route_seq")
        shifted = sem("shifted")
        exp_done = sem("exp_done")
        count_ready = sem("count_ready")
        count_sum = sem("count_sum")
        placed = sem("placed")
        cleared = sem("cleared")
        w_load = sem("w_load")
        scattered = [sem("scattered_c"), sem("scattered_u")]
        gathered_c = sem("gathered_c")
        gathered_u = [sem(f"gathered_u{q}") for q in range(4)]
        x_load = [sem("x_load0"), sem("x_load1")]
        xt_ps = sem("xt_ps")
        xt_sb = sem("xt_sb")
        w1_ready = sem("w1_ready")
        hid_ps = sem("hid_ps")
        hid_sb = sem("hid_sb")
        down_ps = sem("down_ps")
        y_sb = sem("y_sb")
        y_store = [sem("y_store0"), sem("y_store1")]
        mixed_c = sem("mixed_c")
        mixed_u = sem("mixed_u")
        small_load = sem("small_load")
        stored = sem("stored")

        block = ctx.enter_context(nc.Block())

        o = 0

        def take(n):
            nonlocal o
            o += n
            return pool[:, o - n:o]
        w1_all = take(2 * NE * 2 * FF)
        w2_all = take(2 * NE * FC * C2)
        w1_cur = [take(2 * FF).rearrange("p (c f) -> p c f", c=2) for _ in range(2)]
        hid = [take(FF).rearrange("p (f n) -> p f n", f=FC) for _ in range(2)]
        xt_tok = [take(C2) for _ in range(2)]
        xt_ch = [take(2 * P).rearrange("p (a n) -> p a n", a=2) for _ in range(2)]
        y_tok = [take(C2) for _ in range(2)]
        rt = take(24 * PAIRS * NE).rearrange("p (r n) -> p r n", r=24)
        ntile = take(NE * PAIRS).rearrange("p (e j) -> p e j", e=NE)
        later = take(NE * TILES).rearrange("p (e j) -> p e j", e=NE)
        assert o <= pool.shape[1], (o, pool.shape)
        b2_sb = sb("b2_sb", [P, 2 * NE, C2])
        wm = sb("wm", [P, 2, PAIRS])
        cnt = sb("cnt", [P, 8, NE])
        begin = sb("begin", [P, NE])
        iota_sb = sb("iota_sb", [P, PAIRS + 2])
        ids_sb = sb("ids_sb", [P, PAIRS])
        dest = sb("dest", [P, 2, PAIRS], U32)
        src = sb("src", [P, 2, PAIRS], U32)
        expert = sb("expert", [P, TILES], I32)
        zrow = sb("zrow", [P, C2])

        HID_BANKS = [(0, 4), (4, FC)]
        BITS = 27
        NEWTON = 9
        N_WLOADS = 29

        yu = w1_all[:, 0:PAIRS * C2].rearrange("p (j n) -> p j n", j=PAIRS)

        @block.sync
        def _(sp):
            for dst, src in [(id_sb[:], ident), (ones_sb[:], onesc), (gmask_sb[:], gmask), (rmask_sb[:], rmask),
                             (ones_pp[:], ones), (center_sb[:], center), (amask_sb[:], amask), (valid_sb[:], valid), (bmask_sb[:], bmask),
                             (tri_sb[:], tri), (iota_sb[:], iota), (ids_sb[:], ids), (wcv[:, 0:TAP0[7], :], wc), (wcv[:, TAP0[7], :], ident),
                             (w0_sb[:], w0), (aff_sb[:], aff),
                             (projw_sb[:], projw), (projb_sb[:], projb.partition_broadcast(P)),
                             (wqkv_sb[:, 0, :], wqkv[0:P, :]), (wqkv_sb[0:CB, 1, :], wqkv[P:C2, :]),
                             (bq_sb[:, 0:1], bq[0:P, :]), (bq_sb[0:CB, 1:2], bq[P:C2, :]),
                             (bkv_sb[:], bkv.partition_broadcast(P)), (wproj_sb[:, 0, :], wproj[0:P, :]),
                             (wproj_sb[0:CB, 1, :], wproj[P:C2, :]), (bproj_sb[:], bproj.partition_broadcast(P)),
                             (wr_sb[:, 0, :], wr[0:P, :]), (wr_sb[0:CB, 1, :], wr[P:C2, :]),
                             (br_sb[:], br.partition_broadcast(P))]:
                sp.dma_start(dst, src).then_inc(load_w, 16)
            sp.dma_start(b2_sb[:].rearrange("p e n -> p (e n)"), b2.partition_broadcast(P)).then_inc(small_load, 16)

            def load_pair(i):
                cols = xt[:, bass.ds(i * N, N)]
                for r in range(RES0):
                    lo = STRIDE0 * r
                    k = min(TAPS0, SPAN - lo)
                    p0 = (r % HALF) * TAPS0
                    sp.dma_start(xin[p0:p0 + k, r // HALF, :], cols[lo:lo + k, :]).then_inc(load_x, 16)
                over = xt[0:TAPS0 - STRIDE0, bass.ds(i * N, N)].rearrange("p (b q) -> p b q", b=2)
                sp.dma_start(xin[XR - (TAPS0 - STRIDE0):XR, 1, :].rearrange("p (b q) -> p b q", b=2)[:, :, 0:Q - 1],
                             over[:, :, 1:Q]).then_inc(load_x, 16)

            sp.wait_ge(inited, 1)
            for c in range(0, TILES, 2):
                sp.dma_start(xs_dram[c * P:(c + 2) * P, :].rearrange("(a p) n -> p a n", p=P),
                             zrow[:].unsqueeze(1).to_broadcast([P, 2, C2])).then_inc(cleared, 16)
            load_pair(0)
            with sp.Fori(0, PAIRS - 1) as i:
                sp.wait_ge(xn_ready, i + 1)
                load_pair(i + 1)

            sp.wait_ge(logits_done, 1)
            for e in range(2 * NE):
                at_e = w1_all[:, e * 2 * FF:(e + 1) * 2 * FF]
                sp.dma_start(at_e[:, 0:FF], w1[e * C2:e * C2 + P, :]).then_inc(w_load, 16)
                sp.dma_start(at_e[0:CB, FF:2 * FF], w1[e * C2 + P:(e + 1) * C2, :]).then_inc(w_load, 16)
                sp.dma_start(at_e[CB:CB + 1, FF:2 * FF], b1[e:e + 1, :]).then_inc(w_load, 16)
                sp.dma_start(w2_all[:, e * FC * C2:(e + 1) * FC * C2].rearrange("p (c n) -> p c n", c=FC),
                             w2[e * FF:(e + 1) * FF, :].rearrange("(c p) n -> p c n", p=P)).then_inc(w_load, 16)

            def load_tile(row, k):
                sp.dma_start(xt_tok[k], xs_dram[bass.ds(row, P), :]).then_inc(x_load[k], 16)

            def store_tile(t, k, rows):
                rows, row = (yc_dram, t * P) if rows == "common" else (yu_dram, (t - COMMON) * P)
                sp.dma_start(rows[bass.ds(row, P), :], y_tok[k]).then_inc(y_store[k], 16)

            def steps(g, rows):
                for k in range(2):
                    sp.wait_ge(xt_ps, 2 * g + (k + 1))
                    load_tile((2 * g + 2 + k) * P, k)
                    if rows[k]:
                        sp.wait_ge(y_sb, 2 * g + (k + 2))
                        store_tile(2 * g + (k - 1), 1 - k, rows[k])
            sp.wait_ge(scattered[0], 16 * PAIRS)
            for k in range(2):
                load_tile(k * P, k)
            half = COMMON // 2
            steps(0, (None, "common"))
            with sp.Fori(0, half - 2) as g:
                steps(g + 1, ("common", "common"))
            sp.wait_ge(scattered[1], 16 * PAIRS)
            steps(half - 1, ("common", "common"))
            steps(half, ("common", "unique"))
            with sp.Fori(0, UNIQUE // 2 - 2) as g:
                steps(g + (half + 1), ("unique", "unique"))
            for t in range(TILES - 3, TILES):
                sp.wait_ge(y_sb, t + 3)
                store_tile(t, t % 2, "unique")

            for q in range(4):
                sp.wait_ge(mixed_u, (q + 1) * 8)
                for b in range(2):
                    sp.dma_start(out[8 * q:8 * q + 8, b, :, :].rearrange("j t n -> t j n"),
                                 h2[PAD6 * b:PAD6 * b + T6, 2 + 8 * q:10 + 8 * q, :]).then_inc(stored, 16)
            sp.wait_ge(stored, 16 * 8)

        XLOADS = RES0 + 1

        @block.gpsimd
        def _(pool_e):
            nc.gpsimd.memset(mhalf[:], -0.5)
            nc.gpsimd.memset(act0, 0.0)
            nc.gpsimd.memset(act1, 0.0)
            nc.gpsimd.memset(act2, 0.0)
            nc.gpsimd.memset(act3, 0.0)
            nc.gpsimd.memset(pool[:, at[4]:at[7]], 0.0)
            nc.gpsimd.memset(nout[:], 0.0)
            nc.gpsimd.memset(zrow[:], 0.0)
            nc.gpsimd.memset(xn, 0.0)
            nc.gpsimd.memset(vv[:], 1.0)
            nc.gpsimd.memset(xin, 0.0).then_inc(inited, 1)

            def token_rstd(i, k):
                pool_e.wait_ge(tvar_ready, i * 2 + k // 6 + 1)
                nc.gpsimd.tensor_tensor(trs[:], tv[:], mhalf[:, 0:1], ALU.pow).then_inc(trstd_ready, 1)

            def body(i, slots, with_next, with_att):
                for what, k in order(slots, with_next, with_att):
                    if what == "bcast":
                        bl = blocks(SPREAD.get(slots[k][0], N))
                        pool_e.wait_ge(var_ready, i * NS + k + 1)
                        nc.gpsimd.tensor_tensor(rs[0:bl[0][1], k % 2, 0:len(bl)], vv[0:bl[0][1], k % 2, 0:len(bl)],
                                                mhalf[0:bl[0][1], 0:len(bl)], ALU.pow).then_inc(rstd_ready, 1)
                    elif what == "att" and k in (0, 6):
                        token_rstd(i, k)

            with pool_e.Fori(0, PAIRS - 1) as i:
                body(i, SLOTS, True, True)
            body(PAIRS - 1, SLOTS, False, True)
            for k in (0, 6):
                token_rstd(PAIRS, k)
            body(PAIRS, TAIL, False, False)
            for k in (0, 6):
                token_rstd(PAIRS + 1, k)

            pool_e.wait_ge(cleared, 16 * TILES // 2)
            offset = bass.IndirectOffsetOnAxis
            for u in range(2):
                pool_e.wait_ge(placed, u + 1)
                for j in range(PAIRS):
                    nc.gpsimd.indirect_dma_start(xs_dram, offset(ap=dest[:, u, j:j + 1], axis=0), x2[:, 2 + j, :],
                                                 None).then_inc(scattered[u], 16)
            pool_e.wait_ge(scattered[1], 16 * PAIRS)
            for k in range(2):
                pool_e.wait_ge(y_store[k], 16 * (COMMON // 2 + 1))
            for j in range(PAIRS):
                nc.gpsimd.indirect_dma_start(x2[:, 2 + j, :], None, yc_dram,
                                             offset(ap=src[:, 0, j:j + 1], axis=0)).then_inc(gathered_c, 16)
            for k in range(2):
                pool_e.wait_ge(y_store[k], 16 * (TILES // 2 + 1))
            for j in range(PAIRS):
                nc.gpsimd.indirect_dma_start(yu[:, j, :], None, yu_dram,
                                             offset(ap=src[:, 1, j:j + 1], axis=0)).then_inc(gathered_u[j // 8], 16)

        @block.scalar
        def _(act):
            def l0_tile(i, r):
                act.wait_ge(l0_ready, i * RES0 + r + 1)
                act_in = ps_l0[:, r % 2, 0:N].rearrange("p (b q) -> p b q", b=2)
                nc.scalar.activation(act0[:, r, :, 0:Q], act_in, ACT.Gelu, bias=aff_sb[:, 1, 0:1],
                                     scale=aff_sb[:, 0, 0:1]).then_inc(l0_gelu, 1)

            def finish(i, slots, s):
                layer, t = slots[s]
                n = SPREAD.get(layer, N)
                act.wait_ge(norm_done, i * NS + s + 3)
                src = nrm[:, s % 2, 0:n].rearrange("p (b q) -> p b q", b=2)
                dst = {1: act1[:, t, :, 0:Q], 2: act2[:, t % 4, :, 0:Q], 3: act3[:, t % 2, :, 0:Q],
                       4: act4, 5: act5, 6: act6.rearrange("p (b q) -> p b q", b=2), 7: nout[:, :, 0:T6]}[layer]
                nc.scalar.activation(dst, src, ACT.Identity if layer == 7 else ACT.Gelu,
                                     bias=aff_sb[:, 1, layer:layer + 1],
                                     scale=aff_sb[:, 0, layer:layer + 1]).then_inc(gelu_done, 1)

            def body(i, slots, with_next):
                for what, k in order(slots, with_next, False):
                    if what == "conv":
                        act.wait_ge(ycopy_done, i * NS + k + 3)
                        n = SPREAD.get(slots[k][0], N)
                        nc.scalar.activation(sq[:, k % 2, 0:n], ycp[:, k % 2, 0:n], ACT.Square).then_inc(sq_done, 1)
                    elif what == "bcast":
                        finish(i, slots, k)
                    elif what == "l0":
                        l0_tile(i + 1, k)

            act.wait_ge(load_w, 16 * N_WLOADS)
            for _ in range(2):
                nc.scalar.activation(spare(), ones_sb[:], ACT.Gelu).then_inc(gelu_done, 1)
            for r in range(RES0):
                l0_tile(0, r)
            with act.Fori(0, PAIRS - 1) as i:
                body(i, SLOTS, True)
            body(PAIRS - 1, SLOTS, False)
            body(PAIRS, TAIL, False)

            act.wait_ge(shifted, 1)
            nc.scalar.activation(rt[:, 1:3, :], rt[:, 1:3, :], ACT.Exp).then_inc(exp_done, 1)

            def hidden(t, k):
                for c, (f0, f1) in enumerate(HID_BANKS):
                    act.wait_ge(hid_ps, 2 * t + (c + 1))
                    nc.scalar.activation(hid[k][:, f0:f1, :],
                                         up_banks[k][:, c, 0:(f1 - f0) * P].rearrange("p (f n) -> p f n", f=f1 - f0),
                                         ACT.Gelu).then_inc(hid_sb, 1)
            with act.Fori(0, TILES // 2) as g:
                for k in range(2):
                    hidden(2 * g + k, k)

        @block.vector
        def _(dve):
            links = [0]

            def link(ins, base=0):
                links[0] += 1
                ins.then_inc(dve_seq, 1)
                dve.wait_ge(dve_seq, base + links[0])

            dve.wait_ge(inited, 1)
            dve.wait_ge(load_w, 16 * N_WLOADS)
            nc.vector.memset(spare(), 0.0).then_inc(att_sb, 1)
            for _ in range(2):
                nc.vector.memset(spare(), 0.0).then_inc(norm_done, 1)
                nc.vector.memset(spare(), 0.0).then_inc(ycopy_done, 1)
            link(nc.vector.tensor_reduce(wmean[:], wcv[:], AX_X, ALU.add))
            link(nc.vector.tensor_scalar(wmean[:], wmean[:], 1.0 / C, None, ALU.mult))
            nc.vector.tensor_tensor(wcv[:], wcv[:], wmean[:].unsqueeze(2).to_broadcast([P, NTAP, C]),
                                    ALU.subtract).then_inc(w_center, 1)
            dve.wait_ge(w0_ps, 1)
            link(nc.vector.tensor_copy(w0c[:], ps_a[:, 0:TAPS0].unsqueeze(1).to_broadcast([P, HALF, TAPS0])))
            nc.vector.memset(spare(), 0.0).then_inc(w0_done, 1)
            dve.wait_ge(w0_ps, 2)
            link(nc.vector.tensor_tensor(gram[:], ps_a[0:XR, 0:XR], gmask_sb[:], ALU.mult))
            link(nc.vector.tensor_copy(w0t[:], ps_a[0:XR, P:2 * P]))
            for r in range(HALF):
                last = nc.vector.tensor_scalar(w0r[:, r, :], w0t[:], rmask_sb[:, r:r + 1], None, ALU.mult)
            last.then_inc(w0_done, 1)
            LINK0 = links[0]
            ATT_LINKS = 7

            def rsqrt(i):
                n = [0]

                def then(ins):
                    n[0] += 1
                    ins.then_inc(newton, 1)
                    dve.wait_ge(newton, i * NEWTON + n[0])
                v, y, a, c, d = pv[0:BLK, :], nt[0:BLK, 0, :], nt[0:BLK, 1, :], nt[0:BLK, 2, :], nt[0:BLK, 3, :]
                then(nc.vector.tensor_scalar(v, ps_v[0:BLK, 64:128], EPS, EPS, ALU.add, ALU.max))
                then(nc.vector.tensor_scalar(y.bitcast(I32), v.bitcast(I32), -0.5, float(0x5F3759DF), ALU.mult, ALU.add))
                then(nc.vector.tensor_tensor(a, y, y, ALU.mult))
                then(nc.vector.tensor_tensor(c, a, v, ALU.mult))
                then(nc.vector.tensor_scalar(d, c, 0.375, -1.25, ALU.mult, ALU.add))
                then(nc.vector.tensor_tensor(a, d, c, ALU.mult))
                then(nc.vector.scalar_tensor_tensor(d, a, 1.875, y, ALU.add, ALU.mult))
                then(nc.vector.scalar_tensor_tensor(a, d, -0.5, d, ALU.mult, ALU.mult))
                then(nc.vector.tensor_tensor(c, a, v, ALU.mult))
                wide = [BLK, 4 * 2 * HALF, TAPS0]
                nc.vector.scalar_tensor_tensor(prx[0:BLK].rearrange("p (m k) -> p m k", k=TAPS0),
                                               c.unsqueeze(2).to_broadcast(wide), 1.5,
                                               d.unsqueeze(2).to_broadcast(wide), ALU.add, ALU.mult).then_inc(prstd_ready, 1)

            def prep(i, what):
                if what == "zmm":
                    dve.wait_ge(z_ready, i + 1)
                    nc.vector.tensor_tensor(prod, ps_l0[0:XR, :, 0:N], xin, ALU.mult).then_inc(prod_done, 1)
                elif what == "psum":
                    dve.wait_ge(psum_ready, i + 1)
                    rsqrt(i)
                elif what == "pbc":
                    dve.wait_ge(pbc_ready, i + 1)
                    nc.vector.tensor_tensor(xnorm[:], ps_l0[0:XR, :, 0:N], xin, ALU.mult).then_inc(xn_ready, 1)

            def layernorm(i, half, src, base):
                link(nc.vector.bn_stats(st[:], src), base)
                nc.vector.memset(zero1[:], 0.0)
                link(nc.vector.bn_aggr(mv[:], st[:]), base)
                nc.vector.tensor_scalar(tv[:], mv[:, 1:2], EPS, None, ALU.add).then_inc(tvar_ready, 1)
                dve.wait_ge(trstd_ready, i * 2 + half + 1)
                return nc.vector.tensor_scalar(xn[:, 0:C2], src, mv[:, 0:1], trs[:], ALU.subtract, ALU.mult)

            def attention(i, k):
                if k == 0:
                    links[0] = LINK0
                base = i * ATT_LINKS
                dve.wait_ge(att_ps, i * ATT + k + 1)
                if k == 0:
                    link(nc.vector.tensor_tensor(hb[:], ps_a[:, 0:C2], projb_sb[:], ALU.add), base)
                    layernorm(i, 0, hb[:], base)
                    last = nc.vector.tensor_tensor(hp[:], hb[:], bproj_sb[:], ALU.add)
                elif k == 1:
                    last = nc.vector.tensor_copy(xnT[:], ps_a[:, 0:2 * P].rearrange("p (a n) -> p a n", a=2))
                elif k == 2:
                    nc.vector.tensor_scalar(qT[:, 0, :], ps_a[:, 0:P], bq_sb[:, 0:1], None, ALU.add)
                    last = nc.vector.tensor_scalar(qT[0:CB, 1, :], ps_a[0:CB, P:2 * P], bq_sb[0:CB, 1:2], None, ALU.add)
                elif k == 3:
                    link(nc.vector.tensor_tensor(kv[:], ps_a[:, 0:2 * C2], bkv_sb[:], ALU.add), base)
                    for b in range(2):
                        last = nc.vector.tensor_scalar(km[:, b, :], kv[:, 0:C2], bmask_sb[:, b:b + 1], None, ALU.mult)
                elif k == 4:
                    m = ps_a[:, 0:2 * C2].rearrange("p (b n) -> p b n", b=2)
                    nc.vector.tensor_tensor(ms[:, :, 0:P], m[:, :, 0:P],
                                            amask_sb[:, 0:P].unsqueeze(1).to_broadcast([P, 2, P]), ALU.mult)
                    last = nc.vector.tensor_tensor(ms[0:CB, :, P:C2], m[0:CB, :, P:C2],
                                                   amask_sb[0:CB, P:C2].unsqueeze(1).to_broadcast([CB, 2, CB]), ALU.mult)
                elif k == 5:
                    nc.vector.tensor_copy(oT[:, 0, :], ps_a[:, 0:P])
                    last = nc.vector.tensor_copy(oT[0:CB, 1, :], ps_a[0:CB, P:2 * P])
                elif k == 6:
                    nc.vector.tensor_tensor(h2_flat[:, bass.ds(i * C2, C2)], ps_a[:, 0:C2], hp[:], ALU.add)
                    link(nc.vector.tensor_tensor(hb[:], ps_a[:, 0:C2], hp[:], ALU.add), base)
                    last = layernorm(i, 1, hb[:], base)
                elif k == 7:
                    both = ps_a[:, 0:2 * P].rearrange("p (a n) -> p a n", a=2)
                    nc.vector.tensor_copy(x2T[:], both)
                    last = nc.vector.tensor_copy(x2_flat[:, bass.ds(i * C2, C2)], xn[:, 0:C2])
                else:
                    last = nc.vector.tensor_tensor(lg_flat[:, bass.ds(i * 2 * NE, 2 * NE)],
                                                   ps_a[:, 0:2 * NE], br_sb[:], ALU.add)
                last.then_inc(att_sb, 1)

            def body(i, slots, with_next, with_att):
                for what, k in order(slots, with_next, with_att):
                    T = i * NS + k
                    n = SPREAD.get(slots[k][0], N) if what in ("conv", "colsum", "bcast") else 0
                    if what == "conv":
                        dve.wait_ge(y_ready, T + 1)
                        dve.wait_ge(norm_done, T + 1)
                        nc.vector.tensor_copy(ycp[:, k % 2, 0:n], ps_y[:, k % 2, 0:n]).then_inc(ycopy_done, 1)
                    elif what == "colsum":
                        variance(i, slots, k)
                    elif what == "bcast":
                        dve.wait_ge(bcast_ready, T + 1)
                        dve.wait_ge(gelu_done, T + 1)
                        dve.wait_ge(ycopy_done, T + 3)
                        nc.vector.tensor_tensor(nrm[:, k % 2, 0:n], ycp[:, k % 2, 0:n], ps_r[:, k % 2, 0:n],
                                                ALU.mult).then_inc(norm_done, 1)
                    elif what == "att":
                        attention(i, k)
                    elif what in ("zmm", "psum", "pbc"):
                        prep(i + 1, what)

            def variance(i, slots, k):
                bl = blocks(SPREAD.get(slots[k][0], N))
                dve.wait_ge(colsum_ready, i * NS + k + 1)
                nc.vector.tensor_scalar(vv[0:bl[0][1], k % 2, 0:len(bl)], ps_v[0:bl[0][1], 0:len(bl)], EPS, None,
                                        ALU.add).then_inc(var_ready, 1)

            dve.wait_ge(load_x, 16 * XLOADS)
            for what in ("zmm", "psum", "pbc"):
                prep(0, what)
            with dve.Fori(0, PAIRS - 1) as i:
                body(i, SLOTS, True, True)
            body(PAIRS - 1, SLOTS, False, True)
            for k in range(ATT):
                attention(PAIRS, k)
            body(PAIRS, TAIL, False, False)
            for k in range(ATT):
                attention(PAIRS + 1, k)
            assert links[0] == LINK0 + ATT_LINKS, links[0] - LINK0

            dve.wait_ge(att_sb, ATT * (PAIRS + 2) + 1)
            nc.vector.memset(spare(), 0.0).then_inc(logits_done, 1)
            steps = [0]

            def then(ins):
                steps[0] += 1
                ins.then_inc(route_seq, 1)
                dve.wait_ge(route_seq, steps[0])

            def row(r, n=1):
                return rt[:, r, 0:n * PAIRS]

            def mat(r):
                return rt[:, r, :].rearrange("p (e j) -> p e j", e=NE)

            def rep(a):
                return a.unsqueeze(1).to_broadcast([P, NE, PAIRS])

            logit = [lg[:, 2:2 + PAIRS, NE * u:NE * (u + 1)] for u in range(2)]
            for u in range(2):
                then(nc.vector.tensor_reduce(row(3 + u), logit[u], AX_X, ALU.max))
                then(nc.vector.tensor_tensor(mat(1 + u), logit[u].rearrange("p j e -> p e j"), rep(row(3 + u)), ALU.subtract))
                then(nc.vector.tensor_scalar(rt[:, 5 + u, :], rt[:, 1 + u, :], 0.0, None, ALU.is_equal))
            nc.vector.memset(spare(), 0.0).then_inc(shifted, 1)
            dve.wait_ge(exp_done, 1)
            for u in range(2):
                then(nc.vector.tensor_reduce(row(3 + u), mat(1 + u).rearrange("p e j -> p j e"), AX_X, ALU.add))
                then(nc.vector.reciprocal(row(7 + u), row(3 + u)))
                then(nc.vector.reciprocal(row(9 + u), row(7 + u)))
                then(nc.vector.tensor_tensor(row(9 + u), row(9 + u), row(7 + u), ALU.mult))
                then(nc.vector.tensor_copy(row(11), mat(5 + u)[:, 0, :]))
                for e in range(1, NE):
                    then(nc.vector.tensor_copy(row(12), mat(5 + u)[:, e, :]))
                    then(nc.vector.tensor_tensor(mat(5 + u)[:, e, :], row(12), row(11), ALU.is_gt))
                    then(nc.vector.tensor_tensor(row(11), row(11), row(12), ALU.max))
                then(nc.vector.tensor_copy(wm[:, u, :], row(9 + u)))
            for u in range(2):
                then(nc.vector.tensor_scalar(rt[:, 5 + u, :], rt[:, 5 + u, :], valid_sb[:], None, ALU.mult))

            def before():
                then(nc.vector.tensor_copy(mat(17), ps_a[:, 128:256].rearrange("p (e j) -> p e j", e=NE)))
                then(nc.vector.memset(rt[:, 18, :], 0.0))
                then(nc.vector.tensor_copy(mat(18)[:, :, 1:PAIRS], mat(17)[:, :, 0:PAIRS - 1]))
                a, b_ = 18, 19
                d = 1
                while d < PAIRS:
                    then(nc.vector.tensor_copy(rt[:, b_, :], rt[:, a, :]))
                    then(nc.vector.tensor_tensor(mat(b_)[:, :, d:PAIRS], mat(a)[:, :, d:PAIRS], mat(a)[:, :, 0:PAIRS - d], ALU.add))
                    a, b_ = b_, a
                    d *= 2
                return a

            def places(u, counted):
                base, tiles = (0, COMMON) if u == 0 else (COMMON, UNIQUE)
                nc.vector.memset(spare(), 0.0).then_inc(count_ready, 1)
                dve.wait_ge(count_sum, counted)
                a = before()
                then(nc.vector.tensor_tensor(cnt[:, 6, :], mat(a)[:, :, PAIRS - 1], mat(17)[:, :, PAIRS - 1], ALU.add))
                then(nc.vector.tensor_scalar(cnt[:, 6, :], cnt[:, 6, :], 1.0 / P, None, ALU.mult))
                then(nc.vector.tensor_tensor(ntile, cnt[:, 6, :].unsqueeze(2).to_broadcast([P, NE, PAIRS]),
                                             rep(iota_sb[:, 0:PAIRS]), ALU.is_gt))
                then(nc.vector.tensor_reduce(cnt[:, 7, :], ntile, AX_X, ALU.add))
                then(nc.vector.memset(begin[:, 0:1], 0.0))
                for e in range(1, NE):
                    then(nc.vector.tensor_tensor(begin[:, e:e + 1], begin[:, e - 1:e], cnt[:, 7, e - 1:e], ALU.add))
                for e in range(1, NE):
                    nc.vector.tensor_scalar(later[:, e, 0:tiles], iota_sb[:, 0:tiles], begin[:, e:e + 1], None, ALU.is_ge)
                then(nc.vector.memset(later[:, 0, 0:tiles], float(NE * u)))
                for e in range(1, NE):
                    then(nc.vector.tensor_tensor(later[:, 0, 0:tiles], later[:, 0, 0:tiles], later[:, e, 0:tiles], ALU.add))
                then(nc.vector.tensor_copy(expert[:, base:base + tiles], later[:, 0, 0:tiles]))
                then(nc.vector.tensor_tensor(rt[:, a, :], rt[:, a, :], ps_a[:, 256:384], ALU.add))
                then(nc.vector.tensor_scalar(begin[:], begin[:], float(P), None, ALU.mult))
                then(nc.vector.tensor_tensor(mat(a), mat(a), begin[:].unsqueeze(2).to_broadcast([P, NE, PAIRS]), ALU.add))
                then(nc.vector.tensor_tensor(rt[:, a, :], rt[:, a, :], rt[:, 16, :], ALU.mult))
                then(nc.vector.tensor_reduce(row(20), mat(a).rearrange("p e j -> p j e"), AX_X, ALU.add))
                then(nc.vector.tensor_reduce(row(22), mat(16).rearrange("p e j -> p j e"), AX_X, ALU.add))
                then(nc.vector.tensor_copy(src[:, u, :], row(20)))
                then(nc.vector.tensor_scalar(row(22), row(22), -1.0, 1.0, ALU.mult, ALU.add))
                then(nc.vector.scalar_tensor_tensor(row(23), ids_sb[:], float(TRASH[u] - base * P), row(22), ALU.add, ALU.mult))
                then(nc.vector.scalar_tensor_tensor(row(23), row(23), float(base * P), row(20), ALU.add, ALU.add))
                then(nc.vector.tensor_copy(dest[:, u, :], row(23)))
                nc.vector.memset(spare(), 0.0).then_inc(placed, 1)

            then(nc.vector.tensor_copy(rt[:, 16, :], rt[:, 5, :]))
            places(0, 1)
            then(nc.vector.tensor_tensor(mat(13), mat(5), rep(row(7)), ALU.mult))
            thr, cand, step, ge = cnt[:, 0, :], cnt[:, 1, :], cnt[:, 2, :], cnt[:, 3, :]
            then(nc.vector.memset(step, 1.0))
            then(nc.vector.memset(thr, 0.0))
            PER = 5
            seq0 = steps[0]
            with dve.Fori(0, BITS) as b:
                n = [0]

                def link_b(ins):
                    n[0] += 1
                    ins.then_inc(route_seq, 1)
                    dve.wait_ge(route_seq, b * PER + (seq0 + n[0]))
                link_b(nc.vector.tensor_tensor(cand, thr, step, ALU.add))
                link_b(nc.vector.tensor_tensor(mat(14), mat(13), cand.unsqueeze(2).to_broadcast([P, NE, PAIRS]), ALU.is_ge))
                nc.vector.tensor_reduce(cnt[:, 4, :], mat(14), AX_X, ALU.add).then_inc(count_ready, 1)
                dve.wait_ge(count_sum, b + 2)
                link_b(nc.vector.scalar_tensor_tensor(ge, ps_a[:, 0:NE], float(CAP), step, ALU.is_ge, ALU.mult))
                link_b(nc.vector.tensor_tensor(thr, thr, ge, ALU.add))
                link_b(nc.vector.tensor_scalar(step, step, 0.5, None, ALU.mult))
            steps[0] += BITS * PER
            tb = thr.unsqueeze(2).to_broadcast([P, NE, PAIRS])
            then(nc.vector.tensor_tensor(mat(15), mat(13), tb, ALU.is_gt))
            then(nc.vector.tensor_tensor(mat(16), mat(13), tb, ALU.is_equal))
            then(nc.vector.tensor_tensor(mat(16), mat(16), mat(5), ALU.mult))
            nc.vector.tensor_reduce(cnt[:, 4, :], mat(15), AX_X, ALU.add).then_inc(count_ready, 1)
            dve.wait_ge(count_sum, BITS + 2)
            then(nc.vector.tensor_scalar(cnt[:, 5, :], ps_a[:, 0:NE], -1.0, float(CAP), ALU.mult, ALU.add))
            a = before()
            then(nc.vector.tensor_tensor(rt[:, a, :], rt[:, a, :], ps_a[:, 256:384], ALU.add))
            then(nc.vector.tensor_tensor(mat(20), mat(a), cnt[:, 5, :].unsqueeze(2).to_broadcast([P, NE, PAIRS]), ALU.is_lt))
            then(nc.vector.tensor_tensor(rt[:, 20, :], rt[:, 20, :], rt[:, 16, :], ALU.mult))
            then(nc.vector.tensor_tensor(rt[:, 15, :], rt[:, 15, :], rt[:, 20, :], ALU.add))
            then(nc.vector.tensor_reduce(row(21), mat(15).rearrange("p e j -> p j e"), AX_X, ALU.add))
            then(nc.vector.tensor_scalar(row(21), row(21), -1.0, 1.0, ALU.mult, ALU.add))
            then(nc.vector.tensor_tensor(wm[:, 1, :], wm[:, 1, :], row(21), ALU.mult))
            then(nc.vector.tensor_tensor(mat(16), mat(6), rep(row(21)), ALU.mult))
            places(1, BITS + 3)

            dve.wait_ge(small_load, 16)
            dve.wait_ge(w_load, 16 * 4 * 2 * NE)
            for k in range(2):
                nc.vector.memset(xt_ch[k][CB:CB + 1, 1, :], 1.0)
                nc.vector.memset(spare(), 0.0).then_inc(y_sb, 1)
                nc.vector.memset(spare(), 0.0).then_inc(y_store[k], 16)
            nc.vector.memset(spare(), 0.0).then_inc(xt_sb, 1)
            b2_flat = b2_sb[:].rearrange("p e n -> p (e n)")
            def first_weights(t, k, free=True):
                e = dve.value_load(expert[0:1, bass.ds(t, 1)], min_val=0, max_val=2 * NE - 1)
                if free:
                    dve.wait_ge(hid_ps, 2 * t - 2)
                nc.vector.tensor_copy(w1_cur[k][:, 0, :], w1_all[:, bass.ds(e * (2 * FF), FF)])
                nc.vector.tensor_copy(w1_cur[k][0:CB + 1, 1, :],
                                      w1_all[0:CB + 1, bass.ds(e * (2 * FF) + FF, FF)]).then_inc(w1_ready, 1)

            def channel_major(t, k):
                dve.wait_ge(xt_ps, t + 1)
                nc.vector.tensor_copy(xt_ch[k][:, 0, :], ps_v[:, 0:P])
                nc.vector.tensor_copy(xt_ch[k][0:CB, 1, :], ps_v[0:CB, P:2 * P]).then_inc(xt_sb, 1)

            def expert_rows(t, k, turn):
                e = dve.value_load(expert[0:1, bass.ds(t, 1)], min_val=0, max_val=2 * NE - 1)
                dve.wait_ge(down_ps, t + 1)
                dve.wait_ge(y_store[k], 16 * turn + 16)
                nc.vector.tensor_tensor(y_tok[k], out_banks[k][:, 0:C2], b2_flat[:, bass.ds(e * C2, C2)],
                                        ALU.add).then_inc(y_sb, 1)

            first_weights(0, 0, False)
            channel_major(0, 0)
            first_weights(1, 1, False)
            channel_major(1, 1)
            first_weights(2, 0)
            channel_major(2, 0)
            expert_rows(0, 0, 0)
            with dve.Fori(0, TILES // 2 - 2) as g:
                first_weights(2 * g + 3, 1)
                channel_major(2 * g + 3, 1)
                expert_rows(2 * g + 1, 1, g)
                first_weights(2 * g + 4, 0)
                channel_major(2 * g + 4, 0)
                expert_rows(2 * g + 2, 0, g + 1)
            first_weights(TILES - 1, 1)
            channel_major(TILES - 1, 1)
            expert_rows(TILES - 3, 1, TILES // 2 - 2)
            expert_rows(TILES - 2, 0, TILES // 2 - 1)
            expert_rows(TILES - 1, 1, TILES // 2 - 1)

            wm_flat = wm[:].rearrange("p u j -> p (u j)")
            dve.wait_ge(gathered_c, 16 * PAIRS)
            with dve.Fori(0, PAIRS) as j:
                hrow = h2_flat[:, bass.ds((j + 2) * C2, C2)]
                nc.vector.scalar_tensor_tensor(hrow, x2_flat[:, bass.ds((j + 2) * C2, C2)], wm_flat[:, bass.ds(j, 1)],
                                               hrow, ALU.mult, ALU.add).then_inc(mixed_c, 1)
            dve.wait_ge(mixed_c, PAIRS)
            yu_flat = yu.rearrange("p j n -> p (j n)")
            for q in range(4):
                dve.wait_ge(gathered_u[q], 16 * 8)
                with dve.Fori(0, 8) as j:
                    hrow = h2_flat[:, bass.ds((j + (8 * q + 2)) * C2, C2)]
                    nc.vector.scalar_tensor_tensor(hrow, yu_flat[:, bass.ds((j + 8 * q) * C2, C2)],
                                                   wm_flat[:, bass.ds(j + (PAIRS + 8 * q), 1)],
                                                   hrow, ALU.mult, ALU.add).then_inc(mixed_u, 1)

        @block.tensor
        def _(pe):
            mm = nc.tensor.matmul
            pe.wait_ge(load_w, 16 * N_WLOADS)
            last = mm(ps_a[:, 0:TAPS0], center_sb[:], w0_sb[:], start=True, stop=True)
            last.then_inc(w0_ps, 1)
            pe.wait_ge(w0_done, 1)
            w0flat = w0c[:].rearrange("p r k -> p (r k)")
            mm(ps_a[0:XR, 0:XR], w0flat, w0flat, start=True, stop=True)
            mm(ps_a[0:XR, P:2 * P], w0flat, id_sb[:], start=True, stop=True).then_inc(w0_ps, 1)
            pe.wait_ge(w0_done, 2)
            pe.wait_ge(w_center, 1)
            pe.wait_ge(inited, 1)

            def prep(i, what):
                if what == "zmm":
                    pe.wait_ge(load_x, (i + 1) * (16 * XLOADS))
                    pe.wait_ge(l0_gelu, i * RES0)
                    for h in range(2):
                        last = mm(ps_l0[0:XR, h, 0:N], gram[:], xin[:, h, :], start=True, stop=True)
                    last.then_inc(z_ready, 1)
                elif what == "psum":
                    pe.wait_ge(prod_done, i + 1)
                    for j in range(4):
                        for h in range(2):
                            c0 = 64 + (j * 2 + h) * HALF
                            last = mm(ps_v[0:BLK, c0:c0 + HALF], prod[:, h, j * BLK:(j + 1) * BLK], rmask_sb[:],
                                      start=True, stop=True)
                    last.then_inc(psum_ready, 1)
                elif what == "pbc":
                    pe.wait_ge(prstd_ready, i + 1)
                    for h in range(2):
                        for j in range(4):
                            last = mm(ps_l0[0:XR, h, j * BLK:(j + 1) * BLK], prx[0:BLK, (2 * j + h) * XR:(2 * j + h + 1) * XR], id_sb[0:BLK, 0:BLK], start=True, stop=True)
                    last.then_inc(pbc_ready, 1)

            def l0_tile(i, r):
                if r < 2:
                    pe.wait_ge(xn_ready, i + 1)
                else:
                    pe.wait_ge(l0_gelu, i * RES0 + r - 1)
                mm(ps_l0[:, r % 2, 0:N], w0r[:, r % HALF, :], xnorm[:, r // HALF, :], start=True, stop=True).then_inc(l0_ready, 1)

            def need(i, slots, s):
                layer, t = slots[s]
                at = {x: k for k, x in enumerate(slots)}
                if layer == 1:
                    pe.wait_ge(l0_gelu, i * RES0 + min(2 * t + 3, RES0))
                elif layer in (2, 3):
                    half = 4 if layer == 2 else 2
                    reads = [(layer - 1, (2 * t + k) % (2 * half)) for k in range(3)]
                    pe.wait_ge(gelu_done, i * NS + max(at[x] for x in reads) + 3)
                elif layer == 4:
                    pe.wait_ge(gelu_done, i * NS + 2)
                else:
                    pe.wait_ge(gelu_done, i * NS + at[(layer - 1, 0)] + 3)

            def taps(layer, t):
                if layer in (1, 2, 3):
                    src = {1: act0, 2: act1, 3: act2}[layer]
                    R = {1: 16, 2: 8, 3: 4}[layer]
                    return [src[:, (2 * t + k) % R, :, (2 * t + k) // R:(2 * t + k) // R + Q] for k in range(3)]
                if layer == 4:
                    return [act3[:, k % 2, :, k // 2:k // 2 + Q] for k in range(3)]
                if layer == 5:
                    return [act4[:, :, k:k + 2 * T5 - 1:2] for k in range(2)]
                if layer == 6:
                    return [act5[:, :, k:k + 2 * T6 - 1:2] for k in range(2)]
                return [act6.rearrange("p (b q) -> p b q", b=2)]

            def conv(i, slots, s, part):
                layer, t = slots[s]
                n = SPREAD.get(layer, N)
                rows = taps(layer, t)
                first = max(0, len(rows) - 2) if part == 1 else len(rows) - 1 if part == 2 else 0
                last_tap = {0: len(rows) - 2, 1: len(rows) - 1, 2: len(rows)}[part]
                if first == 0:
                    need(i, slots, s)
                    pe.wait_ge(ycopy_done, i * NS + s + 1)
                for k in range(first, last_tap):
                    last = mm(ps_y[:, s % 2, 0:n].rearrange("p (b q) -> p b q", b=2), wcv[:, TAP0[layer] + k, :], rows[k],
                              start=(k == 0), stop=(k == len(rows) - 1))
                if part == 2:
                    last.then_inc(y_ready, 1)

            def colsum(i, slots, s):
                pe.wait_ge(sq_done, i * NS + s + 1)
                bl = blocks(SPREAD.get(slots[s][0], N))
                for j, (c0, w) in enumerate(bl):
                    last = mm(ps_v[0:w, j:j + 1], sq[:, s % 2, c0:c0 + w], ones_sb[:], start=True, stop=True)
                last.then_inc(colsum_ready, 1)

            def bcast(i, slots, s):
                pe.wait_ge(rstd_ready, i * NS + s + 1)
                pe.wait_ge(norm_done, i * NS + s + 1)
                bl = blocks(SPREAD.get(slots[s][0], N))
                for j, (c0, w) in enumerate(bl):
                    last = mm(ps_r[:, s % 2, c0:c0 + w], rs[0:w, s % 2, j:j + 1].to_broadcast([w, P]), id_sb[0:w, 0:w],
                              start=True, stop=True)
                last.then_inc(bcast_ready, 1)

            def attention(i, k, before=None):
                pe.wait_ge(att_sb, i * ATT + k + 1)
                if k == 0:
                    pe.wait_ge(gelu_done, (i * NS if before is None else before) + 2)
                    last = mm(ps_a[:, 0:C2], nout[:].rearrange("p b q -> p (b q)"), projw_sb[:], start=True, stop=True)
                elif k in (1, 7):
                    for c in range(2):
                        last = nc.tensor.transpose(ps_a[:, c * P:(c + 1) * P], xn[:, c * P:(c + 1) * P], id_sb[:])
                elif k == 2:
                    for c, w in ((0, P), (1, CB)):
                        mm(ps_a[0:w, c * P:(c + 1) * P], wqkv_sb[:, 0, c * P:c * P + w], xnT[:, 0, :], start=True, stop=False)
                        last = mm(ps_a[0:w, c * P:(c + 1) * P], wqkv_sb[0:CB, 1, c * P:c * P + w], xnT[0:CB, 1, :],
                                  start=False, stop=True)
                elif k == 3:
                    mm(ps_a[:, 0:2 * C2], xnT[:, 0, :], wqkv_sb[:, 0, C2:3 * C2], start=True, stop=False)
                    last = mm(ps_a[:, 0:2 * C2], xnT[0:CB, 1, :], wqkv_sb[0:CB, 1, C2:3 * C2], start=False, stop=True)
                elif k == 4:
                    for b in range(2):
                        mm(ps_a[:, b * C2:b * C2 + P], km[:, b, 0:P], kv[:, C2:C2 + P], start=True, stop=True)
                        last = mm(ps_a[0:CB, b * C2 + P:(b + 1) * C2], km[:, b, P:C2], kv[:, C2 + P:2 * C2],
                                  start=True, stop=True)
                elif k == 5:
                    for b in range(2):
                        cols = slice(PAD6 * b, PAD6 * (b + 1))
                        mm(ps_a[:, cols], ms[:, b, 0:P], qT[:, 0, cols], start=True, stop=True)
                        last = mm(ps_a[0:CB, P + PAD6 * b:P + PAD6 * (b + 1)], ms[0:CB, b, P:C2], qT[0:CB, 1, cols],
                                  start=True, stop=True)
                elif k == 6:
                    mm(ps_a[:, 0:C2], oT[:, 0, :], wproj_sb[:, 0, :], start=True, stop=False)
                    last = mm(ps_a[:, 0:C2], oT[0:CB, 1, :], wproj_sb[0:CB, 1, :], start=False, stop=True)
                else:
                    mm(ps_a[:, 0:2 * NE], x2T[:, 0, :], wr_sb[:, 0, :], start=True, stop=False)
                    last = mm(ps_a[:, 0:2 * NE], x2T[0:CB, 1, :], wr_sb[0:CB, 1, :], start=False, stop=True)
                last.then_inc(att_ps, 1)

            def body(i, slots, with_next, with_att):
                for what, k in order(slots, with_next, with_att):
                    if what in ("tap0", "tap1", "conv"):
                        conv(i, slots, k, ("tap0", "tap1", "conv").index(what))
                    elif what == "colsum":
                        colsum(i, slots, k)
                    elif what == "bcast":
                        bcast(i, slots, k)
                    elif what == "att":
                        attention(i, k)
                    elif what == "l0":
                        l0_tile(i + 1, k)
                    elif what == "psum":
                        pe.wait_ge(var_ready, i * NS + k)
                        prep(i + 1, what)
                        pe.wait_ge(newton, (i + 1) * NEWTON + 1)
                    else:
                        prep(i + 1, what)

            for what in ("zmm", "psum", "pbc"):
                prep(0, what)
            for r in range(RES0):
                l0_tile(0, r)
            with pe.Fori(0, PAIRS - 1) as i:
                body(i, SLOTS, True, True)
            body(PAIRS - 1, SLOTS, False, True)
            for k in range(ATT):
                attention(PAIRS, k)
            body(PAIRS, TAIL, False, False)
            for k in range(ATT):
                attention(PAIRS + 1, k, before=PAIRS * NS + len(TAIL))

            def places(n):
                pe.wait_ge(count_ready, n)
                mm(ps_a[:, 128:256], ones_pp[:], rt[:, 16, :], start=True, stop=True)
                mm(ps_a[:, 256:384], tri_sb[:], rt[:, 16, :], start=True, stop=True).then_inc(count_sum, 1)
            places(1)
            with pe.Fori(0, BITS) as b:
                pe.wait_ge(count_ready, b + 2)
                mm(ps_a[:, 0:NE], ones_pp[:], cnt[:, 4, :], start=True, stop=True).then_inc(count_sum, 1)
            pe.wait_ge(count_ready, BITS + 2)
            mm(ps_a[:, 0:NE], ones_pp[:], cnt[:, 4, :], start=True, stop=True)
            mm(ps_a[:, 128:256], ones_pp[:], rt[:, 16, :], start=True, stop=True)
            mm(ps_a[:, 256:384], tri_sb[:], rt[:, 16, :], start=True, stop=True).then_inc(count_sum, 1)

            places(BITS + 3)

            pe.wait_ge(placed, 2)

            def transpose(t, k, turn):
                pe.wait_ge(x_load[k], 16 * turn + 16)
                pe.wait_ge(xt_sb, t + 1)
                nc.tensor.transpose(ps_v[:, 0:P], xt_tok[k][:, 0:P], id_sb[:])
                nc.tensor.transpose(ps_v[0:CB, P:2 * P], xt_tok[k][:, P:C2], id_sb[:]).then_inc(xt_ps, 1)

            def up(t, k):
                pe.wait_ge(xt_sb, t + 2)
                pe.wait_ge(w1_ready, t + 1)
                for c, (f0, f1) in enumerate(HID_BANKS):
                    for f in range(f0, f1):
                        at_f = up_banks[k][:, c, (f - f0) * P:(f - f0 + 1) * P]
                        mm(at_f, w1_cur[k][:, 0, f * P:(f + 1) * P], xt_ch[k][:, 0, :], start=True, stop=False)
                        last = mm(at_f, w1_cur[k][0:CB + 1, 1, f * P:(f + 1) * P], xt_ch[k][0:CB + 1, 1, :],
                                  start=False, stop=True)
                    last.then_inc(hid_ps, 1)

            def down(t, k):
                e = pe.value_load(expert[0:1, bass.ds(t, 1)], min_val=0, max_val=2 * NE - 1)
                pe.wait_ge(hid_sb, 2 * t + 2)
                pe.wait_ge(y_sb, t + 1)
                for f in range(FC):
                    last = mm(out_banks[k][:, 0:C2], hid[k][:, f, :], w2_all[:, bass.ds(e * (FC * C2) + f * C2, C2)],
                              start=(f == 0), stop=(f == FC - 1))
                last.then_inc(down_ps, 1)

            transpose(0, 0, 0)
            up(0, 0)
            transpose(1, 1, 0)
            up(1, 1)
            transpose(2, 0, 1)
            down(0, 0)
            with pe.Fori(0, TILES // 2 - 2) as g:
                up(2 * g + 2, 0)
                transpose(2 * g + 3, 1, g + 1)
                down(2 * g + 1, 1)
                up(2 * g + 3, 1)
                transpose(2 * g + 4, 0, g + 2)
                down(2 * g + 2, 0)
            up(TILES - 2, 0)
            transpose(TILES - 1, 1, TILES // 2 - 1)
            down(TILES - 3, 1)
            up(TILES - 1, 1)
            down(TILES - 2, 0)
            down(TILES - 1, 1)


_OUT = (B, T6, C2)


def _constants():
    f = np.float32
    p = np.arange(P)
    ident = np.eye(P, dtype=f)
    rows = np.arange(XR) // TAPS0
    amask = np.zeros((P, C2), f)
    amask[:, 0:P] = (p[:, None] // HEAD == p[None, :] // HEAD) * HEAD ** -0.5
    amask[0:CB, P:] = amask[0:CB, 0:CB]
    return {
        "ident": ident,
        "center": (ident - f(1.0 / P)).astype(f),
        "ones": np.ones((P, P), f),
        "onesc": np.full((P, 1), 1.0 / P, f),
        "gmask": ((rows[:, None] == rows[None, :]) / P).astype(f),
        "rmask": (rows[:, None] == np.arange(HALF)[None, :]).astype(f),
        "amask": amask,
        "valid": (p % PAD6 < T6).astype(f)[:, None].copy(),
        "bmask": ((p[:, None] // PAD6 == np.arange(2)[None, :]) & (p[:, None] % PAD6 < T6)).astype(f),
        "tri": (p[:, None] < p[None, :]).astype(f),
        "iota": np.tile(np.arange(PAIRS + 2, dtype=f), (P, 1)),
        "ids": (np.arange(PAIRS)[None, :] * P + p[:, None]).astype(f),
    }


def kernel(**inputs):
    import concourse.bacc as bacc
    from concourse.bass_utils import run_bass_kernel_spmd

    a = {k: np.asarray(v) for k, v in inputs.items()}
    tok, att, ffn = "L0_tok_", "L0_attn_", "L0_ffn_"
    arrays = {
        "xt": a["x"].reshape(B, Q, SPAN).transpose(2, 0, 1).reshape(SPAN, B * Q),
        "w0": a[tok + "conv_w0"][:, 0, :],
        "wc": np.concatenate([a[f"{tok}conv_w{i}"].transpose(1, 2, 0) for i in range(1, 7)], axis=1),
        "aff": np.stack([np.stack([a[f"{tok}ln_{c}{i}"] for i in range(7)] + [a[f"{tok}fln_{c}"]], axis=1)
                         for c in "gb"], axis=1),
        "projw": a[tok + "proj_w"], "projb": a[tok + "proj_b"],
        "wqkv": a[att + "w_qkv"], "bq": a[att + "b_qkv"][0:C2].reshape(C2, 1), "bkv": a[att + "b_qkv"][C2:],
        "wproj": a[att + "w_proj"], "bproj": a[att + "b_proj"],
        "wr": np.concatenate([a[ffn + "Wsc"], a[ffn + "Wsu"]], axis=1),
        "br": np.concatenate([a[ffn + "bsc"], a[ffn + "bsu"]]),
        "w1": np.concatenate([a[ffn + "W1c"], a[ffn + "W1u"]]).reshape(2 * NE * C2, FF),
        "b1": np.concatenate([a[ffn + "b1c"], a[ffn + "b1u"]]).reshape(2 * NE, FF),
        "w2": np.concatenate([a[ffn + "W2c"], a[ffn + "W2u"]]).reshape(2 * NE * FF, C2),
        "b2": np.concatenate([a[ffn + "b2c"], a[ffn + "b2u"]]).reshape(-1),
        **_constants(),
    }
    arrays = {f"in_{k}": np.ascontiguousarray(v) for k, v in arrays.items()}
    nc = bacc.Bacc("TRN2", target_bir_lowering=False, num_devices=1)
    args = [nc.dram_tensor(k, v.shape, mybir.dt.from_np(v.dtype), kind="ExternalInput").ap() for k, v in arrays.items()]
    out = nc.dram_tensor("out_dram", _OUT, F32, kind="ExternalOutput").ap()
    xs_dram = nc.dram_tensor("xs_dram", (ROWS + 2 * PAIRS * P, C2), F32).ap()
    yc_dram = nc.dram_tensor("yc_dram", (COMMON * P, C2), F32).ap()
    yu_dram = nc.dram_tensor("yu_dram", (UNIQUE * P, C2), F32).ap()
    audio_tower(nc, *args, xs_dram, yc_dram, yu_dram, out.rearrange("(j b) t n -> j b t n", b=2))
    r = run_bass_kernel_spmd(nc, [arrays], core_ids=[0])
    return r.results[0]["out_dram"]
```

```python
from contextlib import ExitStack

import numpy as np

import concourse.bass as bass
from concourse import mybir

ALU = mybir.AluOpType
ACT = mybir.ActivationFunctionType
F32 = mybir.dt.float32
I32 = mybir.dt.int32
U32 = mybir.dt.uint32
BF16 = mybir.dt.bfloat16
AX_X = mybir.AxisListType.X

P = 128
B, SAMPLES = 64, 20000
STRIDE0, TAPS0 = 5, 10
RES0 = 16
Q = SAMPLES // (STRIDE0 * RES0)
SPAN = STRIDE0 * RES0
HALF = RES0 // 2
XR = HALF * TAPS0
PAIRS = B // 2
N = 2 * Q
BLK = Q // 2
QUAD = 32
T5, T6 = 124, 62
PAD6 = 64
C, C2 = 128, 192
CB = C2 - P
HEAD = 16
EPS = 1e-5
NE, FF = 4, 768
FC = FF // P
CAP = B * T6 // NE
TAP0 = {1: 0, 2: 3, 3: 6, 4: 9, 5: 12, 6: 14, 7: 16}
NTAP = 17

TOKENS = B * T6
COMMON = (TOKENS + NE * (P - 1)) // P
UNIQUE = (TOKENS - CAP + NE * (P - 1)) // P
UNIQUE += (COMMON + UNIQUE) % 2
TILES = COMMON + UNIQUE
ROWS = TILES * P
TRASH = [ROWS, ROWS + PAIRS * P]

SLOTS = [(1, 0), (3, 0), (3, 1), (1, 1), (1, 3), (1, 2), (4, 0), (1, 5), (1, 4), (1, 6), (5, 0), (1, 7), (2, 0),
         (2, 1), (6, 0), (2, 2), (2, 3), (7, 0)]
TAIL = [(3, 0), (3, 1), (4, 0), (5, 0), (6, 0), (7, 0)]
NS = len(SLOTS)
SPREAD = {4: N, 5: 2 * T5, 6: 2 * T6, 7: 2 * T6}
LAG = 3
EXTRA = {0: "< z c", 1: "pc", 2: "", 3: "a0", 4: "pb a1", 5: "a2 l l", 6: "a3", 7: "l", 8: "", 9: "l l",
         10: "l a4", 11: "a5", 12: "", 13: "< l l c a6 l l", 14: "< l l c", 15: "", 16: "l l a7",
         17: "< l l a8 c"}
ATT = 9


def residue(k):
    return (k + 2) % RES0


def order(slots, first, last, with_next, with_att):
    n, l0 = len(slots), 0
    out = []
    if n < NS:
        for s in range(n):
            out += [("tap0", s), ("tap1", s), ("conv", s)]
            out += [("att", 2 * s)] if 2 * s < ATT else []
            out.append(("colsum", s))
            out += [("att", 2 * s + 1)] if 2 * s + 1 < ATT else []
            out += [("split", s), ("bcast", s)]
        return out
    for s in range(n):
        out.append(("tap0", s))
        out.append(("tap1", s))
        if s >= LAG or not first:
            out.append(("bcast", s - LAG))
        if s >= 1 or not first:
            out.append(("colsum", s - 1))
        if not EXTRA[s].startswith("< "):
            out.append(("conv", s))
        for word in EXTRA[s].split():
            if word == "<":
                continue
            if word == "c":
                out.append(("conv", s))
            elif word[0] == "a":
                if with_att:
                    out.append(("att", int(word[1:])))
            elif with_next:
                if word == "l":
                    out.append(("l0", l0))
                    l0 += 1
                else:
                    out.append(({"z": "zmm", "pc": "psum", "pb": "pbc"}[word], s))
    if last:
        out += [("bcast", n - 3), ("colsum", n - 1), ("bcast", n - 2), ("split", n - 1), ("bcast", n - 1)]
    assert l0 in (0, RES0)
    return out


def audio_tower(nc, xt, w0, wc, aff, projw, projb, wqkv, bq, bkv, wproj, bproj, wr, br, w1, b1, w2, b2,
                ident, center, ones, onesc, gmask, rmask, amask, valid, bmask, tri, iota, ids, select, partm,
                xs_dram, yc_dram, yu_dram, out):
    with ExitStack() as ctx:
        def sb(name, shape, dt=F32):
            return ctx.enter_context(nc.sbuf_tensor(name, shape, dt))

        def psum(name, shape):
            return ctx.enter_context(nc.psum_tensor(name, shape, F32))

        def sem(name):
            return ctx.enter_context(nc.semaphore(name))

        ps_l0 = psum("ps_l0", [P, 2, 512])
        ps_y = psum("ps_y", [P, 2, 512])
        ps_r = psum("ps_r", [P, 2, 512])
        ps_v = psum("ps_v", [P, 512])
        ps_a = psum("ps_a", [P, 512])
        up_banks = [ps_l0, ps_y]
        out_banks = [ps_r[:, 0, :], ps_r[:, 1, :]]

        id_sb = sb("id_sb", [P, P])
        ones_sb = sb("ones_sb", [P, QUAD])
        select_sb = sb("select_sb", [P, 4, P], BF16)
        partm_sb = sb("partm_sb", [P, 2])
        gmask_sb = sb("gmask_sb", [XR, XR])
        rmask_sb = sb("rmask_sb", [XR, HALF])
        ones_pp = sb("ones_pp", [P, P])
        amask_sb = sb("amask_sb", [P, C2])
        valid_sb = sb("valid_sb", [P, 1])
        bmask_sb = sb("bmask_sb", [P, 2])
        tri_sb = sb("tri_sb", [P, P])
        wmean = sb("wmean", [P, NTAP])
        w0_sb = sb("w0_sb", [P, TAPS0])
        gram = sb("gram", [XR, XR])
        aff_sb = sb("aff_sb", [P, 2, 8])
        bq_sb = sb("bq_sb", [P, 2])
        wr_sb = sb("wr_sb", [P, 2, 2 * NE])
        br_sb = sb("br_sb", [P, 2 * NE])
        mhalf = sb("mhalf", [P, 4])

        QP = Q + 1
        sizes = [RES0 * 2 * QP, 8 * 2 * QP, 4 * 2 * QP, 2 * 2 * QP, 2 * Q, 2 * T5, 2 * T6]
        views = {"wcv": (P, NTAP, C), "center_sb": (P, P), "w0c": (P, HALF, TAPS0), "w0t": (XR, P),
                 "w0r": (XR, HALF, P), "projw_sb": (P, C2), "projb_sb": (P, C2), "wqkv_sb": (P, 2, 3 * C2),
                 "bkv_sb": (P, 2 * C2), "wproj_sb": (P, 2, C2), "bproj_sb": (P, C2), "xnorm": (XR, 2, N),
                 "vv": (P, 2, BLK), "y0": (P, 2, BLK), "na": (P, BLK), "nb": (P, BLK), "c2": (P, 2, BLK), "d2": (P, 2, BLK),
                 "rstd": (P, BLK), "rest": (P, BLK), "select_f": (P, 4, P), "prx": (P, 4 * 2 * XR),
                 "nt": (P, 4, 4 * 2 * HALF), "hb": (P, C2), "hp": (P, C2), "xn": (P, 2 * P),
                 "xnT": (P, 2, P), "qT": (P, 2, P), "kv": (P, 2 * C2), "km": (P, 2, C2), "ms": (P, 2, C2),
                 "oT": (P, 2, P), "x2T": (P, 2, P)}
        size_of = {name: int(np.prod(shape[1:])) for name, shape in views.items()}
        pool = sb("pool", [P, sum(sizes) + 11 * N + sum(size_of.values())])
        at = np.cumsum([0] + sizes)
        act0 = pool[:, 0:at[1]].rearrange("p (r b q) -> p r b q", r=RES0, b=2)
        act1 = pool[:, at[1]:at[2]].rearrange("p (r b q) -> p r b q", r=8, b=2)
        act2 = pool[:, at[2]:at[3]].rearrange("p (r b q) -> p r b q", r=4, b=2)
        act3 = pool[:, at[3]:at[4]].rearrange("p (r b q) -> p r b q", r=2, b=2)
        act4 = pool[:, at[4]:at[5]].rearrange("p (b q) -> p b q", b=2)
        act5 = pool[:, at[5]:at[6]].rearrange("p (b q) -> p b q", b=2)
        act6 = pool[:, at[6]:at[7]]
        work = pool[:, at[7]:at[7] + 11 * N]
        starts = dict(zip(size_of, np.cumsum([at[7] + 11 * N] + list(size_of.values()))))

        def view(name):
            a = pool[0:views[name][0], starts[name]:starts[name] + size_of[name]]
            if len(views[name]) == 3:
                a = a.rearrange("p (a n) -> p a n", a=views[name][1])
            return a
        wcv, center_sb, w0c, w0t, w0r = view("wcv"), view("center_sb"), view("w0c"), view("w0t"), view("w0r")
        projw_sb, projb_sb, wqkv_sb, bkv_sb = view("projw_sb"), view("projb_sb"), view("wqkv_sb"), view("bkv_sb")
        wproj_sb, bproj_sb, xnorm, prx, nt = view("wproj_sb"), view("bproj_sb"), view("xnorm"), view("prx"), view("nt")
        vv, y0, na, nb, c2, d2 = view("vv"), view("y0"), view("na"), view("nb"), view("c2"), view("d2")
        rstd, rest, select_f = view("rstd"), view("rest"), view("select_f")
        hb, hp, xn, xnT, qT, kv = view("hb"), view("hp"), view("xn"), view("xnT"), view("qT"), view("kv")
        km, ms, oT, x2T = view("km"), view("ms"), view("oT"), view("x2T")
        sq = work[:, 0:2 * N].rearrange("p (a n) -> p a n", a=2)
        ycp = work[:, 8 * N:11 * N].rearrange("p (a n) -> p a n", a=LAG)
        nrm = work[:, 2 * N:4 * N].rearrange("p (a n) -> p a n", a=2)
        xin = work[0:XR, 4 * N:6 * N].rearrange("p (a n) -> p a n", a=2)
        prod = work[0:XR, 6 * N:8 * N].rearrange("p (a n) -> p a n", a=2)
        high = sb("high", [P, BLK], BF16)
        second = sb("second", [P, BLK], BF16)
        parts = sb("parts", [P, 2, BLK], BF16)
        nout = sb("nout", [P, 2, PAD6])
        pv = sb("pv", [P, 4 * 2 * HALF])

        st = sb("st", [P, 6])
        mv = sb("mv", [P, 2])
        zero1 = sb("zero1", [P, 1])
        credit = sb("credit", [P, 32])
        credits = iter(range(32))

        def spare():
            c = next(credits)
            return credit[:, c:c + 1]
        tv = sb("tv", [P, 1])
        trs = sb("trs", [P, 1])
        NT = PAIRS + 2
        h2 = sb("h2", [P, NT, C2])
        x2 = sb("x2", [P, NT, C2])
        lg = sb("lg", [P, NT, 2 * NE])
        x2_flat = x2[:].rearrange("p j n -> p (j n)")
        h2_flat = h2[:].rearrange("p j n -> p (j n)")
        lg_flat = lg[:].rearrange("p j n -> p (j n)")

        load_w = sem("load_w")
        load_x = sem("load_x")
        inited = sem("inited")
        xin_inited = sem("xin_inited")
        w_center = sem("w_center")
        w0_ps = sem("w0_ps")
        w0_done = sem("w0_done")
        y_ready = sem("y_ready")
        sq_done = sem("sq_done")
        ycopy_done = sem("ycopy_done")
        colsum_ready = sem("colsum_ready")
        var_ready = sem("var_ready")
        steps_v = sem("steps_v")
        split_seq = sem("split_seq")
        rstd_ready = sem("rstd_ready")
        bcast_ready = sem("bcast_ready")
        norm_done = sem("norm_done")
        gelu_done = sem("gelu_done")
        z_ready = sem("z_ready")
        prod_done = sem("prod_done")
        psum_ready = sem("psum_ready")
        newton = sem("newton")
        prstd_ready = sem("prstd_ready")
        pbc_ready = sem("pbc_ready")
        xn_ready = sem("xn_ready")
        l0_ready = sem("l0_ready")
        l0_gelu = sem("l0_gelu")
        att_ps = sem("att_ps")
        att_sb = sem("att_sb")
        tvar_ready = sem("tvar_ready")
        trstd_ready = sem("trstd_ready")
        dve_seq = sem("dve_seq")
        logits_done = sem("logits_done")
        route_seq = sem("route_seq")
        shifted = sem("shifted")
        exp_done = sem("exp_done")
        count_ready = sem("count_ready")
        count_sum = sem("count_sum")
        placed = sem("placed")
        cleared = sem("cleared")
        w_load = sem("w_load")
        scattered = [sem("scattered_c"), sem("scattered_u")]
        gathered_c = sem("gathered_c")
        gathered_u = [sem(f"gathered_u{q}") for q in range(4)]
        x_load = [sem("x_load0"), sem("x_load1")]
        xt_ps = sem("xt_ps")
        xt_sb = sem("xt_sb")
        w1_ready = sem("w1_ready")
        hid_ps = sem("hid_ps")
        hid_sb = sem("hid_sb")
        down_ps = sem("down_ps")
        y_sb = sem("y_sb")
        y_store = [sem("y_store0"), sem("y_store1")]
        mixed_c = sem("mixed_c")
        mixed_u = sem("mixed_u")
        small_load = sem("small_load")
        stored = sem("stored")

        block = ctx.enter_context(nc.Block())

        o = 0

        def take(n):
            nonlocal o
            o += n
            return pool[:, o - n:o]
        w1_all = take(2 * NE * 2 * FF)
        w2_all = take(2 * NE * FC * C2)
        w1_cur = [take(2 * FF).rearrange("p (c f) -> p c f", c=2) for _ in range(2)]
        hid = [take(FF).rearrange("p (f n) -> p f n", f=FC) for _ in range(2)]
        xt_tok = [take(C2) for _ in range(2)]
        xt_ch = [take(2 * P).rearrange("p (a n) -> p a n", a=2) for _ in range(2)]
        y_tok = [take(C2) for _ in range(2)]
        rt = take(24 * PAIRS * NE).rearrange("p (r n) -> p r n", r=24)
        ntile = take(NE * PAIRS).rearrange("p (e j) -> p e j", e=NE)
        later = take(NE * TILES).rearrange("p (e j) -> p e j", e=NE)
        assert o <= pool.shape[1], (o, pool.shape)
        b2_sb = sb("b2_sb", [P, 2 * NE, C2])
        wm = sb("wm", [P, 2, PAIRS])
        cnt = sb("cnt", [P, 8, NE])
        begin = sb("begin", [P, NE])
        iota_sb = sb("iota_sb", [P, PAIRS + 2])
        ids_sb = sb("ids_sb", [P, PAIRS])
        dest = sb("dest", [P, 2, PAIRS], U32)
        src = sb("src", [P, 2, PAIRS], U32)
        expert = sb("expert", [P, TILES], I32)
        zrow = sb("zrow", [P, C2])

        HID_BANKS = [(0, 4), (4, FC)]
        half = COMMON // 2
        BITS = 27
        STEPS = 8
        EARLY = 12
        NEWTON = 9
        N_WLOADS = 31

        yu = w1_all[:, 0:PAIRS * C2].rearrange("p (j n) -> p j n", j=PAIRS)

        @block.sync
        def _(sp):
            for dst, src in [(id_sb[:], ident), (ones_sb[:], onesc), (gmask_sb[:], gmask), (rmask_sb[:], rmask),
                             (ones_pp[:], ones), (center_sb[:], center), (amask_sb[:], amask),
                             (valid_sb[:], valid), (bmask_sb[:], bmask),
                             (tri_sb[:], tri), (iota_sb[:], iota), (ids_sb[:], ids),
                             (select_f, select), (partm_sb[:], partm), (wcv[:, 0:TAP0[7], :], wc), (wcv[:, TAP0[7], :], ident),
                             (w0_sb[:], w0), (aff_sb[:], aff),
                             (projw_sb[:], projw), (projb_sb[:], projb.partition_broadcast(P)),
                             (wqkv_sb[:, 0, :], wqkv[0:P, :]), (wqkv_sb[0:CB, 1, :], wqkv[P:C2, :]),
                             (bq_sb[:, 0:1], bq[0:P, :]), (bq_sb[0:CB, 1:2], bq[P:C2, :]),
                             (bkv_sb[:], bkv.partition_broadcast(P)), (wproj_sb[:, 0, :], wproj[0:P, :]),
                             (wproj_sb[0:CB, 1, :], wproj[P:C2, :]), (bproj_sb[:], bproj.partition_broadcast(P)),
                             (wr_sb[:, 0, :], wr[0:P, :]), (wr_sb[0:CB, 1, :], wr[P:C2, :]),
                             (br_sb[:], br.partition_broadcast(P))]:
                sp.dma_start(dst, src).then_inc(load_w, 16)
            sp.dma_start(b2_sb[:].rearrange("p e n -> p (e n)"), b2.partition_broadcast(P)).then_inc(small_load, 16)

            def load_pair(i):
                cols = xt[:, bass.ds(i * N, N)]
                for r in range(RES0):
                    lo = STRIDE0 * r
                    k = min(TAPS0, SPAN - lo)
                    p0 = (r % HALF) * TAPS0
                    sp.dma_start(xin[p0:p0 + k, r // HALF, :], cols[lo:lo + k, :]).then_inc(load_x, 16)
                over = xt[0:TAPS0 - STRIDE0, bass.ds(i * N, N)].rearrange("p (b q) -> p b q", b=2)
                sp.dma_start(xin[XR - (TAPS0 - STRIDE0):XR, 1, :].rearrange("p (b q) -> p b q", b=2)[:, :, 0:Q - 1],
                             over[:, :, 1:Q]).then_inc(load_x, 16)

            sp.wait_ge(xin_inited, 1)
            load_pair(0)
            sp.wait_ge(inited, 1)
            for c in range(0, TILES, 2):
                sp.dma_start(xs_dram[c * P:(c + 2) * P, :].rearrange("(a p) n -> p a n", p=P),
                             zrow[:].unsqueeze(1).to_broadcast([P, 2, C2])).then_inc(cleared, 16)
            with sp.Fori(0, PAIRS - 1) as i:
                sp.wait_ge(xn_ready, i + 1)
                load_pair(i + 1)

            sp.wait_ge(logits_done, 1)
            for e in range(2 * NE):
                at_e = w1_all[:, e * 2 * FF:(e + 1) * 2 * FF]
                sp.dma_start(at_e[:, 0:FF], w1[e * C2:e * C2 + P, :]).then_inc(w_load, 16)
                sp.dma_start(at_e[0:CB, FF:2 * FF], w1[e * C2 + P:(e + 1) * C2, :]).then_inc(w_load, 16)
                sp.dma_start(at_e[CB:CB + 1, FF:2 * FF], b1[e:e + 1, :]).then_inc(w_load, 16)
                sp.dma_start(w2_all[:, e * FC * C2:(e + 1) * FC * C2].rearrange("p (c n) -> p c n", c=FC),
                             w2[e * FF:(e + 1) * FF, :].rearrange("(c p) n -> p c n", p=P)).then_inc(w_load, 16)

            def load_tile(row, k):
                sp.dma_start(xt_tok[k], xs_dram[bass.ds(row, P), :]).then_inc(x_load[k], 16)

            def store_tile(t, k, rows):
                rows, row = (yc_dram, t * P) if rows == "common" else (yu_dram, (t - COMMON) * P)
                sp.dma_start(rows[bass.ds(row, P), :], y_tok[k]).then_inc(y_store[k], 16)

            def steps(g, rows):
                for k in range(2):
                    sp.wait_ge(xt_ps, 2 * g + (k + 1))
                    load_tile((2 * g + 2 + k) * P, k)
                    if rows[k]:
                        sp.wait_ge(y_sb, 2 * g + (k + 2))
                        store_tile(2 * g + (k - 1), 1 - k, rows[k])
            sp.wait_ge(scattered[0], 16 * PAIRS)
            for k in range(2):
                load_tile(k * P, k)
            steps(0, (None, "common"))
            with sp.Fori(0, half - 2) as g:
                steps(g + 1, ("common", "common"))
            sp.wait_ge(scattered[1], 16 * PAIRS)
            steps(half - 1, ("common", "common"))
            steps(half, ("common", "unique"))
            with sp.Fori(0, UNIQUE // 2 - 2) as g:
                steps(g + (half + 1), ("unique", "unique"))
            for t in range(TILES - 3, TILES):
                sp.wait_ge(y_sb, t + 3)
                store_tile(t, t % 2, "unique")

            for q in range(4):
                sp.wait_ge(mixed_u, (q + 1) * 8)
                for b in range(2):
                    sp.dma_start(out[8 * q:8 * q + 8, b, :, :].rearrange("j t n -> t j n"),
                                 h2[PAD6 * b:PAD6 * b + T6, 2 + 8 * q:10 + 8 * q, :]).then_inc(stored, 16)
            sp.wait_ge(stored, 16 * 8)

        XLOADS = RES0 + 1

        @block.gpsimd
        def _(pool_e):
            nc.gpsimd.memset(xin, 0.0).then_inc(xin_inited, 1)
            nc.gpsimd.memset(mhalf[:], -0.5)
            nc.gpsimd.memset(act0, 0.0)
            nc.gpsimd.memset(act1, 0.0)
            nc.gpsimd.memset(act2, 0.0)
            nc.gpsimd.memset(act3, 0.0)
            nc.gpsimd.memset(pool[:, at[4]:at[7]], 0.0)
            nc.gpsimd.memset(nout[:], 0.0)
            nc.gpsimd.memset(xn, 0.0)
            nc.gpsimd.memset(zrow[:], 0.0).then_inc(inited, 1)

            def token_rstd(i, k):
                pool_e.wait_ge(tvar_ready, i * 2 + k // 6 + 1)
                nc.gpsimd.tensor_tensor(trs[:], tv[:], mhalf[:, 0:1], ALU.pow).then_inc(trstd_ready, 1)

            def body(i, slots, first=False, last=False, with_next=True, with_att=True):
                for what, k in order(slots, first, last, with_next, with_att):
                    if what == "att" and k in (0, 6):
                        token_rstd(i, k)

            body(0, SLOTS, first=True)
            with pool_e.Fori(0, PAIRS - 2) as j:
                body(j + 1, SLOTS)
            body(PAIRS - 1, SLOTS, last=True, with_next=False)
            body(PAIRS, TAIL, with_next=False)
            for k in (0, 6):
                token_rstd(PAIRS + 1, k)

            pool_e.wait_ge(cleared, 16 * TILES // 2)
            offset = bass.IndirectOffsetOnAxis
            for u in range(2):
                pool_e.wait_ge(placed, u + 1)
                for j in range(PAIRS):
                    nc.gpsimd.indirect_dma_start(xs_dram, offset(ap=dest[:, u, j:j + 1], axis=0), x2[:, 2 + j, :],
                                                 None).then_inc(scattered[u], 16)
            pool_e.wait_ge(scattered[1], 16 * PAIRS)
            for k in range(2):
                pool_e.wait_ge(y_store[k], 16 * (COMMON // 2 + 1))
            for j in range(PAIRS):
                nc.gpsimd.indirect_dma_start(x2[:, 2 + j, :], None, yc_dram,
                                             offset(ap=src[:, 0, j:j + 1], axis=0)).then_inc(gathered_c, 16)
            for k in range(2):
                pool_e.wait_ge(y_store[k], 16 * (TILES // 2 + 1))
            for j in range(PAIRS):
                nc.gpsimd.indirect_dma_start(yu[:, j, :], None, yu_dram,
                                             offset(ap=src[:, 1, j:j + 1], axis=0)).then_inc(gathered_u[j // 8], 16)

        ON_SCALAR = (1, 2, 5)

        @block.scalar
        def _(act):
            def attention(i, k):
                if k not in ON_SCALAR + (7,):
                    return
                act.wait_ge(att_ps, i * ATT + k + 1)
                both = ps_a[:, 0:2 * P].rearrange("p (a n) -> p a n", a=2)
                if k == 1:
                    last = nc.scalar.activation(xnT, both, ACT.Identity)
                elif k == 2:
                    nc.scalar.activation(qT[:, 0, :], ps_a[:, 0:P], ACT.Identity, bias=bq_sb[:, 0:1])
                    last = nc.scalar.activation(qT[0:CB, 1, :], ps_a[0:CB, P:2 * P], ACT.Identity, bias=bq_sb[0:CB, 1:2])
                elif k == 5:
                    nc.scalar.activation(oT[:, 0, :], ps_a[:, 0:P], ACT.Identity)
                    last = nc.scalar.activation(oT[0:CB, 1, :], ps_a[0:CB, P:2 * P], ACT.Identity)
                else:
                    last = nc.scalar.activation(x2T, both, ACT.Identity)
                last.then_inc(att_sb, 1)

            def l0_tile(i, k):
                r = residue(k)
                act.wait_ge(l0_ready, i * RES0 + k + 1)
                act_in = ps_l0[:, k % 2, 0:N].rearrange("p (b q) -> p b q", b=2)
                nc.scalar.activation(act0[:, r, :, 0:Q], act_in, ACT.Gelu, bias=aff_sb[:, 1, 0:1],
                                     scale=aff_sb[:, 0, 0:1]).then_inc(l0_gelu, 1)

            def finish(i, slots, s):
                layer, t = slots[s]
                n = SPREAD.get(layer, N)
                act.wait_ge(norm_done, i * NS + s + 4)
                src = nrm[:, s % 2, 0:n].rearrange("p (b q) -> p b q", b=2)
                dst = {1: act1[:, t, :, 0:Q], 2: act2[:, t % 4, :, 0:Q], 3: act3[:, t % 2, :, 0:Q],
                       4: act4, 5: act5, 6: act6.rearrange("p (b q) -> p b q", b=2), 7: nout[:, :, 0:T6]}[layer]
                nc.scalar.activation(dst, src, ACT.Identity if layer == 7 else ACT.Gelu,
                                     bias=aff_sb[:, 1, layer:layer + 1],
                                     scale=aff_sb[:, 0, layer:layer + 1]).then_inc(gelu_done, 1)

            def body(i, slots, first=False, last=False, with_next=True, with_att=True):
                for what, k in order(slots, first, last, with_next, with_att):
                    if what == "conv":
                        act.wait_ge(y_ready, i * NS + k + 1)
                        n = SPREAD.get(slots[k][0], N)
                        nc.scalar.activation(sq[:, k % 2, 0:n], ps_y[:, k % 2, 0:n], ACT.Square).then_inc(sq_done, 1)
                        act.wait_ge(norm_done, i * NS + k + 1)
                        nc.scalar.activation(ycp[:, k % LAG, 0:n], ps_y[:, k % 2, 0:n], ACT.Identity).then_inc(ycopy_done, 1)
                    elif what == "bcast":
                        finish(i, slots, k)
                    elif what == "l0":
                        l0_tile(i + 1, k)
                    elif what == "att":
                        attention(i, k)

            act.wait_ge(load_w, 16 * N_WLOADS)
            for _ in range(2):
                nc.scalar.activation(spare(), ones_sb[:, 0:1], ACT.Gelu).then_inc(gelu_done, 1)
            for r in range(RES0):
                l0_tile(0, r)
            body(0, SLOTS, first=True)
            with act.Fori(0, PAIRS - 2) as j:
                body(j + 1, SLOTS)
            body(PAIRS - 1, SLOTS, last=True, with_next=False)
            body(PAIRS, TAIL, with_next=False)
            for k in range(ATT):
                attention(PAIRS + 1, k)

            act.wait_ge(shifted, 1)
            nc.scalar.activation(rt[:, 1:3, :], rt[:, 1:3, :], ACT.Exp).then_inc(exp_done, 1)

            def hidden(t, k):
                for c, (f0, f1) in enumerate(HID_BANKS):
                    act.wait_ge(hid_ps, 2 * t + (c + 1))
                    nc.scalar.activation(hid[k][:, f0:f1, :],
                                         up_banks[k][:, c, 0:(f1 - f0) * P].rearrange("p (f n) -> p f n", f=f1 - f0),
                                         ACT.Gelu).then_inc(hid_sb, 1)
            with act.Fori(0, TILES // 2) as g:
                for k in range(2):
                    hidden(2 * g + k, k)

        @block.vector
        def _(dve):
            links = [0]

            def link(ins, base=0):
                links[0] += 1
                ins.then_inc(dve_seq, 1)
                dve.wait_ge(dve_seq, base + links[0])

            dve.wait_ge(inited, 1)
            dve.wait_ge(load_w, 16 * N_WLOADS)
            nc.vector.memset(spare(), 0.0).then_inc(att_sb, 1)
            for _ in range(LAG):
                nc.vector.memset(spare(), 0.0).then_inc(norm_done, 1)
            for _ in range(2):
                nc.vector.memset(spare(), 0.0).then_inc(ycopy_done, 1)
            nc.vector.memset(spare(), 0.0).then_inc(steps_v, 1)
            nc.vector.tensor_copy(select_sb[:], select_f)
            link(nc.vector.tensor_reduce(wmean[:], wcv[:], AX_X, ALU.add))
            link(nc.vector.tensor_scalar(wmean[:], wmean[:], 1.0 / C, None, ALU.mult))
            nc.vector.tensor_tensor(wcv[:], wcv[:], wmean[:].unsqueeze(2).to_broadcast([P, NTAP, C]),
                                    ALU.subtract).then_inc(w_center, 1)
            dve.wait_ge(w0_ps, 1)
            link(nc.vector.tensor_copy(w0c[:], ps_a[:, 0:TAPS0].unsqueeze(1).to_broadcast([P, HALF, TAPS0])))
            nc.vector.memset(spare(), 0.0).then_inc(w0_done, 1)
            dve.wait_ge(w0_ps, 2)
            link(nc.vector.tensor_tensor(gram[:], ps_a[0:XR, 0:XR], gmask_sb[:], ALU.mult))
            link(nc.vector.tensor_copy(w0t[:], ps_a[0:XR, P:2 * P]))
            for r in range(HALF):
                last = nc.vector.tensor_scalar(w0r[:, r, :], w0t[:], rmask_sb[:, r:r + 1], None, ALU.mult)
            last.then_inc(w0_done, 1)
            LINK0 = links[0]
            ATT_LINKS = 7

            def rsqrt(i):
                n = [0]

                def then(ins):
                    n[0] += 1
                    ins.then_inc(newton, 1)
                    dve.wait_ge(newton, i * NEWTON + n[0])
                v, y, a, c, d = pv[0:BLK, :], nt[0:BLK, 0, :], nt[0:BLK, 1, :], nt[0:BLK, 2, :], nt[0:BLK, 3, :]
                then(nc.vector.tensor_scalar(v, ps_v[0:BLK, 256:320], EPS, EPS, ALU.add, ALU.max))
                then(nc.vector.tensor_scalar(y.bitcast(I32), v.bitcast(I32), -0.5, float(0x5F3759DF), ALU.mult, ALU.add))
                then(nc.vector.tensor_tensor(a, y, y, ALU.mult))
                then(nc.vector.tensor_tensor(c, a, v, ALU.mult))
                then(nc.vector.tensor_scalar(d, c, 0.375, -1.25, ALU.mult, ALU.add))
                then(nc.vector.tensor_tensor(a, d, c, ALU.mult))
                then(nc.vector.scalar_tensor_tensor(d, a, 1.875, y, ALU.add, ALU.mult))
                then(nc.vector.scalar_tensor_tensor(a, d, -0.5, d, ALU.mult, ALU.mult))
                then(nc.vector.tensor_tensor(c, a, v, ALU.mult))
                wide = [BLK, 4 * 2 * HALF, TAPS0]
                nc.vector.scalar_tensor_tensor(prx[0:BLK].rearrange("p (m k) -> p m k", k=TAPS0),
                                               c.unsqueeze(2).to_broadcast(wide), 1.5,
                                               d.unsqueeze(2).to_broadcast(wide), ALU.add, ALU.mult).then_inc(prstd_ready, 1)

            def prep(i, what):
                if what == "zmm":
                    dve.wait_ge(z_ready, i + 1)
                    nc.vector.tensor_tensor(prod, ps_l0[0:XR, :, 0:N], xin, ALU.mult).then_inc(prod_done, 1)
                elif what == "psum":
                    dve.wait_ge(psum_ready, i + 1)
                    rsqrt(i)
                elif what == "pbc":
                    dve.wait_ge(pbc_ready, i + 1)
                    nc.vector.tensor_tensor(xnorm[:], ps_l0[0:XR, :, 0:N], xin, ALU.mult).then_inc(xn_ready, 1)

            def layernorm(i, half, src, base):
                link(nc.vector.bn_stats(st[:], src), base)
                nc.vector.memset(zero1[:], 0.0)
                link(nc.vector.bn_aggr(mv[:], st[:]), base)
                nc.vector.tensor_scalar(tv[:], mv[:, 1:2], EPS, None, ALU.add).then_inc(tvar_ready, 1)
                dve.wait_ge(trstd_ready, i * 2 + half + 1)
                return nc.vector.tensor_scalar(xn[:, 0:C2], src, mv[:, 0:1], trs[:], ALU.subtract, ALU.mult)

            def attention(i, k):
                if k in ON_SCALAR:
                    return
                if k == 0:
                    links[0] = LINK0
                base = i * ATT_LINKS
                dve.wait_ge(att_ps, i * ATT + k + 1)
                if k == 0:
                    link(nc.vector.tensor_tensor(hb[:], ps_a[:, 0:C2], projb_sb[:], ALU.add), base)
                    layernorm(i, 0, hb[:], base)
                    last = nc.vector.tensor_tensor(hp[:], hb[:], bproj_sb[:], ALU.add)
                elif k == 3:
                    link(nc.vector.tensor_tensor(kv[:], ps_a[:, 0:2 * C2], bkv_sb[:], ALU.add), base)
                    for b in range(2):
                        last = nc.vector.tensor_scalar(km[:, b, :], kv[:, 0:C2], bmask_sb[:, b:b + 1], None, ALU.mult)
                elif k == 4:
                    m = ps_a[:, 0:2 * C2].rearrange("p (b n) -> p b n", b=2)
                    nc.vector.tensor_tensor(ms[:, :, 0:P], m[:, :, 0:P],
                                            amask_sb[:, 0:P].unsqueeze(1).to_broadcast([P, 2, P]), ALU.mult)
                    last = nc.vector.tensor_tensor(ms[0:CB, :, P:C2], m[0:CB, :, P:C2],
                                                   amask_sb[0:CB, P:C2].unsqueeze(1).to_broadcast([CB, 2, CB]), ALU.mult)
                elif k == 6:
                    nc.vector.tensor_tensor(h2_flat[:, bass.ds(i * C2, C2)], ps_a[:, 0:C2], hp[:], ALU.add)
                    link(nc.vector.tensor_tensor(hb[:], ps_a[:, 0:C2], hp[:], ALU.add), base)
                    last = layernorm(i, 1, hb[:], base)
                elif k == 7:
                    nc.vector.tensor_copy(x2_flat[:, bass.ds(i * C2, C2)], xn[:, 0:C2])
                    return
                else:
                    last = nc.vector.tensor_tensor(lg_flat[:, bass.ds(i * 2 * NE, 2 * NE)],
                                                   ps_a[:, 0:2 * NE], br_sb[:], ALU.add)
                last.then_inc(att_sb, 1)

            def body(i, slots, first=False, last=False, with_next=True, with_att=True):
                unsplit = None if first or slots is TAIL else (i * NS - 2, SPREAD.get(slots[-2][0], N) // 4, 0)
                for what, k in order(slots, first, last, with_next, with_att):
                    T = i * NS + k
                    n = SPREAD.get(slots[k][0], N) if what in ("split", "colsum", "bcast") else 0
                    if what == "colsum":
                        newton_and_split((T, n // 4, k % 2), unsplit)
                        unsplit = (T, n // 4, k % 2)
                    elif what == "split":
                        newton_and_split(None, unsplit)
                        unsplit = None
                    elif what == "bcast":
                        dve.wait_ge(bcast_ready, T + 1)
                        dve.wait_ge(gelu_done, T + 1)
                        dve.wait_ge(ycopy_done, T + 3)
                        nc.vector.tensor_tensor(nrm[:, k % 2, 0:n], ycp[:, k % LAG, 0:n], ps_r[:, k % 2, 0:n],
                                                ALU.mult).then_inc(norm_done, 1)
                    elif what == "att":
                        attention(i, k)
                    elif what in ("zmm", "psum", "pbc"):
                        prep(i + 1, what)

            stt, ts, tt = nc.vector.scalar_tensor_tensor, nc.vector.tensor_scalar, nc.vector.tensor_tensor

            def newton_step(slot, n):
                T, w, b = slot
                v, y, a, e, c, d = vv[:, b, 0:w], y0[:, b, 0:w], na[:, 0:w], nb[:, 0:w], c2[:, b, 0:w], d2[:, b, 0:w]
                if n:
                    dve.wait_ge(steps_v, T * STEPS + (n + 1))
                if n == 0:
                    dve.wait_ge(colsum_ready, T + 1)
                    last = ts(v, ps_v[:, 0:w], EPS, None, ALU.add)
                elif n == 1:
                    last = ts(y.bitcast(I32), v.bitcast(I32), -0.5, float(0x5F3759DF), ALU.mult, ALU.add)
                elif n == 2:
                    last = tt(a, y, y, ALU.mult)
                elif n == 3:
                    last = tt(e, a, v, ALU.mult)
                elif n == 4:
                    last = stt(a, e, -10.0 / 3.0, e, ALU.add, ALU.mult)
                elif n == 5:
                    last = stt(d, a, 5.0, y, ALU.add, ALU.mult)
                elif n == 6:
                    last = stt(a, d, -0.5 * 0.375 ** 3, d, ALU.mult, ALU.mult)
                else:
                    last = tt(c, a, v, ALU.mult)
                last.then_inc(steps_v, 1)

            def split_step(slot, n):
                T, w, b = slot
                c, d = c2[:, b, 0:w], d2[:, b, 0:w]
                if n == 0:
                    dve.wait_ge(steps_v, T * STEPS + (STEPS + 1))
                    stt(high[:, 0:w], c, 1.5 * 0.375, d, ALU.add, ALU.mult)
                elif n == 1:
                    stt(rstd[:, 0:w], c, 1.5 * 0.375, d, ALU.add, ALU.mult).then_inc(split_seq, 1)
                elif n == 2:
                    dve.wait_ge(split_seq, T * 2 + 1)
                    stt(second[:, 0:w], high[:, 0:w], partm_sb[:, 0:1], rstd[:, 0:w], ALU.mult, ALU.add)
                elif n == 3:
                    stt(rest[:, 0:w], high[:, 0:w], partm_sb[:, 0:1], rstd[:, 0:w], ALU.mult, ALU.add).then_inc(split_seq, 1)
                else:
                    dve.wait_ge(split_seq, T * 2 + 2)
                    stt(parts[:, b, 0:w], second[:, 0:w], partm_sb[:, 1:2], rest[:, 0:w], ALU.mult, ALU.add).then_inc(rstd_ready, 1)

            def newton_and_split(slot, before):
                for n in range(STEPS):
                    if slot is not None:
                        newton_step(slot, n)
                    if before is not None and n < 5:
                        split_step(before, n)

            dve.wait_ge(load_x, 16 * XLOADS)
            for what in ("zmm", "psum", "pbc"):
                prep(0, what)
            body(0, SLOTS, first=True)
            with dve.Fori(0, PAIRS - 2) as j:
                body(j + 1, SLOTS)
            body(PAIRS - 1, SLOTS, last=True, with_next=False)
            body(PAIRS, TAIL, with_next=False)
            for k in range(ATT):
                attention(PAIRS + 1, k)
            assert links[0] == LINK0 + ATT_LINKS, links[0] - LINK0

            dve.wait_ge(att_sb, ATT * (PAIRS + 2) + 1)
            nc.vector.memset(spare(), 0.0).then_inc(logits_done, 1)
            steps = [0]

            def then(ins):
                steps[0] += 1
                ins.then_inc(route_seq, 1)
                dve.wait_ge(route_seq, steps[0])

            def row(r, n=1):
                return rt[:, r, 0:n * PAIRS]

            def mat(r):
                return rt[:, r, :].rearrange("p (e j) -> p e j", e=NE)

            def rep(a):
                return a.unsqueeze(1).to_broadcast([P, NE, PAIRS])

            logit = [lg[:, 2:2 + PAIRS, NE * u:NE * (u + 1)] for u in range(2)]
            for u in range(2):
                then(nc.vector.tensor_reduce(row(3 + u), logit[u], AX_X, ALU.max))
                then(nc.vector.tensor_tensor(mat(1 + u), logit[u].rearrange("p j e -> p e j"), rep(row(3 + u)), ALU.subtract))
                then(nc.vector.tensor_scalar(rt[:, 5 + u, :], rt[:, 1 + u, :], 0.0, None, ALU.is_equal))
            nc.vector.memset(spare(), 0.0).then_inc(shifted, 1)
            dve.wait_ge(exp_done, 1)
            for u in range(2):
                then(nc.vector.tensor_reduce(row(3 + u), mat(1 + u).rearrange("p e j -> p j e"), AX_X, ALU.add))
                then(nc.vector.reciprocal(row(7 + u), row(3 + u)))
                then(nc.vector.reciprocal(row(9 + u), row(7 + u)))
                then(nc.vector.tensor_tensor(row(9 + u), row(9 + u), row(7 + u), ALU.mult))
                then(nc.vector.tensor_copy(row(11), mat(5 + u)[:, 0, :]))
                for e in range(1, NE):
                    then(nc.vector.tensor_copy(row(12), mat(5 + u)[:, e, :]))
                    then(nc.vector.tensor_tensor(mat(5 + u)[:, e, :], row(12), row(11), ALU.is_gt))
                    then(nc.vector.tensor_tensor(row(11), row(11), row(12), ALU.max))
                then(nc.vector.tensor_copy(wm[:, u, :], row(9 + u)))
            for u in range(2):
                then(nc.vector.tensor_scalar(rt[:, 5 + u, :], rt[:, 5 + u, :], valid_sb[:], None, ALU.mult))

            def before():
                then(nc.vector.tensor_copy(mat(17), ps_a[:, 128:256].rearrange("p (e j) -> p e j", e=NE)))
                then(nc.vector.memset(rt[:, 18, :], 0.0))
                then(nc.vector.tensor_copy(mat(18)[:, :, 1:PAIRS], mat(17)[:, :, 0:PAIRS - 1]))
                a, b_ = 18, 19
                d = 1
                while d < PAIRS:
                    then(nc.vector.tensor_copy(rt[:, b_, :], rt[:, a, :]))
                    then(nc.vector.tensor_tensor(mat(b_)[:, :, d:PAIRS], mat(a)[:, :, d:PAIRS], mat(a)[:, :, 0:PAIRS - d], ALU.add))
                    a, b_ = b_, a
                    d *= 2
                assert a == PREFIX

            PREFIX = 18 + (PAIRS - 1).bit_length() % 2
            a = PREFIX

            def expert_tiles(counted):
                dve.wait_ge(count_sum, counted)
                before()
                then(nc.vector.tensor_tensor(cnt[:, 6, :], mat(a)[:, :, PAIRS - 1], mat(17)[:, :, PAIRS - 1], ALU.add))
                then(nc.vector.tensor_scalar(cnt[:, 6, :], cnt[:, 6, :], 1.0 / P, None, ALU.mult))
                then(nc.vector.tensor_tensor(ntile, cnt[:, 6, :].unsqueeze(2).to_broadcast([P, NE, PAIRS]),
                                             rep(iota_sb[:, 0:PAIRS]), ALU.is_gt))
                then(nc.vector.tensor_reduce(cnt[:, 7, :], ntile, AX_X, ALU.add))
                then(nc.vector.memset(begin[:, 0:1], 0.0))
                for e in range(1, NE):
                    then(nc.vector.tensor_tensor(begin[:, e:e + 1], begin[:, e - 1:e], cnt[:, 7, e - 1:e], ALU.add))

            def tile_experts(u):
                base, tiles = (0, COMMON) if u == 0 else (COMMON, UNIQUE)
                for e in range(1, NE):
                    nc.vector.tensor_scalar(later[:, e, 0:tiles], iota_sb[:, 0:tiles], begin[:, e:e + 1], None, ALU.is_ge)
                then(nc.vector.memset(later[:, 0, 0:tiles], float(NE * u)))
                for e in range(1, NE):
                    then(nc.vector.tensor_tensor(later[:, 0, 0:tiles], later[:, 0, 0:tiles], later[:, e, 0:tiles], ALU.add))
                then(nc.vector.tensor_copy(expert[:, base:base + tiles], later[:, 0, 0:tiles]))

            def token_rows(u):
                base = 0 if u == 0 else COMMON
                then(nc.vector.tensor_tensor(rt[:, a, :], rt[:, a, :], ps_a[:, 256:384], ALU.add))
                then(nc.vector.tensor_scalar(begin[:], begin[:], float(P), None, ALU.mult))
                then(nc.vector.tensor_tensor(mat(a), mat(a), begin[:].unsqueeze(2).to_broadcast([P, NE, PAIRS]), ALU.add))
                then(nc.vector.tensor_tensor(rt[:, a, :], rt[:, a, :], rt[:, 16, :], ALU.mult))
                then(nc.vector.tensor_reduce(row(20), mat(a).rearrange("p e j -> p j e"), AX_X, ALU.add))
                then(nc.vector.tensor_reduce(row(22), mat(16).rearrange("p e j -> p j e"), AX_X, ALU.add))
                then(nc.vector.tensor_copy(src[:, u, :], row(20)))
                then(nc.vector.tensor_scalar(row(22), row(22), -1.0, 1.0, ALU.mult, ALU.add))
                then(nc.vector.scalar_tensor_tensor(row(23), ids_sb[:], float(TRASH[u] - base * P), row(22), ALU.add, ALU.mult))
                then(nc.vector.scalar_tensor_tensor(row(23), row(23), float(base * P), row(20), ALU.add, ALU.add))
                then(nc.vector.tensor_copy(dest[:, u, :], row(23)))
                nc.vector.memset(spare(), 0.0).then_inc(placed, 1)

            then(nc.vector.tensor_copy(rt[:, 16, :], rt[:, 5, :]))
            nc.vector.memset(spare(), 0.0).then_inc(count_ready, 1)
            expert_tiles(1)
            tile_experts(0)
            token_rows(0)
            then(nc.vector.tensor_tensor(mat(13), mat(5), rep(row(7)), ALU.mult))
            thr, cand, step, ge = cnt[:, 0, :], cnt[:, 1, :], cnt[:, 2, :], cnt[:, 3, :]
            then(nc.vector.memset(step, 1.0))
            then(nc.vector.memset(thr, 0.0))
            PER = 5
            seq0 = steps[0]

            def count_above(b):
                nc.vector.tensor_tensor(cand, thr, step, ALU.add).then_inc(route_seq, 1)
                dve.wait_ge(route_seq, b * PER + (seq0 + 1))
                nc.vector.tensor_tensor(mat(14), mat(13), cand.unsqueeze(2).to_broadcast([P, NE, PAIRS]),
                                        ALU.is_ge).then_inc(route_seq, 1)
                dve.wait_ge(route_seq, b * PER + (seq0 + 2))
                nc.vector.tensor_reduce(cnt[:, 4, :], mat(14), AX_X, ALU.add).then_inc(count_ready, 1)

            def next_bit(b):
                dve.wait_ge(count_sum, b + 2)
                nc.vector.scalar_tensor_tensor(ge, ps_a[:, 0:NE], float(CAP), step, ALU.is_ge, ALU.mult).then_inc(route_seq, 1)
                dve.wait_ge(route_seq, b * PER + (seq0 + 3))
                nc.vector.tensor_tensor(thr, thr, ge, ALU.add).then_inc(route_seq, 1)
                dve.wait_ge(route_seq, b * PER + (seq0 + 4))
                nc.vector.tensor_scalar(step, step, 0.5, None, ALU.mult).then_inc(route_seq, 1)
                dve.wait_ge(route_seq, b * PER + (seq0 + 5))
                count_above(b + 1)

            def ties():
                tb = thr.unsqueeze(2).to_broadcast([P, NE, PAIRS])
                then(nc.vector.tensor_tensor(mat(15), mat(13), tb, ALU.is_gt))
                then(nc.vector.tensor_tensor(mat(16), mat(13), tb, ALU.is_equal))
                then(nc.vector.tensor_tensor(mat(16), mat(16), mat(5), ALU.mult))
                nc.vector.tensor_reduce(cnt[:, 4, :], mat(15), AX_X, ALU.add).then_inc(count_ready, 1)

            def tie_ranks():
                dve.wait_ge(count_sum, BITS + 2)
                then(nc.vector.tensor_scalar(cnt[:, 5, :], ps_a[:, 0:NE], -1.0, float(CAP), ALU.mult, ALU.add))
                before()

            def dropped():
                then(nc.vector.tensor_tensor(rt[:, a, :], rt[:, a, :], ps_a[:, 256:384], ALU.add))
                then(nc.vector.tensor_tensor(mat(20), mat(a), cnt[:, 5, :].unsqueeze(2).to_broadcast([P, NE, PAIRS]), ALU.is_lt))
                then(nc.vector.tensor_tensor(rt[:, 20, :], rt[:, 20, :], rt[:, 16, :], ALU.mult))
                then(nc.vector.tensor_tensor(rt[:, 15, :], rt[:, 15, :], rt[:, 20, :], ALU.add))
                then(nc.vector.tensor_reduce(row(21), mat(15).rearrange("p e j -> p j e"), AX_X, ALU.add))
                then(nc.vector.tensor_scalar(row(21), row(21), -1.0, 1.0, ALU.mult, ALU.add))
                then(nc.vector.tensor_tensor(wm[:, 1, :], wm[:, 1, :], row(21), ALU.mult))
                then(nc.vector.tensor_tensor(mat(16), mat(6), rep(row(21)), ALU.mult))
                nc.vector.memset(spare(), 0.0).then_inc(count_ready, 1)

            dve.wait_ge(small_load, 16)
            dve.wait_ge(w_load, 16 * 4 * 2 * NE)
            for k in range(2):
                nc.vector.memset(xt_ch[k][CB:CB + 1, 1, :], 1.0)
                nc.vector.memset(spare(), 0.0).then_inc(y_sb, 1)
                nc.vector.memset(spare(), 0.0).then_inc(y_store[k], 16)
            nc.vector.memset(spare(), 0.0).then_inc(xt_sb, 1)
            b2_flat = b2_sb[:].rearrange("p e n -> p (e n)")
            def first_weights(t, k, free=True):
                e = dve.value_load(expert[0:1, bass.ds(t, 1)], min_val=0, max_val=2 * NE - 1)
                if free:
                    dve.wait_ge(hid_ps, 2 * t - 2)
                nc.vector.tensor_copy(w1_cur[k][:, 0, :], w1_all[:, bass.ds(e * (2 * FF), FF)])
                nc.vector.tensor_copy(w1_cur[k][0:CB + 1, 1, :],
                                      w1_all[0:CB + 1, bass.ds(e * (2 * FF) + FF, FF)]).then_inc(w1_ready, 1)

            def channel_major(t, k):
                dve.wait_ge(xt_ps, t + 1)
                nc.vector.tensor_copy(xt_ch[k][:, 0, :], ps_v[:, 0:P])
                nc.vector.tensor_copy(xt_ch[k][0:CB, 1, :], ps_v[0:CB, P:2 * P]).then_inc(xt_sb, 1)

            def expert_rows(t, k, turn):
                e = dve.value_load(expert[0:1, bass.ds(t, 1)], min_val=0, max_val=2 * NE - 1)
                dve.wait_ge(down_ps, t + 1)
                dve.wait_ge(y_store[k], 16 * turn + 16)
                nc.vector.tensor_tensor(y_tok[k], out_banks[k][:, 0:C2], b2_flat[:, bass.ds(e * C2, C2)],
                                        ALU.add).then_inc(y_sb, 1)

            count_above(0)
            with dve.Fori(0, EARLY) as b:
                next_bit(b)
            first_weights(0, 0, False)
            channel_major(0, 0)
            first_weights(1, 1, False)
            channel_major(1, 1)
            first_weights(2, 0)
            channel_major(2, 0)
            expert_rows(0, 0, 0)

            def two_tiles(g, k1=None, k2=None, k3=None):
                first_weights(2 * g + 3, 1)
                if k1:
                    k1()
                channel_major(2 * g + 3, 1)
                expert_rows(2 * g + 1, 1, g)
                if k2:
                    k2()
                first_weights(2 * g + 4, 0)
                if k3:
                    k3()
                channel_major(2 * g + 4, 0)
                expert_rows(2 * g + 2, 0, g + 1)
            done = (BITS - EARLY) // 3
            with dve.Fori(0, done) as g:
                two_tiles(g, lambda: next_bit(3 * g + EARLY), lambda: next_bit(3 * g + (EARLY + 1)),
                          lambda: next_bit(3 * g + (EARLY + 2)))
            steps[0] += BITS * PER + 2
            two_tiles(done, None, ties, None)
            two_tiles(done + 1, tie_ranks, dropped, None)
            two_tiles(done + 2, lambda: expert_tiles(BITS + 3), lambda: tile_experts(1), lambda: token_rows(1))
            with dve.Fori(0, TILES // 2 - 2 - done - 3) as g:
                two_tiles(g + (done + 3))
            first_weights(TILES - 1, 1)
            channel_major(TILES - 1, 1)
            expert_rows(TILES - 3, 1, TILES // 2 - 2)
            expert_rows(TILES - 2, 0, TILES // 2 - 1)
            expert_rows(TILES - 1, 1, TILES // 2 - 1)

            wm_flat = wm[:].rearrange("p u j -> p (u j)")
            dve.wait_ge(gathered_c, 16 * PAIRS)
            with dve.Fori(0, PAIRS) as j:
                hrow = h2_flat[:, bass.ds((j + 2) * C2, C2)]
                nc.vector.scalar_tensor_tensor(hrow, x2_flat[:, bass.ds((j + 2) * C2, C2)], wm_flat[:, bass.ds(j, 1)],
                                               hrow, ALU.mult, ALU.add).then_inc(mixed_c, 1)
            dve.wait_ge(mixed_c, PAIRS)
            yu_flat = yu.rearrange("p j n -> p (j n)")
            for q in range(4):
                dve.wait_ge(gathered_u[q], 16 * 8)
                with dve.Fori(0, 8) as j:
                    hrow = h2_flat[:, bass.ds((j + (8 * q + 2)) * C2, C2)]
                    nc.vector.scalar_tensor_tensor(hrow, yu_flat[:, bass.ds((j + 8 * q) * C2, C2)],
                                                   wm_flat[:, bass.ds(j + (PAIRS + 8 * q), 1)],
                                                   hrow, ALU.mult, ALU.add).then_inc(mixed_u, 1)

        @block.tensor
        def _(pe):
            mm = nc.tensor.matmul
            pe.wait_ge(load_w, 16 * N_WLOADS)
            last = mm(ps_a[:, 0:TAPS0], center_sb[:], w0_sb[:], start=True, stop=True)
            last.then_inc(w0_ps, 1)
            pe.wait_ge(w0_done, 1)
            w0flat = w0c[:].rearrange("p r k -> p (r k)")
            mm(ps_a[0:XR, 0:XR], w0flat, w0flat, start=True, stop=True)
            mm(ps_a[0:XR, P:2 * P], w0flat, id_sb[:], start=True, stop=True).then_inc(w0_ps, 1)
            pe.wait_ge(w0_done, 2)
            pe.wait_ge(w_center, 1)
            pe.wait_ge(inited, 1)

            def prep(i, what):
                if what == "zmm":
                    pe.wait_ge(load_x, (i + 1) * (16 * XLOADS))
                    pe.wait_ge(l0_gelu, i * RES0)
                    for h in range(2):
                        last = mm(ps_l0[0:XR, h, 0:N], gram[:], xin[:, h, :], start=True, stop=True)
                    last.then_inc(z_ready, 1)
                elif what == "psum":
                    pe.wait_ge(prod_done, i + 1)
                    for j in range(4):
                        for h in range(2):
                            c0 = 256 + (j * 2 + h) * HALF
                            last = mm(ps_v[0:BLK, c0:c0 + HALF], prod[:, h, j * BLK:(j + 1) * BLK], rmask_sb[:],
                                      start=True, stop=True)
                    last.then_inc(psum_ready, 1)
                elif what == "pbc":
                    pe.wait_ge(prstd_ready, i + 1)
                    for h in range(2):
                        for j in range(4):
                            m = 2 * j + h
                            last = mm(ps_l0[0:XR, h, j * BLK:(j + 1) * BLK], prx[0:BLK, m * XR:(m + 1) * XR],
                                      id_sb[0:BLK, 0:BLK], start=True, stop=True)
                    last.then_inc(pbc_ready, 1)

            def l0_tile(i, k):
                r = residue(k)
                if k < 2:
                    pe.wait_ge(xn_ready, i + 1)
                else:
                    pe.wait_ge(l0_gelu, i * RES0 + k - 1)
                mm(ps_l0[:, k % 2, 0:N], w0r[:, r % HALF, :], xnorm[:, r // HALF, :], start=True, stop=True).then_inc(l0_ready, 1)

            def need(i, slots, s, first):
                layer, t = slots[s]
                at = {x: k for k, x in enumerate(slots)}
                if layer == 1:
                    last = max((2 * t + k - 2) % RES0 for k in range(3))
                    pe.wait_ge(l0_gelu, i * RES0 + last + 1)
                elif layer == 2:
                    pe.wait_ge(gelu_done, i * NS + max(at[(1, (2 * t + k) % 8)] for k in range(3)) + 3)
                elif layer == 3:
                    if not first:
                        last = max(SLOTS.index((2, (2 * t + k) % 4)) for k in range(3))
                        pe.wait_ge(gelu_done, i * NS + (last - NS + 3))
                elif layer == 4:
                    pe.wait_ge(gelu_done, i * NS + max(at[(3, t)] for t in range(2)) + 3)
                else:
                    pe.wait_ge(gelu_done, i * NS + at[(layer - 1, 0)] + 3)

            def taps(layer, t):
                if layer in (1, 2, 3):
                    src = {1: act0, 2: act1, 3: act2}[layer]
                    R = {1: 16, 2: 8, 3: 4}[layer]
                    return [src[:, (2 * t + k) % R, :, (2 * t + k) // R:(2 * t + k) // R + Q] for k in range(3)]
                if layer == 4:
                    return [act3[:, k % 2, :, k // 2:k // 2 + Q] for k in range(3)]
                if layer == 5:
                    return [act4[:, :, k:k + 2 * T5 - 1:2] for k in range(2)]
                if layer == 6:
                    return [act5[:, :, k:k + 2 * T6 - 1:2] for k in range(2)]
                return [act6.rearrange("p (b q) -> p b q", b=2)]

            def conv(i, slots, s, part, first):
                layer, t = slots[s]
                n = SPREAD.get(layer, N)
                rows = taps(layer, t)
                start = max(0, len(rows) - 2) if part == 1 else len(rows) - 1 if part == 2 else 0
                last_tap = {0: len(rows) - 2, 1: len(rows) - 1, 2: len(rows)}[part]
                if start == 0 and last_tap > 0:
                    need(i, slots, s, first)
                    pe.wait_ge(ycopy_done, i * NS + s + 1)
                for k in range(start, last_tap):
                    last = mm(ps_y[:, s % 2, 0:n].rearrange("p (b q) -> p b q", b=2), wcv[:, TAP0[layer] + k, :], rows[k],
                              start=(k == 0), stop=(k == len(rows) - 1))
                if part == 2:
                    last.then_inc(y_ready, 1)

            def colsum(i, slots, s, first):
                pe.wait_ge(sq_done, i * NS + s + 1)
                if not (first and s == 0):
                    pe.wait_ge(steps_v, (i * NS + s) * STEPS - (STEPS - 2))
                w = SPREAD.get(slots[s][0], N) // 4
                for j in range(4):
                    last = mm(ps_v[QUAD * j:QUAD * (j + 1), 0:w], ones_sb[:], sq[:, s % 2, j * w:(j + 1) * w],
                              start=True, stop=True)
                last.then_inc(colsum_ready, 1)

            def bcast(i, slots, s):
                pe.wait_ge(rstd_ready, i * NS + s + 1)
                pe.wait_ge(norm_done, i * NS + s + 2)
                w = SPREAD.get(slots[s][0], N) // 4
                for j in range(4):
                    last = mm(ps_r[:, s % 2, j * w:(j + 1) * w], select_sb[:, j, :], parts[:, s % 2, 0:w],
                              start=True, stop=True)
                last.then_inc(bcast_ready, 1)

            def attention(i, k, before=None):
                pe.wait_ge(att_sb, i * ATT + k + 1)
                if k == 0:
                    pe.wait_ge(gelu_done, (i * NS if before is None else before) + 2)
                    last = mm(ps_a[:, 0:C2], nout[:].rearrange("p b q -> p (b q)"), projw_sb[:], start=True, stop=True)
                elif k in (1, 7):
                    for c in range(2):
                        last = nc.tensor.transpose(ps_a[:, c * P:(c + 1) * P], xn[:, c * P:(c + 1) * P], id_sb[:])
                elif k == 2:
                    for c, w in ((0, P), (1, CB)):
                        mm(ps_a[0:w, c * P:(c + 1) * P], wqkv_sb[:, 0, c * P:c * P + w], xnT[:, 0, :], start=True, stop=False)
                        last = mm(ps_a[0:w, c * P:(c + 1) * P], wqkv_sb[0:CB, 1, c * P:c * P + w], xnT[0:CB, 1, :],
                                  start=False, stop=True)
                elif k == 3:
                    mm(ps_a[:, 0:2 * C2], xnT[:, 0, :], wqkv_sb[:, 0, C2:3 * C2], start=True, stop=False)
                    last = mm(ps_a[:, 0:2 * C2], xnT[0:CB, 1, :], wqkv_sb[0:CB, 1, C2:3 * C2], start=False, stop=True)
                elif k == 4:
                    for b in range(2):
                        mm(ps_a[:, b * C2:b * C2 + P], km[:, b, 0:P], kv[:, C2:C2 + P], start=True, stop=True)
                        last = mm(ps_a[0:CB, b * C2 + P:(b + 1) * C2], km[:, b, P:C2], kv[:, C2 + P:2 * C2],
                                  start=True, stop=True)
                elif k == 5:
                    for b in range(2):
                        cols = slice(PAD6 * b, PAD6 * (b + 1))
                        mm(ps_a[:, cols], ms[:, b, 0:P], qT[:, 0, cols], start=True, stop=True)
                        last = mm(ps_a[0:CB, P + PAD6 * b:P + PAD6 * (b + 1)], ms[0:CB, b, P:C2], qT[0:CB, 1, cols],
                                  start=True, stop=True)
                elif k == 6:
                    mm(ps_a[:, 0:C2], oT[:, 0, :], wproj_sb[:, 0, :], start=True, stop=False)
                    last = mm(ps_a[:, 0:C2], oT[0:CB, 1, :], wproj_sb[0:CB, 1, :], start=False, stop=True)
                else:
                    mm(ps_a[:, 0:2 * NE], x2T[:, 0, :], wr_sb[:, 0, :], start=True, stop=False)
                    last = mm(ps_a[:, 0:2 * NE], x2T[0:CB, 1, :], wr_sb[0:CB, 1, :], start=False, stop=True)
                last.then_inc(att_ps, 1)

            def body(i, slots, first=False, last=False, with_next=True, with_att=True):
                conv0_sums = False
                for what, k in order(slots, first, last, with_next, with_att):
                    if what in ("tap0", "tap1", "conv"):
                        conv(i, slots, k, ("tap0", "tap1", "conv").index(what), first)
                    elif what == "colsum":
                        if conv0_sums:
                            pe.wait_ge(newton, (i + 1) * NEWTON + 1)
                            conv0_sums = False
                        colsum(i, slots, k, first)
                    elif what == "bcast":
                        bcast(i, slots, k)
                    elif what == "att":
                        attention(i, k)
                    elif what == "l0":
                        l0_tile(i + 1, k)
                    elif what == "psum":
                        pe.wait_ge(steps_v, (i * NS + k) * STEPS - (STEPS - 2))
                        prep(i + 1, what)
                        conv0_sums = True
                    else:
                        prep(i + 1, what)

            for what in ("zmm", "psum", "pbc"):
                prep(0, what)
            for r in range(RES0):
                l0_tile(0, r)
            body(0, SLOTS, first=True)
            with pe.Fori(0, PAIRS - 2) as j:
                body(j + 1, SLOTS)
            body(PAIRS - 1, SLOTS, last=True, with_next=False)
            body(PAIRS, TAIL, with_next=False)
            for k in range(ATT):
                attention(PAIRS + 1, k, before=PAIRS * NS + len(TAIL))

            def count_masks(n):
                pe.wait_ge(count_ready, n)
                mm(ps_a[:, 128:256], ones_pp[:], rt[:, 16, :], start=True, stop=True)
                mm(ps_a[:, 256:384], tri_sb[:], rt[:, 16, :], start=True, stop=True).then_inc(count_sum, 1)

            def count_bit(b):
                pe.wait_ge(count_ready, b + 2)
                mm(ps_a[:, 0:NE], ones_pp[:], cnt[:, 4, :], start=True, stop=True).then_inc(count_sum, 1)

            def count_ties():
                pe.wait_ge(count_ready, BITS + 3)
                mm(ps_a[:, 0:NE], ones_pp[:], cnt[:, 4, :], start=True, stop=True)
                count_masks(BITS + 3)
            count_masks(1)
            with pe.Fori(0, EARLY) as b:
                count_bit(b)

            pe.wait_ge(placed, 1)

            def transpose(t, k, turn):
                pe.wait_ge(x_load[k], 16 * turn + 16)
                pe.wait_ge(xt_sb, t + 1)
                nc.tensor.transpose(ps_v[:, 0:P], xt_tok[k][:, 0:P], id_sb[:])
                nc.tensor.transpose(ps_v[0:CB, P:2 * P], xt_tok[k][:, P:C2], id_sb[:]).then_inc(xt_ps, 1)

            def up(t, k):
                pe.wait_ge(xt_sb, t + 2)
                pe.wait_ge(w1_ready, t + 1)
                for c, (f0, f1) in enumerate(HID_BANKS):
                    for f in range(f0, f1):
                        at_f = up_banks[k][:, c, (f - f0) * P:(f - f0 + 1) * P]
                        mm(at_f, w1_cur[k][:, 0, f * P:(f + 1) * P], xt_ch[k][:, 0, :], start=True, stop=False)
                        last = mm(at_f, w1_cur[k][0:CB + 1, 1, f * P:(f + 1) * P], xt_ch[k][0:CB + 1, 1, :],
                                  start=False, stop=True)
                    last.then_inc(hid_ps, 1)

            def down(t, k):
                e = pe.value_load(expert[0:1, bass.ds(t, 1)], min_val=0, max_val=2 * NE - 1)
                pe.wait_ge(hid_sb, 2 * t + 2)
                pe.wait_ge(y_sb, t + 1)
                for f in range(FC):
                    last = mm(out_banks[k][:, 0:C2], hid[k][:, f, :], w2_all[:, bass.ds(e * (FC * C2) + f * C2, C2)],
                              start=(f == 0), stop=(f == FC - 1))
                last.then_inc(down_ps, 1)

            transpose(0, 0, 0)
            up(0, 0)
            transpose(1, 1, 0)
            up(1, 1)
            transpose(2, 0, 1)
            down(0, 0)

            def two_tiles(g, k1=None, k2=None, k3=None):
                up(2 * g + 2, 0)
                if k1:
                    k1()
                transpose(2 * g + 3, 1, g + 1)
                down(2 * g + 1, 1)
                if k2:
                    k2()
                up(2 * g + 3, 1)
                if k3:
                    k3()
                transpose(2 * g + 4, 0, g + 2)
                down(2 * g + 2, 0)
            done = (BITS - EARLY) // 3
            with pe.Fori(0, done) as g:
                two_tiles(g, lambda: count_bit(3 * g + EARLY), lambda: count_bit(3 * g + (EARLY + 1)),
                          lambda: count_bit(3 * g + (EARLY + 2)))
            two_tiles(done)
            two_tiles(done + 1, count_ties, None, None)
            two_tiles(done + 2, lambda: count_masks(BITS + 4), None, None)
            with pe.Fori(0, half - 4 - done) as g:
                two_tiles(g + (done + 3))
            pe.wait_ge(placed, 2)
            with pe.Fori(0, TILES // 2 - 1 - half) as g:
                two_tiles(g + (half - 1))
            up(TILES - 2, 0)
            transpose(TILES - 1, 1, TILES // 2 - 1)
            down(TILES - 3, 1)
            up(TILES - 1, 1)
            down(TILES - 2, 0)
            down(TILES - 1, 1)


_OUT = (B, T6, C2)


def _constants():
    f = np.float32
    p = np.arange(P)
    ident = np.eye(P, dtype=f)
    rows = np.arange(XR) // TAPS0
    amask = np.zeros((P, C2), f)
    amask[:, 0:P] = (p[:, None] // HEAD == p[None, :] // HEAD) * HEAD ** -0.5
    amask[0:CB, P:] = amask[0:CB, 0:CB]
    select = ((p[:, None] // QUAD == np.arange(4)[None, :]) & (p[:, None] % QUAD < 3)).astype(f)
    return {
        "ident": ident,
        "center": (ident - f(1.0 / P)).astype(f),
        "ones": np.ones((P, P), f),
        "onesc": np.full((P, QUAD), 1.0 / P, f),
        "gmask": ((rows[:, None] == rows[None, :]) / P).astype(f),
        "rmask": (rows[:, None] == np.arange(HALF)[None, :]).astype(f),
        "amask": amask,
        "valid": (p % PAD6 < T6).astype(f)[:, None].copy(),
        "bmask": ((p[:, None] // PAD6 == np.arange(2)[None, :]) & (p[:, None] % PAD6 < T6)).astype(f),
        "tri": (p[:, None] < p[None, :]).astype(f),
        "iota": np.tile(np.arange(PAIRS + 2, dtype=f), (P, 1)),
        "ids": (np.arange(PAIRS)[None, :] * P + p[:, None]).astype(f),
        "select": np.repeat(select[:, :, None], P, axis=2),
        "partm": -np.stack([p % QUAD >= 1, p % QUAD >= 2], axis=1).astype(f),
    }


def kernel(**inputs):
    import concourse.bacc as bacc
    from concourse.bass_utils import run_bass_kernel_spmd

    a = {k: np.asarray(v) for k, v in inputs.items()}
    tok, att, ffn = "L0_tok_", "L0_attn_", "L0_ffn_"
    arrays = {
        "xt": a["x"].reshape(B, Q, SPAN).transpose(2, 0, 1).reshape(SPAN, B * Q),
        "w0": a[tok + "conv_w0"][:, 0, :],
        "wc": np.concatenate([a[f"{tok}conv_w{i}"].transpose(1, 2, 0) for i in range(1, 7)], axis=1),
        "aff": np.stack([np.stack([a[f"{tok}ln_{c}{i}"] for i in range(7)] + [a[f"{tok}fln_{c}"]], axis=1)
                         for c in "gb"], axis=1),
        "projw": a[tok + "proj_w"], "projb": a[tok + "proj_b"],
        "wqkv": a[att + "w_qkv"], "bq": a[att + "b_qkv"][0:C2].reshape(C2, 1), "bkv": a[att + "b_qkv"][C2:],
        "wproj": a[att + "w_proj"], "bproj": a[att + "b_proj"],
        "wr": np.concatenate([a[ffn + "Wsc"], a[ffn + "Wsu"]], axis=1),
        "br": np.concatenate([a[ffn + "bsc"], a[ffn + "bsu"]]),
        "w1": np.concatenate([a[ffn + "W1c"], a[ffn + "W1u"]]).reshape(2 * NE * C2, FF),
        "b1": np.concatenate([a[ffn + "b1c"], a[ffn + "b1u"]]).reshape(2 * NE, FF),
        "w2": np.concatenate([a[ffn + "W2c"], a[ffn + "W2u"]]).reshape(2 * NE * FF, C2),
        "b2": np.concatenate([a[ffn + "b2c"], a[ffn + "b2u"]]).reshape(-1),
        **_constants(),
    }
    arrays = {f"in_{k}": np.ascontiguousarray(v) for k, v in arrays.items()}
    nc = bacc.Bacc("TRN2", target_bir_lowering=False, num_devices=1)
    args = [nc.dram_tensor(k, v.shape, mybir.dt.from_np(v.dtype), kind="ExternalInput").ap() for k, v in arrays.items()]
    out = nc.dram_tensor("out_dram", _OUT, F32, kind="ExternalOutput").ap()
    xs_dram = nc.dram_tensor("xs_dram", (ROWS + 2 * PAIRS * P, C2), F32).ap()
    yc_dram = nc.dram_tensor("yc_dram", (COMMON * P, C2), F32).ap()
    yu_dram = nc.dram_tensor("yu_dram", (UNIQUE * P, C2), F32).ap()
    audio_tower(nc, *args, xs_dram, yc_dram, yu_dram, out.rearrange("(j b) t n -> j b t n", b=2))
    r = run_bass_kernel_spmd(nc, [arrays], core_ids=[0])
    return r.results[0]["out_dram"]
```
